# Optimizing a Trainium2 kernel written in Bass

```python
import numpy as np
import jax
import jax.numpy as jnp

def _softmax(x, axis=-1):
    return jax.nn.softmax(x, axis=axis)

def _gelu(x):
    return jax.nn.gelu(x, approximate=True)

def _silu(x):
    return jax.nn.silu(x)

def _sigmoid(x):
    return jax.nn.sigmoid(x)

def _layernorm(x, axis=-1, eps=1e-05):
    m = jnp.mean(x, axis=axis, keepdims=True)
    v = jnp.var(x, axis=axis, keepdims=True)
    return (x - m) / jnp.sqrt(v + eps)

def _scatter_add(tgt, idx, src, axis=0):
    return tgt.at[idx].add(src)

def _segment_sum(src, seg, n):
    return jax.ops.segment_sum(src, seg, n)
kernel_name = 'mk_xattn_seq_d4_seqx_r8_d997e7'

def setup_inputs(seed: int=0):
    np.random.seed(seed)
    _w = jnp.asarray

    def _rec_inputs():
        import jax
        import jax.numpy as jnp
        _rk = jax.random.key(seed)
        x = -0.0005146 + 1 * jax.random.normal(jax.random.fold_in(_rk, 1), (32, 64, 256), jnp.float32)
        _lenS = 64 - jax.random.randint(jax.random.fold_in(_rk, 7), (32,), 0, max(1, 64 // 4) + 1, jnp.int32)
        _lenS2 = 64 - jax.random.randint(jax.random.fold_in(_rk, 8), (32,), 0, max(1, 64 // 4) + 1, jnp.int32)
        _ctx_2048P = jax.random.normal(jax.random.fold_in(_rk, 11), (32, 16, 256), jnp.float32)
        _ctx_2048c = jax.random.dirichlet(jax.random.fold_in(_rk, 511), 0.3 * jnp.ones((16,), jnp.float32), (32, 64))
        _ctx_2048t = jnp.einsum('bsk,bkd->bsd', _ctx_2048c, _ctx_2048P)
        _ctx_2048t = _ctx_2048t * jax.lax.rsqrt(jnp.mean(jnp.square(_ctx_2048t)) + 1e-12) * 0.953939
        ctx_2048 = -0.000392918 + 0.999932 * (_ctx_2048t + 0.3 * jax.random.normal(jax.random.fold_in(_rk, 611), (32, 64, 256), jnp.float32))
        _validS = jnp.arange(64)[None, :] < _lenS[:, None]
        _validS2 = jnp.arange(64)[None, :] < _lenS2[:, None]
        _causal = jnp.tril(jnp.ones((64, 64), dtype=bool))
        mask_BxS2_ik0 = jnp.where(jnp.broadcast_to(_validS2[:, :], (32, 64)), 0, 1).astype(jnp.int32)
        mask_1x1xSxS2_fc1 = jnp.where(jnp.broadcast_to(_validS2[0:1, None, None, :], (1, 1, 64, 64)), 1.0, 0.0).astype(jnp.float32)
        mask_Bx1xSxS2_ff1 = jnp.where(jnp.ones((32, 1, 64, 64), dtype=bool), 1.0, 0.0).astype(jnp.float32)
        mask_BxS2_bf1 = jnp.ones((32, 64), dtype=bool)
        return (x, ctx_2048, mask_BxS2_ik0, mask_1x1xSxS2_fc1, mask_Bx1xSxS2_ff1, mask_BxS2_bf1)
    x, ctx_2048, mask_BxS2_ik0, mask_1x1xSxS2_fc1, mask_Bx1xSxS2_ff1, mask_BxS2_bf1 = _rec_inputs()

    def _L0_xattn_setup():
        import jax, jax.numpy as jnp
        import numpy as np
        B, P, K, H, NH = (4, 256, 32, 256, 16)
        DH = H // NH
        EPS = 1e-06

        def rmsnorm(x, w):
            var = jnp.mean(jnp.square(x), axis=-1, keepdims=True)
            return x * jax.lax.rsqrt(var + EPS) * w
        key = jax.random.key(seed)
        ks = jax.random.split(key, 12)
        s = 0.02
        return {'x': jax.random.normal(ks[0], (B, P, H), jnp.float32), 'latents': jax.random.normal(ks[1], (B, K, H), jnp.float32), 'attention_mask': jax.random.randint(ks[2], (B, P), 0, 2, jnp.int32), 'q_w': s * jax.random.normal(ks[3], (H, H), jnp.float32), 'q_b': jnp.zeros((H,), jnp.float32), 'kv_w': s * jax.random.normal(ks[4], (H, 2 * H), jnp.float32), 'kv_b': jnp.zeros((2 * H,), jnp.float32), 'out_w': s * jax.random.normal(ks[5], (H, H), jnp.float32), 'out_b': jnp.zeros((H,), jnp.float32), 'postnorm_w': jnp.ones((H,), jnp.float32), 'mlp_w1': s * jax.random.normal(ks[6], (H, 4 * H), jnp.float32), 'mlp_b1': jnp.zeros((4 * H,), jnp.float32), 'mlp_w2': s * jax.random.normal(ks[7], (4 * H, H), jnp.float32), 'mlp_b2': jnp.zeros((H,), jnp.float32)}
    _L0_xattn_all = _L0_xattn_setup()
    _L0_xattn_in = {k: v for k, v in _L0_xattn_all.items() if k in ('q_w', 'q_b', 'kv_w', 'kv_b', 'out_w', 'out_b', 'postnorm_w', 'mlp_w1', 'mlp_b1', 'mlp_w2', 'mlp_b2')}
    del _L0_xattn_all

    def _L1_xattn_setup():
        import jax, jax.numpy as jnp
        import numpy as np
        N_HEAD = 32
        EPS = 1e-05

        def _ln(x, w, b):
            m = jnp.mean(x, axis=-1, keepdims=True)
            v = jnp.mean((x - m) ** 2, axis=-1, keepdims=True)
            return (x - m) * jax.lax.rsqrt(v + EPS) * w + b

        def _forward(x, state, i, ln1_w, ln1_b, ln2_w, ln2_b, maa_x, maa_w, maa_k, maa_v, maa_r, maa_g, maa_w1, maa_w2, time_decay, decay_w1, decay_w2, faaaa, Wr, Wk, Wv, Wg, Wo, gn_w, gn_b, fmaa_k, fmaa_r, fWk, fWr, fWv):
            B, L, C = x.shape
            H = N_HEAD
            S = C // H
            i0 = (2 + S) * i
            xa = _ln(x, ln1_w, ln1_b)
            sx = jnp.concatenate([state[:, i0 + 1][:, None], xa[:, :-1]], axis=1) - xa
            xxx = xa + sx * maa_x
            t = jnp.tanh(xxx @ maa_w1).reshape(B, L, 5, -1)
            m = jnp.einsum('blfd,fdc->blfc', t, maa_w2)
            mw, mk, mv, mr, mg = (m[:, :, j] for j in range(5))
            xw = xa + sx * (maa_w + mw)
            xk = xa + sx * (maa_k + mk)
            xv = xa + sx * (maa_v + mv)
            xr = xa + sx * (maa_r + mr)
            xg = xa + sx * (maa_g + mg)
            w = time_decay + jnp.tanh(xw @ decay_w1) @ decay_w2
            w = jnp.exp(-jnp.exp(w)).reshape(B, L, H, S)
            r = (xr @ Wr.T).reshape(B, L, H, S)
            k = (xk @ Wk.T).reshape(B, L, H, S)
            v = (xv @ Wv.T).reshape(B, L, H, S)
            g = jax.nn.silu(xg @ Wg.T)
            s0 = state[:, i0 + 2:i0 + 2 + S].reshape(B, H, S, S)

            def step(s, inp):
                k_l, v_l, w_l, r_l = inp
                a = k_l[..., :, None] * v_l[..., None, :]
                out = jnp.einsum('bhs,bhst->bht', r_l, faaaa * a + s)
                s_new = a + w_l[..., None] * s
                return (s_new, out)
            seq = tuple((z.transpose(1, 0, 2, 3) for z in (k, v, w, r)))
            _, outs = jax.lax.scan(step, s0, seq)
            y = outs.transpose(1, 0, 2, 3)
            gm = jnp.mean(y, axis=-1, keepdims=True)
            gv = jnp.mean((y - gm) ** 2, axis=-1, keepdims=True)
            y = ((y - gm) * jax.lax.rsqrt(gv + EPS)).reshape(B, L, C) * gn_w + gn_b
            x = x + y * g @ Wo.T
            xc = _ln(x, ln2_w, ln2_b)
            sxc = jnp.concatenate([state[:, i0][:, None], xc[:, :-1]], axis=1) - xc
            xk2 = xc + sxc * fmaa_k
            xr2 = xc + sxc * fmaa_r
            rr = jax.nn.sigmoid(xr2 @ fWr.T)
            kk = jnp.square(jax.nn.relu(xk2 @ fWk.T))
            x = x + rr * (kk @ fWv.T)
            return x
        key = jax.random.key(seed)
        B, L, C, H = (8, 64, 256, N_HEAD)
        S = C // H
        DM, DD = (32, 64)
        ks = jax.random.split(key, 32)
        n = lambda k, shp, s=1.0: jax.random.normal(k, shp, dtype=jnp.float32) * s
        u = lambda k, shp: jax.random.uniform(k, shp, dtype=jnp.float32)
        inp = {'x': n(ks[0], (B, L, C)), 'state': n(ks[1], (B, 2 + S, C), 0.1), 'i': 0, 'ln1_w': jnp.ones((C,), jnp.float32), 'ln1_b': jnp.zeros((C,), jnp.float32), 'ln2_w': jnp.ones((C,), jnp.float32), 'ln2_b': jnp.zeros((C,), jnp.float32), 'maa_x': u(ks[2], (C,)), 'maa_w': u(ks[3], (C,)), 'maa_k': u(ks[4], (C,)), 'maa_v': u(ks[5], (C,)), 'maa_r': u(ks[6], (C,)), 'maa_g': u(ks[7], (C,)), 'maa_w1': n(ks[8], (C, 5 * DM), 0.02), 'maa_w2': n(ks[9], (5, DM, C), 0.02), 'time_decay': n(ks[10], (C,), 0.5), 'decay_w1': n(ks[11], (C, DD), 0.02), 'decay_w2': n(ks[12], (DD, C), 0.02), 'faaaa': n(ks[13], (H, S, 1), 0.1), 'Wr': n(ks[14], (C, C), 0.02), 'Wk': n(ks[15], (C, C), 0.02), 'Wv': n(ks[16], (C, C), 0.02), 'Wg': n(ks[17], (C, C), 0.02), 'Wo': n(ks[18], (C, C), 0.02), 'gn_w': jnp.ones((C,), jnp.float32), 'gn_b': jnp.zeros((C,), jnp.float32), 'fmaa_k': u(ks[19], (C,)), 'fmaa_r': u(ks[20], (C,)), 'fWk': n(ks[21], (C, C), 0.02), 'fWr': n(ks[22], (C, C), 0.02), 'fWv': n(ks[23], (C, C), 0.02)}
        return inp
    _L1_xattn_all = _L1_xattn_setup()
    _L1_xattn_in = {k: v for k, v in _L1_xattn_all.items() if k in ('ln1_w', 'ln1_b', 'ln2_w', 'ln2_b', 'maa_x', 'maa_w', 'maa_k', 'maa_v', 'maa_r', 'maa_g', 'maa_w1', 'maa_w2', 'time_decay', 'decay_w1', 'decay_w2', 'faaaa', 'Wr', 'Wk', 'Wv', 'Wg', 'Wo', 'gn_w', 'gn_b', 'fmaa_k', 'fmaa_r', 'fWk', 'fWr', 'fWv')}
    del _L1_xattn_all

    def _L2_xattn_setup():
        import jax, jax.numpy as jnp
        import numpy as np
        H = 256
        NH = 16
        HD = H // NH
        EPS = 1e-05

        def gelu(x):
            return 0.5 * x * (1.0 + jnp.tanh(0.7978845608028654 * x * (1.0 + 0.044715 * x * x)))

        def layernorm(x, scale, bias):
            m = jnp.mean(x, axis=-1, keepdims=True)
            v = jnp.mean(jnp.square(x - m), axis=-1, keepdims=True)
            return (x - m) * jax.lax.rsqrt(v + EPS) * scale + bias

        def split_heads(x):
            b, s, _ = x.shape
            return x.reshape(b, s, NH, HD).transpose(0, 2, 1, 3)

        def merge_heads(x):
            b, nh, s, hd = x.shape
            return x.transpose(0, 2, 1, 3).reshape(b, s, nh * hd)

        def attention(q, k, v, mask):
            scores = jnp.einsum('bhqd,bhkd->bhqk', q, k) / jnp.sqrt(jnp.float32(HD))
            scores = scores * mask - 10000.0 * (1.0 - mask)
            probs = jax.nn.softmax(scores, axis=-1)
            return jnp.einsum('bhqk,bhkd->bhqd', probs, v)
        key = jax.random.key(seed)
        ks = jax.random.split(key, 16)
        b, s, t = (2, 128, 128)
        w = lambda k, i, o: jax.random.normal(k, (i, o), jnp.float32) * 0.02
        inp = {'hidden_states': jax.random.normal(ks[0], (b, s, H), jnp.float32), 'encoder_states': jax.random.normal(ks[1], (b, t, H), jnp.float32), 'ltor_mask': jnp.tril(jnp.ones((1, 1, s, s), jnp.float32)), 'cross_mask': jnp.ones((b, 1, s, t), jnp.float32), 'ln1_s': jnp.ones((H,), jnp.float32), 'ln1_b': jnp.zeros((H,), jnp.float32), 'w_qkv': w(ks[2], H, 3 * H), 'b_qkv': jnp.zeros((3 * H,), jnp.float32), 'w_ao': w(ks[3], H, H), 'b_ao': jnp.zeros((H,), jnp.float32), 'ln2_s': jnp.ones((H,), jnp.float32), 'ln2_b': jnp.zeros((H,), jnp.float32), 'w_q': w(ks[4], H, H), 'b_q': jnp.zeros((H,), jnp.float32), 'w_kv': w(ks[5], H, 2 * H), 'b_kv': jnp.zeros((2 * H,), jnp.float32), 'w_co': w(ks[6], H, H), 'b_co': jnp.zeros((H,), jnp.float32), 'ln3_s': jnp.ones((H,), jnp.float32), 'ln3_b': jnp.zeros((H,), jnp.float32), 'w1': w(ks[7], H, 4 * H), 'b1': jnp.zeros((4 * H,), jnp.float32), 'w2': w(ks[8], 4 * H, H), 'b2': jnp.zeros((H,), jnp.float32)}
        return inp
    _L2_xattn_all = _L2_xattn_setup()
    _L2_xattn_in = {k: v for k, v in _L2_xattn_all.items() if k in ('ln1_s', 'ln1_b', 'w_qkv', 'b_qkv', 'w_ao', 'b_ao', 'ln2_s', 'ln2_b', 'w_q', 'b_q', 'w_kv', 'b_kv', 'w_co', 'b_co', 'ln3_s', 'ln3_b', 'w1', 'b1', 'w2', 'b2')}
    del _L2_xattn_all

    def _L3_xattn_setup():
        import jax, jax.numpy as jnp
        import numpy as np
        HIDDEN = 256
        HEADS = 16
        HEAD_DIM = HIDDEN // HEADS
        LN_EPS = 1e-05
        GATE_INIT = 0.5

        def _layer_norm(x, gamma, beta):
            mu = jnp.mean(x, axis=-1, keepdims=True)
            var = jnp.mean(jnp.square(x - mu), axis=-1, keepdims=True)
            return (x - mu) * jax.lax.rsqrt(var + LN_EPS) * gamma + beta
        key = jax.random.key(seed)
        ks = jax.random.split(key, 8)
        B, T_TEXT, T_AUDIO = (4, 256, 1500)
        s = 0.02
        return {'hidden_states': jax.random.normal(ks[0], (B, T_TEXT, HIDDEN), jnp.float32), 'audio_kv': jax.random.normal(ks[1], (B, T_AUDIO, HIDDEN), jnp.float32), 'audio_attention_mask': jnp.ones((B, T_AUDIO), dtype=bool), 'Wq': jax.random.normal(ks[2], (HIDDEN, HIDDEN), jnp.float32) * s, 'Wk': jax.random.normal(ks[3], (HIDDEN, HIDDEN), jnp.float32) * s, 'Wv': jax.random.normal(ks[4], (HIDDEN, HIDDEN), jnp.float32) * s, 'Wo': jax.random.normal(ks[5], (HIDDEN, HIDDEN), jnp.float32) * s, 'ln_gamma': jnp.ones((HIDDEN,), jnp.float32), 'ln_beta': jnp.zeros((HIDDEN,), jnp.float32), 'gate': jnp.array([GATE_INIT], jnp.float32)}
    _L3_xattn_all = _L3_xattn_setup()
    _L3_xattn_in = {k: v for k, v in _L3_xattn_all.items() if k in ('Wq', 'Wk', 'Wv', 'Wo', 'ln_gamma', 'ln_beta', 'gate')}
    del _L3_xattn_all
    return {'x': x, 'ctx_2048': ctx_2048, 'mask_BxS2_ik0': mask_BxS2_ik0, 'mask_1x1xSxS2_fc1': mask_1x1xSxS2_fc1, 'mask_Bx1xSxS2_ff1': mask_Bx1xSxS2_ff1, 'mask_BxS2_bf1': mask_BxS2_bf1, 'L0_xattn_q_w': _L0_xattn_in['q_w'], 'L0_xattn_q_b': _L0_xattn_in['q_b'], 'L0_xattn_kv_w': _L0_xattn_in['kv_w'], 'L0_xattn_kv_b': _L0_xattn_in['kv_b'], 'L0_xattn_out_w': _L0_xattn_in['out_w'], 'L0_xattn_out_b': _L0_xattn_in['out_b'], 'L0_xattn_postnorm_w': _L0_xattn_in['postnorm_w'], 'L0_xattn_mlp_w1': _L0_xattn_in['mlp_w1'], 'L0_xattn_mlp_b1': _L0_xattn_in['mlp_b1'], 'L0_xattn_mlp_w2': _L0_xattn_in['mlp_w2'], 'L0_xattn_mlp_b2': _L0_xattn_in['mlp_b2'], 'L1_xattn_ln1_w': _L1_xattn_in['ln1_w'], 'L1_xattn_ln1_b': _L1_xattn_in['ln1_b'], 'L1_xattn_ln2_w': _L1_xattn_in['ln2_w'], 'L1_xattn_ln2_b': _L1_xattn_in['ln2_b'], 'L1_xattn_maa_x': _L1_xattn_in['maa_x'], 'L1_xattn_maa_w': _L1_xattn_in['maa_w'], 'L1_xattn_maa_k': _L1_xattn_in['maa_k'], 'L1_xattn_maa_v': _L1_xattn_in['maa_v'], 'L1_xattn_maa_r': _L1_xattn_in['maa_r'], 'L1_xattn_maa_g': _L1_xattn_in['maa_g'], 'L1_xattn_maa_w1': _L1_xattn_in['maa_w1'], 'L1_xattn_maa_w2': _L1_xattn_in['maa_w2'], 'L1_xattn_time_decay': _L1_xattn_in['time_decay'], 'L1_xattn_decay_w1': _L1_xattn_in['decay_w1'], 'L1_xattn_decay_w2': _L1_xattn_in['decay_w2'], 'L1_xattn_faaaa': _L1_xattn_in['faaaa'], 'L1_xattn_Wr': _L1_xattn_in['Wr'], 'L1_xattn_Wk': _L1_xattn_in['Wk'], 'L1_xattn_Wv': _L1_xattn_in['Wv'], 'L1_xattn_Wg': _L1_xattn_in['Wg'], 'L1_xattn_Wo': _L1_xattn_in['Wo'], 'L1_xattn_gn_w': _L1_xattn_in['gn_w'], 'L1_xattn_gn_b': _L1_xattn_in['gn_b'], 'L1_xattn_fmaa_k': _L1_xattn_in['fmaa_k'], 'L1_xattn_fmaa_r': _L1_xattn_in['fmaa_r'], 'L1_xattn_fWk': _L1_xattn_in['fWk'], 'L1_xattn_fWr': _L1_xattn_in['fWr'], 'L1_xattn_fWv': _L1_xattn_in['fWv'], 'L2_xattn_ln1_s': _L2_xattn_in['ln1_s'], 'L2_xattn_ln1_b': _L2_xattn_in['ln1_b'], 'L2_xattn_w_qkv': _L2_xattn_in['w_qkv'], 'L2_xattn_b_qkv': _L2_xattn_in['b_qkv'], 'L2_xattn_w_ao': _L2_xattn_in['w_ao'], 'L2_xattn_b_ao': _L2_xattn_in['b_ao'], 'L2_xattn_ln2_s': _L2_xattn_in['ln2_s'], 'L2_xattn_ln2_b': _L2_xattn_in['ln2_b'], 'L2_xattn_w_q': _L2_xattn_in['w_q'], 'L2_xattn_b_q': _L2_xattn_in['b_q'], 'L2_xattn_w_kv': _L2_xattn_in['w_kv'], 'L2_xattn_b_kv': _L2_xattn_in['b_kv'], 'L2_xattn_w_co': _L2_xattn_in['w_co'], 'L2_xattn_b_co': _L2_xattn_in['b_co'], 'L2_xattn_ln3_s': _L2_xattn_in['ln3_s'], 'L2_xattn_ln3_b': _L2_xattn_in['ln3_b'], 'L2_xattn_w1': _L2_xattn_in['w1'], 'L2_xattn_b1': _L2_xattn_in['b1'], 'L2_xattn_w2': _L2_xattn_in['w2'], 'L2_xattn_b2': _L2_xattn_in['b2'], 'L3_xattn_Wq': _L3_xattn_in['Wq'], 'L3_xattn_Wk': _L3_xattn_in['Wk'], 'L3_xattn_Wv': _L3_xattn_in['Wv'], 'L3_xattn_Wo': _L3_xattn_in['Wo'], 'L3_xattn_ln_gamma': _L3_xattn_in['ln_gamma'], 'L3_xattn_ln_beta': _L3_xattn_in['ln_beta'], 'L3_xattn_gate': _L3_xattn_in['gate']}

def reference(x, ctx_2048, mask_BxS2_ik0, mask_1x1xSxS2_fc1, mask_Bx1xSxS2_ff1, mask_BxS2_bf1, L0_xattn_q_w, L0_xattn_q_b, L0_xattn_kv_w, L0_xattn_kv_b, L0_xattn_out_w, L0_xattn_out_b, L0_xattn_postnorm_w, L0_xattn_mlp_w1, L0_xattn_mlp_b1, L0_xattn_mlp_w2, L0_xattn_mlp_b2, L1_xattn_ln1_w, L1_xattn_ln1_b, L1_xattn_ln2_w, L1_xattn_ln2_b, L1_xattn_maa_x, L1_xattn_maa_w, L1_xattn_maa_k, L1_xattn_maa_v, L1_xattn_maa_r, L1_xattn_maa_g, L1_xattn_maa_w1, L1_xattn_maa_w2, L1_xattn_time_decay, L1_xattn_decay_w1, L1_xattn_decay_w2, L1_xattn_faaaa, L1_xattn_Wr, L1_xattn_Wk, L1_xattn_Wv, L1_xattn_Wg, L1_xattn_Wo, L1_xattn_gn_w, L1_xattn_gn_b, L1_xattn_fmaa_k, L1_xattn_fmaa_r, L1_xattn_fWk, L1_xattn_fWr, L1_xattn_fWv, L2_xattn_ln1_s, L2_xattn_ln1_b, L2_xattn_w_qkv, L2_xattn_b_qkv, L2_xattn_w_ao, L2_xattn_b_ao, L2_xattn_ln2_s, L2_xattn_ln2_b, L2_xattn_w_q, L2_xattn_b_q, L2_xattn_w_kv, L2_xattn_b_kv, L2_xattn_w_co, L2_xattn_b_co, L2_xattn_ln3_s, L2_xattn_ln3_b, L2_xattn_w1, L2_xattn_b1, L2_xattn_w2, L2_xattn_b2, L3_xattn_Wq, L3_xattn_Wk, L3_xattn_Wv, L3_xattn_Wo, L3_xattn_ln_gamma, L3_xattn_ln_beta, L3_xattn_gate):
    import jax
    import jax.numpy as jnp

    def _L0_xattn_ref(x, latents, attention_mask, q_w, q_b, kv_w, kv_b, out_w, out_b, postnorm_w, mlp_w1, mlp_b1, mlp_w2, mlp_b2):
        import jax, jax.numpy as jnp
        import numpy as np
        B, P, K, H, NH = (4, 256, 32, 256, 16)
        DH = H // NH
        EPS = 1e-06

        def rmsnorm(x, w):
            var = jnp.mean(jnp.square(x), axis=-1, keepdims=True)
            return x * jax.lax.rsqrt(var + EPS) * w
        b, p, _ = x.shape
        k_len = latents.shape[1]
        residual = latents
        h = jnp.concatenate([x, latents], axis=1)
        q = (latents @ q_w + q_b).reshape(b, k_len, NH, DH)
        kv = (h @ kv_w + kv_b).reshape(b, p + k_len, NH, DH, 2)
        kmat, v = (kv[..., 0], kv[..., 1])
        attn = jnp.einsum('bkhd,bnhd->bhkn', q, kmat) / DH
        full_mask = jnp.concatenate([attention_mask.astype(bool), jnp.ones((b, k_len), bool)], axis=-1)
        attn = jnp.where(full_mask[:, None, None, :], attn, -jnp.inf)
        attn = jax.nn.softmax(attn.astype(jnp.float32), axis=-1).astype(q.dtype)
        attn_out = jnp.einsum('bhkn,bnhd->bkhd', attn, v).reshape(b, k_len, H)
        attn_out = attn_out @ out_w + out_b + residual
        out = rmsnorm(attn_out, postnorm_w)
        out = jax.nn.gelu(out @ mlp_w1 + mlp_b1) @ mlp_w2 + mlp_b2
        return out + residual

    def _L1_xattn_ref(x, state, i, ln1_w, ln1_b, ln2_w, ln2_b, maa_x, maa_w, maa_k, maa_v, maa_r, maa_g, maa_w1, maa_w2, time_decay, decay_w1, decay_w2, faaaa, Wr, Wk, Wv, Wg, Wo, gn_w, gn_b, fmaa_k, fmaa_r, fWk, fWr, fWv):
        import jax, jax.numpy as jnp
        import numpy as np
        N_HEAD = 32
        EPS = 1e-05

        def _ln(x, w, b):
            m = jnp.mean(x, axis=-1, keepdims=True)
            v = jnp.mean((x - m) ** 2, axis=-1, keepdims=True)
            return (x - m) * jax.lax.rsqrt(v + EPS) * w + b

        def _forward(x, state, i, ln1_w, ln1_b, ln2_w, ln2_b, maa_x, maa_w, maa_k, maa_v, maa_r, maa_g, maa_w1, maa_w2, time_decay, decay_w1, decay_w2, faaaa, Wr, Wk, Wv, Wg, Wo, gn_w, gn_b, fmaa_k, fmaa_r, fWk, fWr, fWv):
            B, L, C = x.shape
            H = N_HEAD
            S = C // H
            i0 = (2 + S) * i
            xa = _ln(x, ln1_w, ln1_b)
            sx = jnp.concatenate([state[:, i0 + 1][:, None], xa[:, :-1]], axis=1) - xa
            xxx = xa + sx * maa_x
            t = jnp.tanh(xxx @ maa_w1).reshape(B, L, 5, -1)
            m = jnp.einsum('blfd,fdc->blfc', t, maa_w2)
            mw, mk, mv, mr, mg = (m[:, :, j] for j in range(5))
            xw = xa + sx * (maa_w + mw)
            xk = xa + sx * (maa_k + mk)
            xv = xa + sx * (maa_v + mv)
            xr = xa + sx * (maa_r + mr)
            xg = xa + sx * (maa_g + mg)
            w = time_decay + jnp.tanh(xw @ decay_w1) @ decay_w2
            w = jnp.exp(-jnp.exp(w)).reshape(B, L, H, S)
            r = (xr @ Wr.T).reshape(B, L, H, S)
            k = (xk @ Wk.T).reshape(B, L, H, S)
            v = (xv @ Wv.T).reshape(B, L, H, S)
            g = jax.nn.silu(xg @ Wg.T)
            s0 = state[:, i0 + 2:i0 + 2 + S].reshape(B, H, S, S)

            def step(s, inp):
                k_l, v_l, w_l, r_l = inp
                a = k_l[..., :, None] * v_l[..., None, :]
                out = jnp.einsum('bhs,bhst->bht', r_l, faaaa * a + s)
                s_new = a + w_l[..., None] * s
                return (s_new, out)
            seq = tuple((z.transpose(1, 0, 2, 3) for z in (k, v, w, r)))
            _, outs = jax.lax.scan(step, s0, seq)
            y = outs.transpose(1, 0, 2, 3)
            gm = jnp.mean(y, axis=-1, keepdims=True)
            gv = jnp.mean((y - gm) ** 2, axis=-1, keepdims=True)
            y = ((y - gm) * jax.lax.rsqrt(gv + EPS)).reshape(B, L, C) * gn_w + gn_b
            x = x + y * g @ Wo.T
            xc = _ln(x, ln2_w, ln2_b)
            sxc = jnp.concatenate([state[:, i0][:, None], xc[:, :-1]], axis=1) - xc
            xk2 = xc + sxc * fmaa_k
            xr2 = xc + sxc * fmaa_r
            rr = jax.nn.sigmoid(xr2 @ fWr.T)
            kk = jnp.square(jax.nn.relu(xk2 @ fWk.T))
            x = x + rr * (kk @ fWv.T)
            return x
        return _forward(x, state, i, ln1_w, ln1_b, ln2_w, ln2_b, maa_x, maa_w, maa_k, maa_v, maa_r, maa_g, maa_w1, maa_w2, time_decay, decay_w1, decay_w2, faaaa, Wr, Wk, Wv, Wg, Wo, gn_w, gn_b, fmaa_k, fmaa_r, fWk, fWr, fWv)

    def _L2_xattn_ref(hidden_states, encoder_states, ltor_mask, cross_mask, ln1_s, ln1_b, w_qkv, b_qkv, w_ao, b_ao, ln2_s, ln2_b, w_q, b_q, w_kv, b_kv, w_co, b_co, ln3_s, ln3_b, w1, b1, w2, b2):
        import jax, jax.numpy as jnp
        import numpy as np
        H = 256
        NH = 16
        HD = H // NH
        EPS = 1e-05

        def gelu(x):
            return 0.5 * x * (1.0 + jnp.tanh(0.7978845608028654 * x * (1.0 + 0.044715 * x * x)))

        def layernorm(x, scale, bias):
            m = jnp.mean(x, axis=-1, keepdims=True)
            v = jnp.mean(jnp.square(x - m), axis=-1, keepdims=True)
            return (x - m) * jax.lax.rsqrt(v + EPS) * scale + bias

        def split_heads(x):
            b, s, _ = x.shape
            return x.reshape(b, s, NH, HD).transpose(0, 2, 1, 3)

        def merge_heads(x):
            b, nh, s, hd = x.shape
            return x.transpose(0, 2, 1, 3).reshape(b, s, nh * hd)

        def attention(q, k, v, mask):
            scores = jnp.einsum('bhqd,bhkd->bhqk', q, k) / jnp.sqrt(jnp.float32(HD))
            scores = scores * mask - 10000.0 * (1.0 - mask)
            probs = jax.nn.softmax(scores, axis=-1)
            return jnp.einsum('bhqk,bhkd->bhqd', probs, v)
        ln_out = layernorm(hidden_states, ln1_s, ln1_b)
        qkv = ln_out @ w_qkv + b_qkv
        q, k, v = jnp.split(qkv, 3, axis=-1)
        ctx = merge_heads(attention(split_heads(q), split_heads(k), split_heads(v), ltor_mask))
        attn_out = ctx @ w_ao + b_ao
        x = hidden_states + attn_out
        ln_out = layernorm(x, ln2_s, ln2_b)
        q = ln_out @ w_q + b_q
        kv = encoder_states @ w_kv + b_kv
        k, v = jnp.split(kv, 2, axis=-1)
        ctx = merge_heads(attention(split_heads(q), split_heads(k), split_heads(v), cross_mask))
        cross_out = ctx @ w_co + b_co
        x = x + cross_out
        ln_out = layernorm(x, ln3_s, ln3_b)
        mlp_out = gelu(ln_out @ w1 + b1) @ w2 + b2
        return x + mlp_out

    def _L3_xattn_ref(hidden_states, audio_kv, audio_attention_mask, Wq, Wk, Wv, Wo, ln_gamma, ln_beta, gate):
        import jax, jax.numpy as jnp
        import numpy as np
        HIDDEN = 256
        HEADS = 16
        HEAD_DIM = HIDDEN // HEADS
        LN_EPS = 1e-05
        GATE_INIT = 0.5

        def _layer_norm(x, gamma, beta):
            mu = jnp.mean(x, axis=-1, keepdims=True)
            var = jnp.mean(jnp.square(x - mu), axis=-1, keepdims=True)
            return (x - mu) * jax.lax.rsqrt(var + LN_EPS) * gamma + beta
        B, Tt, D = hidden_states.shape
        Ta = audio_kv.shape[1]
        scale = HEAD_DIM ** (-0.5)
        a = _layer_norm(audio_kv, ln_gamma, ln_beta)
        Q = (hidden_states @ Wq.T).reshape(B, Tt, HEADS, HEAD_DIM).transpose(0, 2, 1, 3)
        K = (a @ Wk.T).reshape(B, Ta, HEADS, HEAD_DIM).transpose(0, 2, 1, 3)
        V = (a @ Wv.T).reshape(B, Ta, HEADS, HEAD_DIM).transpose(0, 2, 1, 3)
        scores = jnp.einsum('bhtd,bhsd->bhts', Q, K) * scale
        mask = audio_attention_mask[:, None, None, :]
        scores = jnp.where(mask, scores, jnp.float32(-jnp.inf))
        attn = jax.nn.softmax(scores, axis=-1)
        out = jnp.einsum('bhts,bhsd->bhtd', attn, V)
        out = out.transpose(0, 2, 1, 3).reshape(B, Tt, D)
        out = out @ Wo.T
        return hidden_states + jnp.tanh(gate) * out
    x = _L0_xattn_ref(ctx_2048, x, mask_BxS2_ik0, L0_xattn_q_w, L0_xattn_q_b, L0_xattn_kv_w, L0_xattn_kv_b, L0_xattn_out_w, L0_xattn_out_b, L0_xattn_postnorm_w, L0_xattn_mlp_w1, L0_xattn_mlp_b1, L0_xattn_mlp_w2, L0_xattn_mlp_b2)
    x = _L1_xattn_ref(x, ctx_2048, 0, L1_xattn_ln1_w, L1_xattn_ln1_b, L1_xattn_ln2_w, L1_xattn_ln2_b, L1_xattn_maa_x, L1_xattn_maa_w, L1_xattn_maa_k, L1_xattn_maa_v, L1_xattn_maa_r, L1_xattn_maa_g, L1_xattn_maa_w1, L1_xattn_maa_w2, L1_xattn_time_decay, L1_xattn_decay_w1, L1_xattn_decay_w2, L1_xattn_faaaa, L1_xattn_Wr, L1_xattn_Wk, L1_xattn_Wv, L1_xattn_Wg, L1_xattn_Wo, L1_xattn_gn_w, L1_xattn_gn_b, L1_xattn_fmaa_k, L1_xattn_fmaa_r, L1_xattn_fWk, L1_xattn_fWr, L1_xattn_fWv)
    x = _L2_xattn_ref(x, ctx_2048, mask_1x1xSxS2_fc1, mask_Bx1xSxS2_ff1, L2_xattn_ln1_s, L2_xattn_ln1_b, L2_xattn_w_qkv, L2_xattn_b_qkv, L2_xattn_w_ao, L2_xattn_b_ao, L2_xattn_ln2_s, L2_xattn_ln2_b, L2_xattn_w_q, L2_xattn_b_q, L2_xattn_w_kv, L2_xattn_b_kv, L2_xattn_w_co, L2_xattn_b_co, L2_xattn_ln3_s, L2_xattn_ln3_b, L2_xattn_w1, L2_xattn_b1, L2_xattn_w2, L2_xattn_b2)
    x = _L3_xattn_ref(x, ctx_2048, mask_BxS2_bf1, L3_xattn_Wq, L3_xattn_Wk, L3_xattn_Wv, L3_xattn_Wo, L3_xattn_ln_gamma, L3_xattn_ln_beta, L3_xattn_gate)
    return x

_drawn_inputs = setup_inputs


def setup_inputs(seed=0):
    import zlib

    import numpy as np

    out = dict(_drawn_inputs(seed))
    spreads = {'L0_xattn_q_b': (0.0, 0.8),
     'L0_xattn_kv_b': (0.0, 0.8),
     'L0_xattn_out_b': (0.0, 0.663),
     'L0_xattn_postnorm_w': (1.0, 0.6),
     'L0_xattn_mlp_b1': (0.0, 0.1),
     'L0_xattn_mlp_b2': (0.0, 0.1),
     'L1_xattn_ln1_w': (1.0, 0.6),
     'L1_xattn_ln1_b': (0.0, 0.578),
     'L1_xattn_ln2_w': (1.0, 0.6),
     'L1_xattn_ln2_b': (0.0, 0.8),
     'L1_xattn_gn_w': (1.0, 0.6),
     'L1_xattn_gn_b': (0.0, 0.8),
     'L2_xattn_ln1_s': (1.0, 0.6),
     'L2_xattn_ln1_b': (0.0, 2.0),
     'L2_xattn_b_qkv': (0.0, 2.0),
     'L2_xattn_b_ao': (0.0, 2.0),
     'L2_xattn_ln2_s': (1.0, 0.6),
     'L2_xattn_ln2_b': (0.0, 2.0),
     'L2_xattn_b_q': (0.0, 2.0),
     'L2_xattn_b_kv': (0.0, 2.0),
     'L2_xattn_b_co': (0.0, 2.0),
     'L2_xattn_ln3_s': (1.0, 0.6),
     'L2_xattn_ln3_b': (0.0, 2.0),
     'L2_xattn_b1': (0.0, 2.0),
     'L2_xattn_b2': (0.0, 2.0),
     'L3_xattn_ln_gamma': (1.0, 0.6),
     'L3_xattn_ln_beta': (0.0, 2.0)}
    factors = {'L0_xattn_q_w': 8.0,
     'L0_xattn_kv_w': 8.0,
     'L0_xattn_out_w': 8.0,
     'L1_xattn_maa_x': 8.0,
     'L1_xattn_maa_w': 8.0,
     'L1_xattn_maa_v': 2.704,
     'L1_xattn_maa_w1': 8.0,
     'L1_xattn_maa_w2': 8.0,
     'L1_xattn_time_decay': 3.598,
     'L1_xattn_decay_w1': 8.0,
     'L1_xattn_decay_w2': 8.0,
     'L1_xattn_faaaa': 7.74,
     'L1_xattn_fmaa_k': 7.51,
     'L1_xattn_fmaa_r': 8.0,
     'L1_xattn_fWk': 4.235,
     'L1_xattn_fWr': 8.0,
     'L1_xattn_fWv': 3.87,
     'L2_xattn_w_qkv': 22.184,
     'L2_xattn_w_q': 200.0,
     'L3_xattn_Wq': 64.0,
     'L3_xattn_Wk': 64.0,
     'L2_xattn_w_ao': 8.0,
     'L2_xattn_w_kv': 8.0,
     'L2_xattn_w_co': 8.0,
     'L2_xattn_w1': 8.0,
     'L2_xattn_w2': 8.0,
     'L3_xattn_Wv': 8.0,
     'L3_xattn_Wo': 8.0}
    for name, (base, spread) in spreads.items():
        noise = np.random.default_rng([zlib.crc32(name.encode()), seed]).standard_normal(out[name].shape)
        drawn = base * np.exp(spread * noise) if base else spread * noise
        out[name] = jnp.asarray(drawn.astype(out[name].dtype))
    for name, factor in factors.items():
        out[name] = (out[name] * factor).astype(out[name].dtype)
    return out
```

```python
from contextlib import ExitStack

import concourse.bass as bass
from concourse import mybir

ALU = mybir.AluOpType
ACT = mybir.ActivationFunctionType
AX_X = mybir.AxisListType.X
F32 = mybir.dt.float32
BF16 = mybir.dt.bfloat16
I32 = mybir.dt.int32

P = 128
B, S, C = 32, 64, 256
G = 4
NG = B // G
T = G * S
TT = T // P
CT = C // P
D = 16
PAIRS = C // (2 * D)
PT_ = 4
SH = 8
FF = 4 * C
FT = FF // P
MASKED = -1e30
RSQRT_SEED = float(0x5F3759DF)

VECS = ["l0_bq", "l0_bk", "l0_post", "l0_b1", "ln1_w", "ln1_b", "ln2_w", "ln2_b", "maa_x", "maa_k", "maa_v",
        "maa_r", "maa_g", "maa_w", "decay", "gn_w", "gn_b", "fmaa_k", "fmaa_r", "l2_ln1_s", "l2_ln1_b",
        "l2_ln2_s", "l2_ln2_b", "l2_ln3_s", "l2_ln3_b", "l2_bq", "l2_bk", "l2_bq2", "l2_bk2", "l2_b1",
        "l3_ln_s", "l3_ln_b"]
VEC_WIDTH = {v: (FT if v in ("l0_b1", "l2_b1") else CT) for v in VECS}
VEC_AT = {v: sum(VEC_WIDTH[u] for u in VECS[:i]) for i, v in enumerate(VECS)}
NVEC = sum(VEC_WIDTH.values())
ROWS = ["l0_bv", "l0_bo", "l0_b2", "l2_bo", "l2_bo2", "l2_b2"]
FRONT_W = {"l0_q": (2, 256), "l0_k": (2, 256), "l0_v": (2, 256), "l0_o": (2, 256), "l0_w1": (2, 1024),
           "l0_w2": (8, 256), "maa_w1": (2, 160), "decay_w1": (2, 64), "maa_w2": (1, 256),
           "wr": (2, 256), "wk": (2, 256), "wv": (2, 256), "wg": (2, 256)}
BACK_W = {"wo": (2, 256), "fwk": (2, 256), "fwr": (2, 256), "fwv": (2, 256), "l2_q": (2, 256), "l2_k": (2, 256),
          "l2_v": (2, 256), "l2_o": (2, 256), "l2_q2": (2, 256), "l2_k2": (2, 256), "l2_v2": (2, 256),
          "l2_o2": (2, 256), "l2_w1": (2, 1024), "l2_w2": (8, 256), "l3_q": (2, 256), "l3_k": (2, 256),
          "l3_v": (2, 256), "l3_o": (2, 256)}
MIXES = [("maa_k", 1), ("maa_v", 2), ("maa_r", 3), ("maa_g", 4), ("maa_w", 0)]
KINDS = {"r": 0, "k": 1, "v": 2, "w": 3}


def width(table):
    return sum(k * n for k, n in table.values())


def bass_four_layers_kernel(nc, a):
    with ExitStack() as ctx:
        def sb(name, shape, dt=F32):
            return ctx.enter_context(nc.sbuf_tensor(name, [P] + shape, dt))

        passed = {}

        def after_wait(eng, name):
            if name not in passed:
                passed[name] = ctx.enter_context(nc.semaphore(f"{name}_passed"))
            eng.sem_inc(passed[name], 1)

        def part(tile, at, k, n):
            return tile[:, at:at + k * n].rearrange("p (k n) -> p k n", k=k)

        class Signal:

            def __init__(self, name, per, step=1):
                self.sem, self.per, self.step = ctx.enter_context(nc.semaphore(name)), per, step

            def at(self, g, k):
                assert 1 <= k <= self.per
                return (g * self.per + k) * self.step

            def before(self, g):
                return (g * self.per + 1) * self.step

        class Half:

            def __init__(self, name, tiles):
                self.bank = [ctx.enter_context(nc.psum_tensor(f"{name}_bank{i}", [P, 512], F32)) for i in range(4)]
                self.full = [ctx.enter_context(nc.semaphore(f"{name}_full{i}")) for i in range(4)]
                self.free = [ctx.enter_context(nc.semaphore(f"{name}_free{i}")) for i in range(4)]
                self.at, self.fills, self.frees = {}, [0] * 4, [0] * 4
                turn = 0
                for key, where, readers in tiles:
                    if where is None:
                        where, turn = turn, (turn + 1) % 3
                    self.at[key] = (where, self.fills[where] + 1, self.frees[where] + 1)
                    self.fills[where] += 1
                    self.frees[where] += readers
                self.xn = sb(f"{name}_xn", [TT, C])
                self.xnT = sb(f"{name}_xnT", [CT, T])
                self.heads = self.xn[:, :, :].rearrange("p t c -> p (t c)").rearrange("p (b k) -> p b k", b=G)
                self.headsT = self.xnT[:, :, :].rearrange("p r (b q) -> p r b q", b=G)
                self.stats = sb(f"{name}_stats", [TT, 6])
                self.mv = sb(f"{name}_mv", [TT, 2])
                self.nmax = sb(f"{name}_nmax", [4, PAIRS])
                self.rden = sb(f"{name}_rden", [2, 2 * PAIRS])

            def tile(self, *key):
                return self.bank[self.at[key][0]]

            def full_sem(self, *key):
                return self.full[self.at[key][0]]

            def full_at(self, g, *key):
                i, full, _ = self.at[key]
                return g * self.fills[i] + full

            def free_sem(self, *key):
                return self.free[self.at[key][0]]

            def free_at(self, g, *key):
                i, _, free = self.at[key]
                return g * self.frees[i] + free

        LAG = {"l0": 1, "a": 1, "b": 1, "c": 1}
        MASK_STEP = {"l0": 0, "a": 1, "b": 1, "c": 0}
        O_BANK = 3

        def attention_tiles(tag, units, per_out):
            out, lag = [], LAG[tag]
            for step in range(units + 2 + lag):
                if 0 <= step - 1 - lag < units:
                    out.append((("probsT", tag, step - 1 - lag), None, 1))
                if step < units:
                    out.append((("scores", tag, step), None, 1))
                if step >= 2 + lag and (step - 2 - lag) % per_out == 0:
                    out.append((("heads", tag, (step - 2 - lag) // per_out), O_BANK, 1))
            return out + [(("headsT", tag), None, 1), (("rows", tag), None, 1)]

        def mlp_tiles(tag):
            return [(("hidden", tag, m), None, 1) for m in range(FT // 2)] + [(("rows", tag), None, 1)]

        mix_tiles = []
        for n in range(len(MIXES) + 1):
            if n < len(MIXES):
                mix_tiles.append((("mix", MIXES[n][0]), None, 1))
            if n >= 1:
                name = MIXES[n - 1][0]
                if name == "maa_w":
                    mix_tiles += [(("decay1",), None, 1), (("decay2",), None, 1)]
                else:
                    mix_tiles.append((("proj", name), None, 2 if name == "maa_g" else 1))
        front_tiles = (
            [(("inT", ct), None, 1) for ct in range(CT)] + [(("q", "l0", 0), None, 1), (("q", "l0", 1), None, 1)]
            + [(("k", "l0", m), None, 2) for m in range(CT)] + [(("v", "l0", j), None, 1) for j in range(2)]
            + attention_tiles("l0", 2 * G, 4) + [(("normT", "l0"), None, 1)] + mlp_tiles("l0m")
            + [(("normT", "ln1"), None, 1), (("lora",), None, 1)] + mix_tiles
        )
        back_tiles = (
            [(("ctxT",), None, 1), (("rows", "wo"), None, 1), (("normT", "ln2"), None, 1), (("fk",), None, 1), (("fr",), None, 1), (("fv",), None, 1)]
            + [(("normT", "a"), None, 1), (("q", "a", 0), None, 1), (("q", "a", 1), None, 1), (("k", "a"), None, 2), (("v", "a"), None, 1)]
            + attention_tiles("a", G, 2)
            + [(("normT", "b"), None, 1), (("q", "b", 0), None, 1), (("q", "b", 1), None, 1), (("k", "b"), None, 2), (("v", "b"), None, 1)]
            + attention_tiles("b", G, 2)
            + [(("normT", "m"), None, 1)] + mlp_tiles("l2m")
            + [(("normT", "c"), None, 1), (("xT",), None, 1), (("q", "c", 0), None, 1), (("q", "c", 1), None, 1), (("k", "c"), None, 2), (("v", "c"), None, 1)]
            + attention_tiles("c", G, 2)
        )
        FB = Half("front", front_tiles)
        BB = Half("back", back_tiles)

        w_front = sb("w_front", [width(FRONT_W)])
        w_back = sb("w_back", [width(BACK_W)])

        def weights(tile, table):
            out, at = {}, 0
            for name, (k, n) in table.items():
                out[name] = tile[:, at:at + k * n].rearrange("p (k n) -> p k n", k=k)
                at += k * n
            return out

        W = {**weights(w_front, FRONT_W), **weights(w_back, BACK_W)}
        maa_w2g = sb("maa_w2g", [C])
        decay_w2 = sb("decay_w2", [C])
        vecs = sb("vecs", [NVEC])
        rows = sb("rows", [len(ROWS) * C])
        bv_half = sb("bv_half", [2 * P])
        ident = sb("ident", [P])
        parity = sb("parity", [2])
        par16 = sb("par16", [2])
        par4 = sb("par4", [2])
        qb = sb("qb", [3, 2])
        bonus_u = sb("bonus_u", [SH])
        tgate = sb("tgate", [2])
        ones_bf = sb("ones_bf", [P], BF16)
        mask0_raw = sb("mask0_raw", [T], I32)
        mask3_raw = sb("mask3_raw", [T], mybir.dt.uint8)
        mask0 = sb("mask0", [G, P], BF16)
        mask3 = sb("mask3", [T], BF16)
        self_m = sb("self_m", [S])
        self_c = sb("self_c", [S])
        cross_m = sb("cross_m", [G, S])
        cross_c = sb("cross_c", [G, S])

        x_in = sb("x_in", [TT, C])
        ctx_in = FB.xn
        in_region = sb("in_region", [CT * G * P])
        inT = in_region[:, :].rearrange("p (h b t) -> p h b t", h=CT, b=G)
        x1 = sb("x1", [TT, C])
        xaS = sb("xaS", [CT, G, S + 1])
        gate2 = sb("gate2", [CT, T])
        sx = part(in_region, 0, CT, T)
        lora_t = part(in_region, CT * T, 2, T)
        wide_region = sb("wide_region", [FT * T])
        FB.hidden = part(wide_region, 0, FT, T)
        rkvw = wide_region[:, :].rearrange("p (k h t) -> p k h t", k=4, h=CT)
        attn_region = sb("attn_region", [2 * CT * T + 2 * 512])
        FB.qeo = attn_region[:, 0:2 * CT * T].rearrange("p (m b r q) -> p m b r q", m=CT, b=G, r=2)
        FB.probs = part(attn_region, 2 * CT * T, 2, 512)
        dec_t = attn_region[:, 0:T]
        mixed = attn_region[:, 2 * CT * T:].rearrange("p (i h t) -> p i h t", i=2, h=CT)
        y_region = sb("y_region", [2 * 512])
        FB.probsT = part(y_region, 0, 2, 512)
        bonus, y = y_region[:, 0:SH * S], y_region[:, SH * S:]
        ysq = FB.xn[:, :, :].rearrange("p t c -> p (t c)")
        ysum = sb("ysum", [S])
        bonus_sum = sb("bonus_sum", [S])
        s0 = sb("s0", [SH * SH])
        z = attn_region[:, :].rearrange("p (k x) -> p k x", k=4)
        key_region = sb("key_region", [CT * PT_ * 2 * T])
        FB.kb = key_region[:, :].rearrange("p (m j t) -> p m j t", m=CT, j=PT_)
        HS = SH // 2
        state, decay = (key_region[:, i * HS * SH * S:(i + 1) * HS * SH * S].rearrange("p (s v t) -> p s v t", s=HS, v=SH)
                        for i in range(2))
        va = sb("va", [G, 2 * PAIRS, D + 1])
        sumsq = sb("sumsq", [TT])
        FB.nw = sb("front_nw", [3, S])

        ctx_b = sb("ctx_b", [TT, C])
        ctxT = sb("ctxT", [CT, G, S])
        bx = sb("bx", [TT, C])
        g_in = sb("g_in", [CT, T])
        xcS = sb("xcS", [CT, G, S + 1])
        vb = sb("vb", [G, PT_, 2, 2, D + 1])
        rr = sb("rr", [TT, C])
        yT = sb("yT", [CT, T])
        o_out = part(yT[:, :, :].rearrange("p h t -> p (h t)"), 0, TT, C)
        BB.nw = sb("back_nw", [3, TT])
        mix_region = sb("mix_region", [4 * CT * T])
        sxc, xk2, xr2, kk = (part(mix_region, i * CT * T, CT, T) for i in range(4))
        BB.qeo = mix_region[:, 0:2 * CT * T].rearrange("p (m b r q) -> p m b r q", m=CT, b=G, r=2)
        BB.probs = part(mix_region, 2 * CT * T, 2, 512)
        BB.probsT = sb("back_probsT", [2, 512])
        BB.hidden = sb("back_hidden", [FT, T])
        BB.kb = sb("back_kb", [CT, PT_, T])

        def vec(name, i=0):
            at = VEC_AT[name] + i
            return vecs[:, at:at + 1]

        def row(name):
            at = ROWS.index(name) * C
            return rows[:, at:at + C]

        d_rkvw = nc.dram_tensor("d_rkvw", [NG, 4, P, SH * S], F32, kind="Internal").ap()
        d_gate = nc.dram_tensor("d_gate", [NG, CT, P, T], F32, kind="Internal").ap()
        d_x1 = nc.dram_tensor("d_x1", [NG, T, C], F32, kind="Internal").ap()
        d_y = nc.dram_tensor("d_y", [NG, P, SH * S], F32, kind="Internal").ap()
        x_d = a["x"].rearrange("(g b) s c -> g (b s) c", g=NG)
        ctx_d = a["ctx"].rearrange("(g b) s c -> g (b s) c", g=NG)
        out_d = a["out"].rearrange("(g b) s c -> g (b s) c", g=NG)

        loaded = Signal("constants_loaded", 1, 16)
        NLOADS = 19
        ready = Signal("constants_ready", 1)
        NREADY = 7
        stored = Signal("stored", 1, 16)
        sig = {}

        def new(name, per, step=1):
            sig[name] = Signal(name, per, step)

        new("x_loaded", 3, 16)
        new("back_loaded", 6, 16)
        new("mask0", 1)
        new("mask3", 1)
        new("inT", CT)
        new("x_bias", 2)
        new("x1_stored", 1, 16)
        for tag in ("l0", "a", "b", "c"):
            units = 2 * G if tag == "l0" else G
            new(f"q_{tag}", 2)
            new(f"k_{tag}", 4 if tag == "l0" else 2)
            new(f"v_{tag}", 2 if tag == "l0" else 1)
            if tag in "ab":
                new(f"masked_{tag}", units)
                new(f"added_{tag}", units)
            new(f"shifted_{tag}", units)
            new(f"probs_{tag}", units)
            new(f"probsT_{tag}", units)
            new(f"heads_{tag}", 2)
            new(f"headsT_{tag}", 1)
        new("attn_l0", 1)
        for tag in ("l0", "ln1", "ln2", "a", "b", "m", "c"):
            new(f"variance_{tag}", 1)
            new(f"rstd_{tag}", 1)
            new(f"normed_{tag}", 1)
            new(f"normT_{tag}", 1)
        new("hidden_l0m", FT)
        new("hidden_l2m", FT)
        new("x1", 1)
        new("state_col1", 1)
        new("xxx", 1)
        new("lora", 1)
        new("half_mix", 5)
        new("mix", 5)
        new("dec_t", 1)
        new("rkvw", 4)
        new("th_g", 1)
        new("gate2", 1)
        new("scratch_stored", 10, 16)
        new("z_loaded", 2, 16)
        new("state_in", 4)
        new("decay_in", 4)
        new("scanned", 2)
        new("y_part", 1)
        new("keys_cleared", 1)
        new("bonus", 1)
        new("variance_y", 1)
        new("rstd_y", 1)
        new("y_normed", 1)
        new("y_stored", 1, 16)
        new("yT_loaded", CT * G, 16)
        new("gated", 1)
        new("ctxT", 1)
        new("bx", 5)
        new("bx_bias", 3)
        new("state_col2", 1)
        new("xk2", 1)
        new("xr2", 1)
        new("kk", 1)
        new("rr", 1)
        new("xT", 1)
        new("o_out", 1)

        STAGES = (
            "FFFBBBFFBFBBFFBFBBFBFFFBFBFBBBBFBFBFBFBFBFBFBFBFBBFBFBFBBFFBFBFFBBFBBFBBBBFBB"
        )

        def run(front=None, back=None):
            stages = {"F": front, "B": back}
            for half in STAGES:
                if stages[half] is not None:
                    next(stages[half])
            for half in (front, back):
                assert half is None or next(half, "end") == "end"

        def all_groups(eng, front, back):
            run(front=front(eng, 0))
            with eng.Fori(0, NG - 1) as g:
                run(front=front(eng, g + 1), back=back(eng, g))
            run(back=back(eng, NG - 1))

        def is_first(g):
            return isinstance(g, int) and g == 0

        block = ctx.enter_context(nc.Block())

        def store_kind(sp, g, kind):
            n = KINDS[kind]
            for ct in range(CT):
                dst = d_rkvw[g, n].rearrange("(b h) (s t) -> (h s) b t", b=G, s=SH)[ct * P:(ct + 1) * P]
                sp.dma_start(dst, rkvw[:, n, ct, :].rearrange("p (b t) -> p b t", b=G)).then_inc(sig["scratch_stored"].sem, 16)

        def idle(stages):
            for _ in range(stages):
                yield

        def sp_front(sp, g):
            yield from idle(17)
            sp.wait_ge(sig["x1"].sem, sig["x1"].at(g, 1))
            after_wait(sp, "sync")
            sp.dma_start(d_x1[g].rearrange("(t p) c -> p t c", p=P), x1[:, :, :]).then_inc(sig["x1_stored"].sem, 16)
            yield
            yield from idle(3)
            for n, kind in enumerate(("k", "v", "r")):
                sp.wait_ge(sig["rkvw"].sem, sig["rkvw"].at(g, n + 1))
                after_wait(sp, "sync")
                store_kind(sp, g, kind)
                yield
            yield
            sp.wait_ge(sig["gate2"].sem, sig["gate2"].at(g, 1))
            after_wait(sp, "sync")
            for ct in range(CT):
                sp.dma_start(d_gate[g, ct], gate2[:, ct, :]).then_inc(sig["scratch_stored"].sem, 16)
            yield
            sp.wait_ge(sig["rkvw"].sem, sig["rkvw"].at(g, 4))
            after_wait(sp, "sync")
            store_kind(sp, g, "w")
            yield
            sp.wait_ge(sig["x1_stored"].sem, sig["x1_stored"].at(g, 1))
            sp.wait_ge(sig["scratch_stored"].sem, sig["scratch_stored"].at(g, 10))
            after_wait(sp, "sync")
            sp.dma_start(z[:, :, :], d_rkvw[g].rearrange("k p x -> p k x")).then_inc(sig["z_loaded"].sem, 16)
            sp.dma_start(s0[:, :], a["s0"][g]).then_inc(sig["z_loaded"].sem, 16)
            yield
            yield from idle(6)
            sp.wait_ge(sig["y_normed"].sem, sig["y_normed"].at(g, 1))
            after_wait(sp, "sync")
            sp.dma_start(d_y[g], y[:, :]).then_inc(sig["y_stored"].sem, 16)
            yield

        def sp_back(sp, g):
            sp.wait_ge(sig["y_stored"].sem, sig["y_stored"].at(g, 1))
            after_wait(sp, "sync")
            sp.dma_start(ctx_b[:, :, :], ctx_d[g].rearrange("(t p) c -> p t c", p=P)).then_inc(sig["back_loaded"].sem, 16)
            sp.dma_start(mask3_raw[0:1, :], a["mask3"][g]).then_inc(sig["back_loaded"].sem, 16)
            for half in range(2):
                sp.dma_start(cross_m[64 * half:64 * half + 64, :, :], a["cross_mask"][g].rearrange("b q k -> q b k")).then_inc(sig["back_loaded"].sem, 16)
            sp.dma_start(bx[:, :, :], d_x1[g].rearrange("(t p) c -> p t c", p=P)).then_inc(sig["back_loaded"].sem, 16)
            sp.dma_start(g_in[:, :, :], d_gate[g].rearrange("h p x -> p h x")).then_inc(sig["back_loaded"].sem, 16)
            sp.wait_ge(stored.sem, stored.before(g))
            after_wait(sp, "sync")
            for ct in range(CT):
                for b in range(G):
                    src = d_y[g].rearrange("(b h) (v t) -> b (h v) t", b=G, v=SH)
                    sp.dma_start(yT[:, ct, b * S:(b + 1) * S], src[b, ct * P:(ct + 1) * P]).then_inc(sig["yT_loaded"].sem, 16)
            yield
            yield from idle(40)
            sp.wait_ge(sig["o_out"].sem, sig["o_out"].at(g, 1))
            after_wait(sp, "sync")
            sp.dma_start(out_d[g].rearrange("(t p) c -> p t c", p=P), o_out[:, :, :]).then_inc(stored.sem, 16)
            yield

        @block.sync
        def _(sp):
            def load(dst, src):
                sp.dma_start(dst, src).then_inc(loaded.sem, 16)

            nf = width(FRONT_W)
            load(ident[:, :], a["ident"])
            load(parity[:, :], a["parity"])
            load(vecs[:, :], a["vecs"])
            load(rows[:, :], a["rows"].partition_broadcast(P))
            load(bv_half[0:64, :], a["bv_half"][0:1, :].partition_broadcast(64))
            load(bv_half[64:128, :], a["bv_half"][1:2, :].partition_broadcast(64))
            load(maa_w2g[0:32, :], a["maa_w2g"])
            load(decay_w2[0:64, :], a["decay_w2"])
            for b in range(G):
                load(bonus_u[b * 32:(b + 1) * 32, :], a["faaaa"])
            load(tgate[:, 0:1], a["gate"].partition_broadcast(P))
            load(self_m[0:64, :], a["self_mask"])
            load(self_m[64:128, :], a["self_mask"])
            load(w_front[:, 0:2048], a["w_front"][:, 0:2048])
            load(w_front[:, 2048:nf], a["w_front"][:, 2048:nf])
            load(w_back[:, 0:4096], a["w_back"][:, 0:4096])
            load(w_back[:, 4096:], a["w_back"][:, 4096:])
            all_groups(sp, sp_front, sp_back)
            sp.wait_ge(stored.sem, 16 * (NG + 1))

        def tokens(ap):
            return ap.rearrange("p (b t) -> p b t", b=G)

        def pe_transposes(pe, K, g, key, sources):
            pe.wait_ge(K.free_sem(*key), K.free_at(g, *key))
            t = K.tile(*key)
            for i, src in enumerate(sources):
                ins = pe.transpose(t[:, i * P:(i + 1) * P], src, ident[:, :])
            ins.then_inc(K.full_sem(*key), 1)

        def pe_cols(pe, K, g, key, w, x, halves=CT):
            pe.wait_ge(K.free_sem(*key), K.free_at(g, *key))
            t = K.tile(*key)
            for m in range(halves):
                for ct in range(CT):
                    o = t[:, m * T:(m + 1) * T]
                    r = x(ct)
                    if len(r.shape) == 3:
                        o = o.rearrange("p (b t) -> p b t", b=G)
                    ins = pe.matmul(o, w[:, ct, m * P:(m + 1) * P], r, start=(ct == 0), stop=(ct == CT - 1))
            ins.then_inc(K.full_sem(*key), 1)

        def pe_queries(pe, K, g, tag, w, x):
            for m in range(CT):
                pe.wait_ge(K.free_sem("q", tag, m), K.free_at(g, "q", tag, m))
                t = K.tile("q", tag, m)
                for ct in range(CT):
                    r = x(ct)
                    o = tokens(t[:, 0:T]) if len(r.shape) == 3 else t[:, 0:T]
                    ins = pe.matmul(o, w[:, ct, m * P:(m + 1) * P], r, start=(ct == 0), stop=(ct == CT - 1))
                ins.then_inc(K.full_sem("q", tag, m), 1)

        def pe_rows(pe, K, g, key, w, x, n_k, wait=None):
            pe.wait_ge(K.free_sem(*key), K.free_at(g, *key))
            t = K.tile(*key)
            for tt in range(TT):
                for k in range(n_k):
                    if wait is not None and tt == 0:
                        wait(k)
                    ins = pe.matmul(t[:, tt * C:(tt + 1) * C], x(k, tt), w[:, k, :], start=(k == 0), stop=(k == n_k - 1))
            ins.then_inc(K.full_sem(*key), 1)

        def pe_attention(pe, K, g, tag, w_o):
            units, per_out = (2 * G, 4) if tag == "l0" else (G, 2)
            keys = P if tag == "l0" else S

            def scores(u):
                pe.wait_ge(K.free_sem("scores", tag, u), K.free_at(g, "scores", tag, u))
                t = K.tile("scores", tag, u)
                b = u // 2 if tag == "l0" else u
                for m in ([u % 2] if tag == "l0" else range(CT)):
                    at = 0 if tag == "l0" else m * PT_ * keys
                    o = t[:, at:at + PT_ * keys].rearrange("p (j k) -> p j k", j=PT_)
                    q = K.qeo[:, m, b, :, :].rearrange("p r q -> p (r q)")
                    masked = tag in ("l0", "c")
                    ins = pe.matmul(o, q, K.kb[:, m, :, b * keys:(b + 1) * keys], start=True, stop=not masked)
                    if masked:
                        mask = mask0[0:1, b, :] if tag == "l0" else mask3[0:1, b * S:(b + 1) * S]
                        ins = pe.matmul(o, ones_bf[0:1, :], mask.unsqueeze(1).to_broadcast([1, PT_, keys]),
                                        start=False, stop=True)
                ins.then_inc(K.full_sem("scores", tag, u), 1)

            def weighted(u):
                pe.wait_ge(sig[f"probsT_{tag}"].sem, sig[f"probsT_{tag}"].at(g, u + 1))
                key = ("heads", tag, u // per_out)
                if u % per_out == 0:
                    pe.wait_ge(K.free_sem(*key), K.free_at(g, *key))
                t = K.tile(*key)
                b = u // 2 if tag == "l0" else u
                base = (b % 2) * PAIRS * (D + 1)
                for i in range(PT_):
                    for r in range(2):
                        pT = K.probsT[:, u % 2, i * P + r * S:i * P + (r + 1) * S]
                        if tag == "l0":
                            at, n = base + ((u % 2) * PT_ + i) * (D + 1), D + 1
                            v = va[:, b, (u % 2) * PAIRS + 2 * i + r, :]
                        else:
                            at, n = base + i * 2 * (D + 1), 2 * (D + 1)
                            v = vb[:, b, i, r, :, :].rearrange("p h e -> p (h e)")
                        ins = pe.matmul(t[r * S:(r + 1) * S, at:at + n], pT, v, start=True, stop=True)
                if u % per_out == per_out - 1:
                    ins.then_inc(K.full_sem(*key), 1)

            pe.wait_ge(sig[f"q_{tag}"].sem, sig[f"q_{tag}"].at(g, 2))
            pe.wait_ge(sig[f"k_{tag}"].sem, sig[f"k_{tag}"].at(g, 4 if tag == "l0" else 2))
            if tag in ("l0", "c"):
                pe.wait_ge(sig["mask0" if tag == "l0" else "mask3"].sem, sig["mask0" if tag == "l0" else "mask3"].at(g, 1))
            lag = LAG[tag]
            for step in range(units + 2 + lag):
                u = step - 1 - lag
                if 0 <= u < units:
                    pe.wait_ge(sig[f"probs_{tag}"].sem, sig[f"probs_{tag}"].at(g, u + 1))
                    pe_transposes(pe, K, g, ("probsT", tag, u), [K.probs[:, u % 2, i * P:(i + 1) * P] for i in range(4)])
                if step < units:
                    scores(step)
                if u == 1:
                    pe.wait_ge(sig[f"v_{tag}"].sem, sig[f"v_{tag}"].at(g, 2 if tag == "l0" else 1))
                if u >= 1:
                    weighted(u - 1)
                yield
            pe.wait_ge(sig[f"heads_{tag}"].sem, sig[f"heads_{tag}"].at(g, 2))
            pe_transposes(pe, K, g, ("headsT", tag), [K.heads[:, b, :] for b in range(G)])
            yield
            pe.wait_ge(sig[f"headsT_{tag}"].sem, sig[f"headsT_{tag}"].at(g, 1))
            pe_rows(pe, K, g, ("rows", tag), w_o,
                    lambda r, tt: K.headsT[:, r, 2 * tt:2 * tt + 2, :].rearrange("p b q -> p (b q)"), 2)
            yield

        def pe_normT(pe, K, g, tag):
            pe.wait_ge(sig[f"normed_{tag}"].sem, sig[f"normed_{tag}"].at(g, 1))
            pe_transposes(pe, K, g, ("normT", tag), [K.xn[:, tt, ct * P:(ct + 1) * P] for ct in range(CT) for tt in range(TT)])

        def pe_mlp(pe, K, g, tag, w1, w2):
            for m in range(FT // 2):
                pe.wait_ge(K.free_sem("hidden", tag, m), K.free_at(g, "hidden", tag, m))
                t = K.tile("hidden", tag, m)
                for i in range(2):
                    for ct in range(CT):
                        ins = pe.matmul(t[:, i * T:(i + 1) * T], w1[:, ct, (2 * m + i) * P:(2 * m + i + 1) * P],
                                        K.xnT[:, ct, :], start=(ct == 0), stop=(ct == CT - 1))
                ins.then_inc(K.full_sem("hidden", tag, m), 1)
            yield
            pe_rows(pe, K, g, ("rows", tag), w2, lambda k, tt: K.hidden[:, k, tt * P:(tt + 1) * P], FT,
                    wait=lambda k: pe.wait_ge(sig[f"hidden_{tag}"].sem, sig[f"hidden_{tag}"].at(g, k + 1)))
            yield

        def pe_kv(pe, K, g, tag, x, w_k, w_v):
            pe_cols(pe, K, g, ("k", tag), w_k, x)
            pe.wait_ge(K.free_sem("v", tag), K.free_at(g, "v", tag))
            t = K.tile("v", tag)
            for b in range(G):
                for h in range(2):
                    for ct in range(CT):
                        xb = x(ct)
                        xb = xb[:, b, :] if len(xb.shape) == 3 else xb[:, b * S:(b + 1) * S]
                        ins = pe.matmul(t[h * S:(h + 1) * S, b * P:(b + 1) * P], xb, w_v[:, ct, h * P:(h + 1) * P],
                                        start=(ct == 0), stop=(ct == CT - 1))
            ins.then_inc(K.full_sem("v", tag), 1)

        def pe_front(pe, g):
            K = FB
            pe.wait_ge(sig["x_loaded"].sem, sig["x_loaded"].at(g, 3))
            for ct in range(CT):
                pe_transposes(pe, K, g, ("inT", ct),
                              [t[:, tt, ct * P:(ct + 1) * P] for t in (ctx_in, x_in) for tt in range(TT)])
            yield
            pe.wait_ge(sig["inT"].sem, sig["inT"].at(g, 2))
            pe_queries(pe, K, g, "l0", W["l0_q"], lambda ct: inT[:, ct, :, S:P])
            for m in range(CT):
                pe.wait_ge(K.free_sem("k", "l0", m), K.free_at(g, "k", "l0", m))
                t = K.tile("k", "l0", m)
                for ct in range(CT):
                    ins = pe.matmul(t[:, :], W["l0_k"][:, ct, m * P:(m + 1) * P],
                                    inT[:, ct, :, :].rearrange("p b t -> p (b t)"), start=(ct == 0), stop=(ct == CT - 1))
                ins.then_inc(K.full_sem("k", "l0", m), 1)
            for j in range(2):
                pe.wait_ge(K.free_sem("v", "l0", j), K.free_at(g, "v", "l0", j))
                t = K.tile("v", "l0", j)
                for i in range(2):
                    for ct in range(CT):
                        ins = pe.matmul(t[:, i * C:(i + 1) * C], inT[:, ct, 2 * j + i, :], W["l0_v"][:, ct, :],
                                        start=(ct == 0), stop=(ct == CT - 1))
                ins.then_inc(K.full_sem("v", "l0", j), 1)
            yield
            yield from pe_attention(pe, K, g, "l0", W["l0_o"])
            pe_normT(pe, K, g, "l0")
            yield
            pe.wait_ge(sig["normT_l0"].sem, sig["normT_l0"].at(g, 1))
            yield from pe_mlp(pe, K, g, "l0m", W["l0_w1"], W["l0_w2"])
            pe_normT(pe, K, g, "ln1")
            yield
            pe.wait_ge(sig["xxx"].sem, sig["xxx"].at(g, 1))
            pe.wait_ge(K.free_sem("lora"), K.free_at(g, "lora"))
            t = K.tile("lora")
            for ct in range(CT):
                pe.matmul(t[:, 0:T], W["maa_w1"][:, ct, 0:P], mixed[:, 0, ct, :], start=(ct == 0), stop=(ct == CT - 1))
            for ct in range(CT):
                ins = pe.matmul(t[0:32, T:2 * T], W["maa_w1"][:, ct, P:160], mixed[:, 0, ct, :],
                                start=(ct == 0), stop=(ct == CT - 1))
            ins.then_inc(K.full_sem("lora"), 1)
            yield
            pe.wait_ge(sig["lora"].sem, sig["lora"].at(g, 1))
            for n in range(len(MIXES) + 1):
                if n < len(MIXES):
                    name, f = MIXES[n]
                    pe.wait_ge(K.free_sem("mix", name), K.free_at(g, "mix", name))
                    t = K.tile("mix", name)
                    for ct in range(CT):
                        if f < 4:
                            w, r = W["maa_w2"][32 * f:32 * f + 32, 0, ct * P:(ct + 1) * P], lora_t[32 * f:32 * f + 32, 0, :]
                        else:
                            w, r = maa_w2g[0:32, ct * P:(ct + 1) * P], lora_t[0:32, 1, :]
                        ins = pe.matmul(t[:, ct * T:(ct + 1) * T], w, r, start=True, stop=True)
                    ins.then_inc(K.full_sem("mix", name), 1)
                if n >= 1:
                    name = MIXES[n - 1][0]
                    pe.wait_ge(sig["mix"].sem, sig["mix"].at(g, n))
                    x = lambda ct: mixed[:, n % 2, ct, :]
                    if name != "maa_w":
                        pe_cols(pe, K, g, ("proj", name), W["w" + name[-1]], x)
                        yield
                        continue
                    pe.wait_ge(K.free_sem("decay1"), K.free_at(g, "decay1"))
                    t = K.tile("decay1")
                    for ct in range(CT):
                        ins = pe.matmul(t[0:64, 0:T], W["decay_w1"][:, ct, :], x(ct), start=(ct == 0), stop=(ct == CT - 1))
                    ins.then_inc(K.full_sem("decay1"), 1)
                    yield
                    pe.wait_ge(sig["dec_t"].sem, sig["dec_t"].at(g, 1))
                    pe.wait_ge(K.free_sem("decay2"), K.free_at(g, "decay2"))
                    t = K.tile("decay2")
                    for m in range(CT):
                        ins = pe.matmul(t[:, m * T:(m + 1) * T], decay_w2[0:64, m * P:(m + 1) * P], dec_t[0:64, :],
                                        start=True, stop=True)
                    ins.then_inc(K.full_sem("decay2"), 1)
                    yield
                else:
                    yield
            yield from idle(8)

        def pe_back(pe, g):
            K = BB
            pe.wait_ge(sig["back_loaded"].sem, sig["back_loaded"].at(g, 6))
            pe_transposes(pe, K, g, ("ctxT",), [ctx_b[:, tt, ct * P:(ct + 1) * P] for ct in range(CT) for tt in range(TT)])
            yield
            pe.wait_ge(sig["gated"].sem, sig["gated"].at(g, 1))
            pe_rows(pe, K, g, ("rows", "wo"), W["wo"], lambda ct, tt: yT[:, ct, tt * P:(tt + 1) * P], CT)
            yield
            yield
            pe_normT(pe, K, g, "ln2")
            yield
            pe.wait_ge(sig["xk2"].sem, sig["xk2"].at(g, 1))
            pe_cols(pe, K, g, ("fk",), W["fwk"], lambda ct: xk2[:, ct, :])
            pe.wait_ge(sig["xr2"].sem, sig["xr2"].at(g, 1))
            pe_rows(pe, K, g, ("fr",), W["fwr"], lambda ct, tt: xr2[:, ct, tt * P:(tt + 1) * P], CT)
            yield
            pe.wait_ge(sig["kk"].sem, sig["kk"].at(g, 1))
            pe_rows(pe, K, g, ("fv",), W["fwv"], lambda ct, tt: kk[:, ct, tt * P:(tt + 1) * P], CT)
            yield
            x = lambda ct: K.xnT[:, ct, :]
            pe_normT(pe, K, g, "a")
            yield
            pe.wait_ge(sig["normT_a"].sem, sig["normT_a"].at(g, 1))
            pe_queries(pe, K, g, "a", W["l2_q"], x)
            pe_kv(pe, K, g, "a", x, W["l2_k"], W["l2_v"])
            yield
            yield from pe_attention(pe, K, g, "a", W["l2_o"])
            pe_normT(pe, K, g, "b")
            yield
            pe.wait_ge(sig["normT_b"].sem, sig["normT_b"].at(g, 1))
            pe_queries(pe, K, g, "b", W["l2_q2"], x)
            pe.wait_ge(sig["ctxT"].sem, sig["ctxT"].at(g, 1))
            pe_kv(pe, K, g, "b", lambda ct: ctxT[:, ct, :, :], W["l2_k2"], W["l2_v2"])
            yield
            yield from pe_attention(pe, K, g, "b", W["l2_o2"])
            pe_normT(pe, K, g, "m")
            yield
            pe.wait_ge(sig["normT_m"].sem, sig["normT_m"].at(g, 1))
            yield from pe_mlp(pe, K, g, "l2m", W["l2_w1"], W["l2_w2"])
            pe_normT(pe, K, g, "c")
            pe.wait_ge(sig["bx"].sem, sig["bx"].at(g, 5))
            pe_transposes(pe, K, g, ("xT",), [bx[:, tt, ct * P:(ct + 1) * P] for ct in range(CT) for tt in range(TT)])
            yield
            pe.wait_ge(sig["xT"].sem, sig["xT"].at(g, 1))
            pe_queries(pe, K, g, "c", W["l3_q"], lambda ct: yT[:, ct, :])
            pe.wait_ge(sig["normT_c"].sem, sig["normT_c"].at(g, 1))
            pe_kv(pe, K, g, "c", x, W["l3_k"], W["l3_v"])
            yield
            yield from pe_attention(pe, K, g, "c", W["l3_o"])

        @block.tensor
        def _(pe):
            pe.wait_ge(loaded.sem, 16 * NLOADS)
            pe.wait_ge(ready.sem, NREADY)
            all_groups(pe, pe_front, pe_back)

        def v_variance(v, K, g, tag, x):
            v.drain()
            for tt in range(TT):
                v.bn_stats(K.stats[:, tt, :], x[:, tt, :])
            v.drain()
            for tt in range(TT):
                v.bn_aggr(K.mv[:, tt, :], K.stats[:, tt, :])
            v.drain()
            v.tensor_scalar(K.nw[:, 0, 0:TT], K.mv[:, :, 1], 1e-5, None, ALU.add).then_inc(sig[f"variance_{tag}"].sem, 1)

        def v_norm(v, K, g, tag, x):
            v.wait_ge(sig[f"rstd_{tag}"].sem, sig[f"rstd_{tag}"].at(g, 1))
            for tt in range(TT):
                ins = v.tensor_scalar(K.xn[:, tt, :], x[:, tt, :], K.mv[:, tt, 0:1], K.nw[:, 1, tt:tt + 1],
                                      ALU.subtract, ALU.mult)
            ins.then_inc(sig[f"normed_{tag}"].sem, 1)

        def v_queries(v, K, g, tag, bias, scale):
            v.wait_ge(K.full_sem("q", tag, 1), K.full_at(g, "q", tag, 1))
            t = K.tile("q", tag, 1)
            for r in range(2):
                src = tokens(t[:, 0:T])
                if bias:
                    ins = v.tensor_scalar(K.qeo[:, 1, :, r, :], src, vec(bias, 1), scale[:, r:r + 1], ALU.add, ALU.mult)
                else:
                    ins = v.tensor_scalar(K.qeo[:, 1, :, r, :], src, scale[:, r:r + 1], None, ALU.mult)
            ins.then_inc(K.free_sem("q", tag, 1), 1)
            v.drain().then_inc(sig[f"q_{tag}"].sem, 1)

        def v_keys(v, K, g, tag, bias):
            v.wait_ge(K.full_sem("k", tag), K.full_at(g, "k", tag))
            t = K.tile("k", tag)
            for j in (2, 3):
                q = slice(32 * j, 32 * j + 32)
                src = t[q, :].rearrange("p (m t) -> p m t", m=CT)
                if bias:
                    at = VEC_AT[bias]
                    ins = v.tensor_tensor(K.kb[q, :, j, 0:T], src, vecs[q, at:at + CT].unsqueeze(2).to_broadcast([32, CT, T]), ALU.add)
                else:
                    ins = v.tensor_copy(K.kb[q, :, j, 0:T], src)
            ins.then_inc(K.free_sem("k", tag), 1)
            v.drain().then_inc(sig[f"k_{tag}"].sem, 1)

        def v_values(v, K, g, tag, bias_at):
            v.wait_ge(K.full_sem("v", tag), K.full_at(g, "v", tag))
            t = K.tile("v", tag)
            for h in range(2):
                q = slice(h * S, (h + 1) * S)
                src = t[q, :].rearrange("p (b e d) -> p b e d", b=G, e=2 * PT_)
                dst = vb[q, :, :, :, h, 0:D].rearrange("p b i r d -> p b (i r) d")
                if bias_at is None:
                    ins = v.tensor_copy(dst, src)
                else:
                    bias = bv_half[q, bias_at:bias_at + P].rearrange("p (e d) -> p e d", d=D)
                    ins = v.tensor_tensor(dst, src, bias.unsqueeze(1).to_broadcast([S, G, 2 * PT_, D]), ALU.add)
            ins.then_inc(K.free_sem("v", tag), 1)
            v.drain().then_inc(sig[f"v_{tag}"].sem, 1)

        def v_attention(v, K, g, tag):
            units, per_out = (2 * G, 4) if tag == "l0" else (G, 2)
            n, keys = (PT_, P) if tag == "l0" else (PAIRS, S)

            def grid(ap):
                return ap.rearrange("p (j k) -> p j k", j=n)

            def shift(u, src, slot):
                v.tensor_reduce(K.nmax[:, u % 4, 0:n], src, AX_X, ALU.max, negate=True)
                v.drain()
                ins = v.tensor_tensor(grid(K.probs[:, slot, :]), src, K.nmax[:, u % 4, 0:n].unsqueeze(2).to_broadcast([P, n, keys]), ALU.add)
                return ins

            if tag == "a":
                v.wait_ge(sig["back_loaded"].sem, sig["back_loaded"].at(g, 6))

            def masked(u):
                v.wait_ge(K.full_sem("scores", tag, u), K.full_at(g, "scores", tag, u))
                t = K.tile("scores", tag, u)
                m = self_m[:, :] if tag == "a" else cross_m[:, u, :]
                ins = v.tensor_tensor(grid(K.probs[:, u % 2, :]), grid(t[:, :]), m.unsqueeze(1).to_broadcast([P, n, keys]), ALU.mult)
                ins.then_inc(K.free_sem("scores", tag, u), 1)
                v.drain().then_inc(sig[f"masked_{tag}"].sem, 1)

            def out(j):
                v.wait_ge(K.full_sem("heads", tag, j), K.full_at(g, "heads", tag, j))
                t = K.tile("heads", tag, j)
                o = t[:, 0:2 * PAIRS * (D + 1)].rearrange("p (n e) -> p n e", e=D + 1)
                v.reciprocal(K.rden[:, j, :], o[:, :, D])
                v.drain()
                ins = v.tensor_tensor(K.heads[:, 2 * j:2 * j + 2, :].rearrange("p b (n d) -> p (b n) d", d=D), o[:, :, 0:D],
                                      K.rden[:, j, :].unsqueeze(2).to_broadcast([P, 2 * PAIRS, D]), ALU.mult)
                ins.then_inc(K.free_sem("heads", tag, j), 1)
                v.drain().then_inc(sig[f"heads_{tag}"].sem, 1)

            lag = LAG[tag]
            for step in range(units + 2 + lag):
                if tag in "ab":
                    if step < units:
                        masked(step)
                    if 1 <= step <= units:
                        u = step - 1
                        v.wait_ge(sig[f"added_{tag}"].sem, sig[f"added_{tag}"].at(g, u + 1))
                        shift(u, grid(K.probs[:, u % 2, :]), u % 2).then_inc(sig[f"shifted_{tag}"].sem, 1)
                elif step < units:
                    v.wait_ge(K.full_sem("scores", tag, step), K.full_at(g, "scores", tag, step))
                    t = K.tile("scores", tag, step)
                    ins = shift(step, grid(t[:, :]), step % 2)
                    ins.then_inc(K.free_sem("scores", tag, step), 1)
                    v.drain().then_inc(sig[f"shifted_{tag}"].sem, 1)
                done = step - 1 - lag
                if done >= per_out and done % per_out == 0:
                    out(done // per_out - 1)
                yield
            yield

        def v_add_rows(v, K, g, key, out, x):
            v.wait_ge(K.full_sem(*key), K.full_at(g, *key))
            t = K.tile(*key)
            ins = v.tensor_tensor(out[:, :, :].rearrange("p t c -> p (t c)"), t[:, :], x[:, :, :].rearrange("p t c -> p (t c)"), ALU.add)
            ins.then_inc(K.free_sem(*key), 1)
            return ins

        def v_front(v, g):
            K = FB
            v.wait_ge(K.full_sem("inT", 1), K.full_at(g, "inT", 1))
            t = K.tile("inT", 1)
            ins = v.tensor_copy(inT[:, 1, :, :].rearrange("p b (u t) -> p u b t", u=2), t[:, :].rearrange("p (u b t) -> p u b t", u=2, b=G))
            ins.then_inc(K.free_sem("inT", 1), 1)
            v.drain().then_inc(sig["inT"].sem, 1)
            yield
            v_queries(v, K, g, "l0", "l0_bq", par16)
            for m in range(CT):
                v.wait_ge(K.full_sem("k", "l0", m), K.full_at(g, "k", "l0", m))
                t = K.tile("k", "l0", m)
                v.wait_ge(sig["keys_cleared"].sem, sig["keys_cleared"].at(g, 1))
                for j in (2, 3):
                    q = slice(32 * j, 32 * j + 32)
                    ins = v.tensor_scalar(K.kb[q, m, j, :], t[q, :], vecs[q, VEC_AT["l0_bk"] + m:VEC_AT["l0_bk"] + m + 1], None, ALU.add)
                ins.then_inc(K.free_sem("k", "l0", m), 1)
                v.drain().then_inc(sig["k_l0"].sem, 1)
            for j in range(2):
                v.wait_ge(K.full_sem("v", "l0", j), K.full_at(g, "v", "l0", j))
                t = K.tile("v", "l0", j)
                ins = v.tensor_tensor(va[:, 2 * j:2 * j + 2, :, 0:D], t[:, :].rearrange("p (b h d) -> p b h d", b=2, d=D),
                                      row("l0_bv").rearrange("p (h d) -> p h d", d=D).unsqueeze(1).to_broadcast([P, 2, 2 * PAIRS, D]), ALU.add)
                ins.then_inc(K.free_sem("v", "l0", j), 1)
                v.drain().then_inc(sig["v_l0"].sem, 1)
            yield
            yield from v_attention(v, K, g, "l0")
            v.wait_ge(sig["x_bias"].sem, sig["x_bias"].at(g, 2))
            v_add_rows(v, K, g, ("rows", "l0"), x1, x1)
            v.drain().then_inc(sig["attn_l0"].sem, 1)
            yield
            v.wait_ge(sig["rstd_l0"].sem, sig["rstd_l0"].at(g, 1))
            for tt in range(TT):
                ins = v.tensor_scalar(K.xn[:, tt, :], x1[:, tt, :], K.nw[:, 1, tt:tt + 1], None, ALU.mult)
            ins.then_inc(sig["normed_l0"].sem, 1)
            yield
            yield
            v_add_rows(v, K, g, ("rows", "l0m"), x1, x_in)
            v.drain().then_inc(sig["x1"].sem, 1)
            v_variance(v, K, g, "ln1", x1)
            yield
            v_norm(v, K, g, "ln1", x1)
            yield
            v_shift(v, g, "ln1", "state_col1", xaS, sx)
            for ct in range(CT):
                ins = v.scalar_tensor_tensor(tokens(mixed[:, 0, ct, :]), tokens(sx[:, ct, :]), vec("maa_x", ct), xaS[:, ct, :, 1:S + 1],
                                             ALU.mult, ALU.add)
            ins.then_inc(sig["xxx"].sem, 1)
            yield
            for n, (name, _) in enumerate(MIXES):
                v.wait_ge(K.full_sem("mix", name), K.full_at(g, "mix", name))
                t = K.tile("mix", name)
                if n >= 2:
                    v.wait_ge(K.full_sem("proj", MIXES[n - 2][0]), K.full_at(g, "proj", MIXES[n - 2][0]))
                for ct in range(CT):
                    ins = v.scalar_tensor_tensor(mixed[:, (n + 1) % 2, ct, :], t[:, ct * T:(ct + 1) * T], vec(name, ct), sx[:, ct, :],
                                                 ALU.add, ALU.mult)
                ins.then_inc(K.free_sem("mix", name), 1)
                v.drain().then_inc(sig["half_mix"].sem, 1)
                yield
            v.wait_ge(K.full_sem("proj", "maa_g"), K.full_at(g, "proj", "maa_g"))
            t = K.tile("proj", "maa_g")
            v.wait_ge(sig["th_g"].sem, sig["th_g"].at(g, 1))
            ins = v.scalar_tensor_tensor(gate2[:, :, :].rearrange("p h t -> p (h t)"), gate2[:, :, :].rearrange("p h t -> p (h t)"), 1.0,
                                         t[:, :], ALU.add, ALU.mult)
            ins.then_inc(K.free_sem("proj", "maa_g"), 1)
            v.drain().then_inc(sig["gate2"].sem, 1)
            yield
            yield
            yield from v_recurrence(v, K, g)

        def v_shift(v, g, tag, col, x, out):
            v.wait_ge(sig[f"normT_{tag}"].sem, sig[f"normT_{tag}"].at(g, 1))
            v.wait_ge(sig[col].sem, sig[col].at(g, 1))
            v.tensor_tensor(out[:, :, :].rearrange("p h (b t) -> p (h b) t", b=G),
                            x[:, :, :, 0:S].rearrange("p h b t -> p (h b) t"),
                            x[:, :, :, 1:S + 1].rearrange("p h b t -> p (h b) t"), ALU.subtract)
            v.drain()

        def v_recurrence(v, K, g):
            flat, half = "p s v t -> p (s v t)", "p v t -> p (v t)"
            r = z[:, 0, :].rearrange("p (s t) -> p s t", s=SH)
            yield
            for i in range(2):
                v.wait_ge(sig["state_in"].sem, sig["state_in"].at(g, 2 * i + 2))
                v.wait_ge(sig["decay_in"].sem, sig["decay_in"].at(g, 2 * i + 2))
                v.tensor_tensor_scan(state.rearrange(flat), decay.rearrange(flat), state.rearrange(flat), 0.0, ALU.mult, ALU.add).then_inc(sig["scanned"].sem, 1)
                v.drain()
                yield
                v.tensor_tensor(state, state, r[:, i * HS:(i + 1) * HS].unsqueeze(2).to_broadcast([P, HS, SH, S]), ALU.mult)
                v.drain()
                v.tensor_tensor(state[:, 0:2].rearrange(flat), state[:, 0:2].rearrange(flat), state[:, 2:4].rearrange(flat), ALU.add)
                v.drain()
                if i == 0:
                    v.tensor_tensor(y, state[:, 0].rearrange(half), state[:, 1].rearrange(half), ALU.add).then_inc(sig["y_part"].sem, 1)
                    yield
                    yield
            v.tensor_tensor(state[:, 0].rearrange(half), state[:, 0].rearrange(half), state[:, 1].rearrange(half), ALU.add)
            v.drain()
            v.tensor_tensor(y, y, state[:, 0].rearrange(half), ALU.add)
            v.drain()
            v.wait_ge(sig["bonus"].sem, sig["bonus"].at(g, 1))
            v.tensor_tensor(y, y, bonus, ALU.add)
            v.drain()
            yield
            y3, ysq3 = (q.rearrange("p (v t) -> p v t", v=SH) for q in (y, ysq))
            v.tensor_reduce(ysum[:, :], y3.rearrange("p v t -> p t v"), AX_X, ALU.add)
            v.drain()
            v.scalar_tensor_tensor(y3, ysum[:, :].unsqueeze(1).to_broadcast([P, SH, S]), -1.0 / SH, y3, ALU.mult, ALU.add)
            v.drain()
            v.tensor_tensor(ysq, y, y, ALU.mult)
            v.drain()
            v.tensor_reduce(ysum[:, :], ysq3.rearrange("p v t -> p t v"), AX_X, ALU.add)
            v.drain()
            v.tensor_scalar(K.nw[:, 0, :], ysum[:, :], 1.0 / SH, 1e-5, ALU.mult, ALU.add).then_inc(sig["variance_y"].sem, 1)
            yield
            v.wait_ge(sig["rstd_y"].sem, sig["rstd_y"].at(g, 1))
            v.tensor_tensor(y3, y3, K.nw[:, 1, :].unsqueeze(1).to_broadcast([P, SH, S]), ALU.mult).then_inc(sig["y_normed"].sem, 1)
            yield
        def v_back(v, g):
            K = BB
            yield
            v.wait_ge(sig["yT_loaded"].sem, sig["yT_loaded"].at(g, CT * G))
            for ct in range(CT):
                v.tensor_scalar(yT[:, ct, :], yT[:, ct, :], vec("gn_w", ct), vec("gn_b", ct), ALU.mult, ALU.add)
            v.drain()
            f = "p h t -> p (h t)"
            v.scalar_tensor_tensor(yT[:, :, :].rearrange(f), yT[:, :, :].rearrange(f), 0.5, g_in[:, :, :].rearrange(f),
                                                    ALU.mult, ALU.mult).then_inc(sig["gated"].sem, 1)
            yield
            v_add_rows(v, K, g, ("rows", "wo"), bx, bx)
            v.drain().then_inc(sig["bx"].sem, 1)
            v_variance(v, K, g, "ln2", bx)
            yield
            v_norm(v, K, g, "ln2", bx)
            yield
            v_shift(v, g, "ln2", "state_col2", xcS, sxc)
            for out, name, done in ((xk2, "fmaa_k", "xk2"), (xr2, "fmaa_r", "xr2")):
                for ct in range(CT):
                    ins = v.scalar_tensor_tensor(tokens(out[:, ct, :]), tokens(sxc[:, ct, :]), vec(name, ct), xcS[:, ct, :, 1:S + 1],
                                                 ALU.mult, ALU.add)
                ins.then_inc(sig[done].sem, 1)
            yield
            v.wait_ge(K.full_sem("fv"), K.full_at(g, "fv"))
            t = K.tile("fv")
            v.wait_ge(sig["rr"].sem, sig["rr"].at(g, 1))
            f = "p t c -> p (t c)"
            ins = v.scalar_tensor_tensor(rr.rearrange(f), rr.rearrange(f), 1.0, t[:, :], ALU.add, ALU.mult)
            ins.then_inc(K.free_sem("fv"), 1)
            v.drain()
            v.scalar_tensor_tensor(bx[:, :, :].rearrange(f), rr.rearrange(f), 0.5, bx[:, :, :].rearrange(f), ALU.mult, ALU.add)
            v.drain().then_inc(sig["bx"].sem, 1)
            v_variance(v, K, g, "a", bx)
            yield
            for n, (tag, after, bq, bk) in enumerate((("a", "b", "l2_bq", "l2_bk"), ("b", "m", "l2_bq2", "l2_bk2"))):
                v_norm(v, K, g, tag, bx)
                yield
                v_queries(v, K, g, tag, bq, par4)
                v_keys(v, K, g, tag, bk)
                v_values(v, K, g, tag, n * P)
                yield
                yield from v_attention(v, K, g, tag)
                v.wait_ge(sig["bx_bias"].sem, sig["bx_bias"].at(g, n + 1))
                v_add_rows(v, K, g, ("rows", tag), bx, bx)
                v.drain().then_inc(sig["bx"].sem, 1)
                v_variance(v, K, g, after, bx)
                yield
            v_norm(v, K, g, "m", bx)
            yield
            yield
            v.wait_ge(sig["bx_bias"].sem, sig["bx_bias"].at(g, 3))
            v_add_rows(v, K, g, ("rows", "l2m"), bx, bx)
            v.drain().then_inc(sig["bx"].sem, 1)
            v_variance(v, K, g, "c", ctx_b)
            yield
            v_norm(v, K, g, "c", ctx_b)
            yield
            v_queries(v, K, g, "c", None, par4)
            v_keys(v, K, g, "c", None)
            v_values(v, K, g, "c", None)
            yield
            yield from v_attention(v, K, g, "c")
            v.wait_ge(K.full_sem("rows", "c"), K.full_at(g, "rows", "c"))
            t = K.tile("rows", "c")
            ins = v.scalar_tensor_tensor(o_out.rearrange(f), t[:, :], tgate[:, 1:2], bx[:, :, :].rearrange(f), ALU.mult, ALU.add)
            ins.then_inc(K.free_sem("rows", "c"), 1)
            v.drain().then_inc(sig["o_out"].sem, 1)
            yield

        @block.vector
        def _(v):
            v.wait_ge(loaded.sem, 16 * NLOADS)
            v.tensor_scalar(par16[:, :], parity[:, :], 1.0 / 16, None, ALU.mult)
            v.tensor_scalar(par4[:, :], parity[:, :], 1.0 / 4, None, ALU.mult)
            v.tensor_scalar(self_c[:, :], self_m[:, :], 10000.0, -10000.0, ALU.mult, ALU.add)
            v.drain()
            for i, (name, par) in enumerate((("l0_bq", par16), ("l2_bq", par4), ("l2_bq2", par4))):
                v.tensor_scalar(qb[:, i, :], par[:, :], vec(name), None, ALU.mult)
            v.drain().then_inc(ready.sem, 1)
            v.wait_ge(ready.sem, NREADY)
            all_groups(v, v_front, v_back)

        def a_normT(s, K, g, tag, out, scale, shift):
            s.wait_ge(K.full_sem("normT", tag), K.full_at(g, "normT", tag))
            t = K.tile("normT", tag)
            for ct in range(CT):
                o, src = out(ct), t[:, ct * T:(ct + 1) * T]
                if len(o.shape) == 3:
                    src = tokens(src)
                ins = s.activation(o, src, ACT.Identity, scale=vec(scale, ct), bias=vec(shift, ct) if shift else 0.0)
            ins.then_inc(K.free_sem("normT", tag), 1)
            s.drain().then_inc(sig[f"normT_{tag}"].sem, 1)

        def a_queries(s, K, g, tag, bias, scale):
            s.wait_ge(K.full_sem("q", tag, 0), K.full_at(g, "q", tag, 0))
            t = K.tile("q", tag, 0)
            for r in range(2):
                ins = s.activation(K.qeo[:, 0, :, r, :], tokens(t[:, 0:T]), ACT.Identity, scale=scale[:, r:r + 1],
                                   bias=qb[:, bias, r:r + 1] if bias is not None else 0.0)
            ins.then_inc(K.free_sem("q", tag, 0), 1)
            s.drain().then_inc(sig[f"q_{tag}"].sem, 1)

        def a_keys(s, K, g, tag, bias):
            s.wait_ge(K.full_sem("k", tag), K.full_at(g, "k", tag))
            t = K.tile("k", tag)
            for j in (0, 1):
                q = slice(32 * j, 32 * j + 32)
                if bias is None:
                    ins = s.copy(K.kb[q, :, j, 0:T], t[q, :].rearrange("p (m t) -> p m t", m=CT))
                    continue
                for m in range(CT):
                    at = VEC_AT[bias] + m
                    ins = s.activation(K.kb[q, m, j, 0:T], t[q, m * T:(m + 1) * T], ACT.Identity, bias=vecs[q, at:at + 1])
            ins.then_inc(K.free_sem("k", tag), 1)
            s.drain().then_inc(sig[f"k_{tag}"].sem, 1)

        def a_attention(s, K, g, tag):
            units, lag = 2 * G if tag == "l0" else G, LAG[tag]
            if tag == "l0" and not is_first(g):
                s.wait_ge(sig["y_stored"].sem, sig["y_stored"].at(g - 1, 1))
            for step in range(units + 2 + lag):
                if 0 <= step - MASK_STEP[tag] < units:
                    u = step - MASK_STEP[tag]
                    s.wait_ge(sig[f"shifted_{tag}"].sem, sig[f"shifted_{tag}"].at(g, u + 1))
                    s.activation(K.probs[:, u % 2, :], K.probs[:, u % 2, :], ACT.Exp).then_inc(sig[f"probs_{tag}"].sem, 1)
                if 0 <= step - lag - 1 < units:
                    u = step - lag - 1
                    s.wait_ge(K.full_sem("probsT", tag, u), K.full_at(g, "probsT", tag, u))
                    t = K.tile("probsT", tag, u)
                    ins = s.copy(K.probsT[:, u % 2, :], t[:, :])
                    ins.then_inc(K.free_sem("probsT", tag, u), 1)
                    s.drain().then_inc(sig[f"probsT_{tag}"].sem, 1)
                yield
            s.wait_ge(K.full_sem("headsT", tag), K.full_at(g, "headsT", tag))
            t = K.tile("headsT", tag)
            ins = s.copy(K.headsT.rearrange("p r b q -> p b r q"), t[:, :].rearrange("p (b r q) -> p b r q", b=G, r=2))
            ins.then_inc(K.free_sem("headsT", tag), 1)
            s.drain().then_inc(sig[f"headsT_{tag}"].sem, 1)
            yield

        def a_mlp(s, K, g, tag, bias):
            for m in range(FT // 2):
                s.wait_ge(K.full_sem("hidden", tag, m), K.full_at(g, "hidden", tag, m))
                t = K.tile("hidden", tag, m)
                for i in range(2):
                    ins = s.activation(K.hidden[:, 2 * m + i, :], t[:, i * T:(i + 1) * T], ACT.Gelu_apprx_tanh, bias=vec(bias, 2 * m + i))
                    if i == 0:
                        ins.then_inc(sig[f"hidden_{tag}"].sem, 1)
                ins.then_inc(K.free_sem("hidden", tag, m), 1)
                s.drain().then_inc(sig[f"hidden_{tag}"].sem, 1)

        def a_front(s, g):
            K = FB
            s.wait_ge(K.full_sem("inT", 0), K.full_at(g, "inT", 0))
            t = K.tile("inT", 0)
            ins = s.copy(inT[:, 0, :, :].rearrange("p b (u t) -> p u b t", u=2), t[:, :].rearrange("p (u b t) -> p u b t", u=2, b=G))
            ins.then_inc(K.free_sem("inT", 0), 1)
            s.drain().then_inc(sig["inT"].sem, 1)
            yield
            a_queries(s, K, g, "l0", 0, par16)
            for m in range(CT):
                s.wait_ge(K.full_sem("k", "l0", m), K.full_at(g, "k", "l0", m))
                t = K.tile("k", "l0", m)
                s.wait_ge(sig["keys_cleared"].sem, sig["keys_cleared"].at(g, 1))
                for j in (0, 1):
                    q = slice(32 * j, 32 * j + 32)
                    at = VEC_AT["l0_bk"] + m
                    ins = s.activation(K.kb[q, m, j, :], t[q, :], ACT.Identity, bias=vecs[q, at:at + 1])
                ins.then_inc(K.free_sem("k", "l0", m), 1)
                s.drain().then_inc(sig["k_l0"].sem, 1)
            yield
            yield from a_attention(s, K, g, "l0")
            s.wait_ge(sig["attn_l0"].sem, sig["attn_l0"].at(g, 1))
            for tt in range(TT):
                s.activation(K.xn[:, tt, :], x1[:, tt, :], ACT.Square, accum_out=sumsq[:, tt:tt + 1])
            s.drain().then_inc(sig["variance_l0"].sem, 1)
            yield
            a_normT(s, K, g, "l0", lambda ct: K.xnT[:, ct, :], "l0_post", None)
            yield
            a_mlp(s, K, g, "l0m", "l0_b1")
            yield
            yield
            a_normT(s, K, g, "ln1", lambda ct: xaS[:, ct, :, 1:S + 1], "ln1_w", "ln1_b")
            yield
            s.wait_ge(K.full_sem("lora"), K.full_at(g, "lora"))
            t = K.tile("lora")
            s.activation(lora_t[:, 0, :], t[:, 0:T], ACT.Tanh)
            ins = s.activation(lora_t[0:32, 1, :], t[0:32, T:2 * T], ACT.Tanh)
            ins.then_inc(K.free_sem("lora"), 1)
            s.drain().then_inc(sig["lora"].sem, 1)
            yield
            yield
            for name, _ in MIXES[:-1]:
                s.wait_ge(K.full_sem("proj", name), K.full_at(g, "proj", name))
                t = K.tile("proj", name)
                if name == "maa_g":
                    ins = s.activation(gate2[:, :, :].rearrange("p h t -> p (h t)"), t[:, :], ACT.Tanh, scale=0.5)
                    done = "th_g"
                else:
                    ins = s.copy(rkvw[:, KINDS[name[-1]], :, :].rearrange("p h t -> p (h t)"), t[:, :])
                    done = "rkvw"
                ins.then_inc(K.free_sem("proj", name), 1)
                s.drain().then_inc(sig[done].sem, 1)
                yield
            s.wait_ge(K.full_sem("decay1"), K.full_at(g, "decay1"))
            t = K.tile("decay1")
            ins = s.activation(dec_t[0:64, :], t[0:64, 0:T], ACT.Tanh)
            ins.then_inc(K.free_sem("decay1"), 1)
            s.drain().then_inc(sig["dec_t"].sem, 1)
            yield
            s.wait_ge(K.full_sem("decay2"), K.full_at(g, "decay2"))
            t = K.tile("decay2")
            for ct in range(CT):
                ins = s.activation(rkvw[:, KINDS["w"], ct, :], t[:, ct * T:(ct + 1) * T], ACT.Exp, bias=vec("decay", ct))
            ins.then_inc(K.free_sem("decay2"), 1)
            s.drain()
            w = rkvw[:, KINDS["w"], :, :].rearrange("p h t -> p (h t)")
            s.activation(w, w, ACT.Exp, scale=-1.0).then_inc(sig["rkvw"].sem, 1)
            yield
            s.wait_ge(sig["z_loaded"].sem, sig["z_loaded"].at(g, 2))
            for i in range(2):
                if i == 1:
                    s.wait_ge(sig["scanned"].sem, sig["scanned"].at(g, 1))
                w = z[:, 3, :].rearrange("p (s t) -> p s t", s=SH)[:, i * HS:(i + 1) * HS, 0:S - 1]
                s.copy(decay[:, :, :, 1:S], w.unsqueeze(2).to_broadcast([P, HS, SH, S - 1])).then_inc(sig["decay_in"].sem, 1)
                yield
                if i == 0:
                    yield
                    yield
            yield from idle(4)

        def a_back(s, g):
            K = BB
            s.wait_ge(K.full_sem("ctxT"), K.full_at(g, "ctxT"))
            t = K.tile("ctxT")
            ins = s.copy(ctxT[:, :, :, :].rearrange("p h b t -> p (h b t)"), t[:, :])
            ins.then_inc(K.free_sem("ctxT"), 1)
            s.drain().then_inc(sig["ctxT"].sem, 1)
            yield
            yield
            yield
            a_normT(s, K, g, "ln2", lambda ct: xcS[:, ct, :, 1:S + 1], "ln2_w", "ln2_b")
            yield
            s.wait_ge(K.full_sem("fk"), K.full_at(g, "fk"))
            t = K.tile("fk")
            f = "p h t -> p (h t)"
            ins = s.activation(kk[:, :, :].rearrange(f), t[:, :], ACT.Relu)
            ins.then_inc(K.free_sem("fk"), 1)
            s.drain()
            s.activation(kk[:, :, :].rearrange(f), kk[:, :, :].rearrange(f), ACT.Square).then_inc(sig["kk"].sem, 1)
            s.wait_ge(K.full_sem("fr"), K.full_at(g, "fr"))
            t = K.tile("fr")
            ins = s.activation(rr.rearrange("p t c -> p (t c)"), t[:, :], ACT.Tanh, scale=0.5)
            ins.then_inc(K.free_sem("fr"), 1)
            s.drain().then_inc(sig["rr"].sem, 1)
            yield
            yield
            for n, (tag, ln, bk) in enumerate((("a", "l2_ln1", "l2_bk"), ("b", "l2_ln2", "l2_bk2"))):
                a_normT(s, K, g, tag, lambda ct: K.xnT[:, ct, :], ln + "_s", ln + "_b")
                yield
                a_queries(s, K, g, tag, n + 1, par4)
                a_keys(s, K, g, tag, bk)
                yield
                yield from a_attention(s, K, g, tag)
                yield
            a_normT(s, K, g, "m", lambda ct: K.xnT[:, ct, :], "l2_ln3_s", "l2_ln3_b")
            yield
            a_mlp(s, K, g, "l2m", "l2_b1")
            yield
            yield
            a_normT(s, K, g, "c", lambda ct: K.xnT[:, ct, :], "l3_ln_s", "l3_ln_b")
            s.wait_ge(K.full_sem("xT"), K.full_at(g, "xT"))
            t = K.tile("xT")
            ins = s.copy(yT[:, :, :].rearrange(f), t[:, :])
            ins.then_inc(K.free_sem("xT"), 1)
            s.drain().then_inc(sig["xT"].sem, 1)
            yield
            a_queries(s, K, g, "c", None, par4)
            a_keys(s, K, g, "c", None)
            yield
            yield from a_attention(s, K, g, "c")
            yield

        @block.scalar
        def _(s):
            s.wait_ge(loaded.sem, 16 * NLOADS)
            s.activation(tgate[:, 1:2], tgate[:, 0:1], ACT.Tanh).then_inc(ready.sem, 1)
            s.wait_ge(ready.sem, NREADY)
            all_groups(s, a_front, a_back)

        def p_rstd(p, K, g, tag, n=TT):
            p.wait_ge(sig[f"variance_{tag}"].sem, sig[f"variance_{tag}"].at(g, 1))
            after_wait(p, "pool")
            x, r, t = K.nw[:, 0, 0:n], K.nw[:, 1, 0:n], K.nw[:, 2, 0:n]
            if tag == "l0":
                p.tensor_scalar(x, sumsq[:, :], 1.0 / C, 1e-6, ALU.mult, ALU.add)
                p.drain()
            p.tensor_scalar(r.bitcast(I32), x.bitcast(I32), -0.5, RSQRT_SEED, ALU.mult, ALU.add)
            p.drain()
            for _ in range(3):
                p.tensor_tensor(t, r, r, ALU.mult)
                p.drain()
                p.tensor_tensor(t, t, x, ALU.mult)
                p.drain()
                p.tensor_scalar(t, t, -0.5, 1.5, ALU.mult, ALU.add)
                p.drain()
                ins = p.tensor_tensor(r, t, r, ALU.mult)
                p.drain()
            p.sem_inc(sig[f"rstd_{tag}"].sem, 1)

        def p_back(p, g):
            K = BB
            p.wait_ge(sig["back_loaded"].sem, sig["back_loaded"].at(g, 6))
            after_wait(p, "pool")
            p.tensor_scalar(mask3[0:1, :], mask3_raw[0:1, :], 0, MASKED, ALU.is_equal, ALU.mult).then_inc(sig["mask3"].sem, 1)
            p.tensor_scalar(cross_c[:, :, :], cross_m[:, :, :], 10000.0, -10000.0, ALU.mult, ALU.add)
            p.drain()
            p.wait_ge(sig["ctxT"].sem, sig["ctxT"].at(g, 1))
            after_wait(p, "pool")
            p.tensor_copy(xcS[:, :, :, 0], ctxT[:, :, :, 0]).then_inc(sig["state_col2"].sem, 1)
            yield
            yield
            p_rstd(p, K, g, "ln2")
            yield
            yield
            yield
            p_rstd(p, K, g, "a")
            yield
            for n, (tag, bias) in enumerate((("a", "l2_bo"), ("b", "l2_bo2"), ("m", "l2_b2"))):
                p.wait_ge(sig[f"normed_{tag}"].sem, sig[f"normed_{tag}"].at(g, 1))
                p.tensor_tensor(bx[:, :, :], bx[:, :, :], row(bias).unsqueeze(1).to_broadcast([P, TT, C]), ALU.add).then_inc(sig["bx_bias"].sem, 1)
                yield
                if tag == "m":
                    continue
                yield
                for u in range(G):
                    p.wait_ge(sig[f"masked_{tag}"].sem, sig[f"masked_{tag}"].at(g, u + 1))
                    c = self_c[:, :] if tag == "a" else cross_c[:, u, :]
                    q = K.probs[:, u % 2, :].rearrange("p (j k) -> p j k", j=PAIRS)
                    p.tensor_tensor(q, q, c.unsqueeze(1).to_broadcast([P, PAIRS, S]), ALU.add).then_inc(sig[f"added_{tag}"].sem, 1)
                    yield
                yield from idle(4)
                p_rstd(p, K, g, "b" if tag == "a" else "m")
                yield
            yield
            p_rstd(p, K, g, "c")
            yield from idle(12)

        def p_front(p, g):
            K = FB
            p.dma_start(x_in[:, :, :], x_d[g].rearrange("(t p) c -> p t c", p=P)).then_inc(sig["x_loaded"].sem, 16)
            p.dma_start(ctx_in[:, :, :], ctx_d[g].rearrange("(t p) c -> p t c", p=P)).then_inc(sig["x_loaded"].sem, 16)
            p.dma_start(mask0_raw[0:1, :], a["mask0"][g]).then_inc(sig["x_loaded"].sem, 16)
            p.memset(K.kb, 0.0).then_inc(sig["keys_cleared"].sem, 1)
            p.wait_ge(sig["x_loaded"].sem, sig["x_loaded"].at(g, 3))
            after_wait(p, "pool")
            p.tensor_scalar(mask0[0:1, :, 0:S], mask0_raw[0:1, :].rearrange("p (b k) -> p b k", b=G), 0, MASKED, ALU.is_equal, ALU.mult).then_inc(sig["mask0"].sem, 1)
            p.tensor_tensor(x1[:, :, :], x_in[:, :, :], row("l0_bo").unsqueeze(1).to_broadcast([P, TT, C]), ALU.add).then_inc(sig["x_bias"].sem, 1)
            yield
            p.drain()
            p.wait_ge(sig["inT"].sem, sig["inT"].at(g, 2))
            p.tensor_tensor(x_in[:, :, :], x_in[:, :, :], row("l0_b2").unsqueeze(1).to_broadcast([P, TT, C]), ALU.add).then_inc(sig["x_bias"].sem, 1)
            p.tensor_copy(xaS[:, :, :, 0], inT[:, :, :, 1]).then_inc(sig["state_col1"].sem, 1)
            yield
            yield from idle(12)
            p_rstd(p, K, g, "l0")
            yield from idle(3)
            p_rstd(p, K, g, "ln1")
            yield from idle(3)
            for n in range(len(MIXES)):
                p.wait_ge(sig["half_mix"].sem, sig["half_mix"].at(g, n + 1))
                m = mixed[:, (n + 1) % 2, :, :].rearrange("p h (b t) -> p (h b) t", b=G)
                p.tensor_tensor(m, m, xaS[:, :, :, 1:S + 1].rearrange("p h b t -> p (h b) t"), ALU.add).then_inc(sig["mix"].sem, 1)
                yield
            yield from idle(2)
            p.wait_ge(sig["z_loaded"].sem, sig["z_loaded"].at(g, 2))
            r, k, vv = (z[:, i, :].rearrange("p (s t) -> p s t", s=SH) for i in range(3))
            for i in range(2):
                if i == 1:
                    p.wait_ge(sig["y_part"].sem, sig["y_part"].at(g, 1))
                h = slice(i * HS, (i + 1) * HS)
                p.tensor_tensor(state[:, :, :, 1:S], k[:, h, 0:S - 1].unsqueeze(2).to_broadcast([P, HS, SH, S - 1]),
                                vv[:, :, 0:S - 1].unsqueeze(1).to_broadcast([P, HS, SH, S - 1]), ALU.mult).then_inc(sig["state_in"].sem, 1)
                p.tensor_copy(state[:, :, :, 0], s0[:, :].rearrange("p (s v) -> p s v", s=SH)[:, h]).then_inc(sig["state_in"].sem, 1)
                p.memset(decay[:, :, :, 0:1], 0.0).then_inc(sig["decay_in"].sem, 1)
                yield
                if i == 1:
                    continue
                p.tensor_tensor(bonus, z[:, 0, :], z[:, 1, :], ALU.mult)
                p.drain()
                b3 = bonus.rearrange("p (s t) -> p s t", s=SH)
                p.tensor_tensor(b3, b3, bonus_u[:, :].unsqueeze(2).to_broadcast([P, SH, S]), ALU.mult)
                p.drain()
                for n in (4, 2):
                    p.tensor_tensor(bonus[:, 0:n * S], bonus[:, 0:n * S], bonus[:, n * S:2 * n * S], ALU.add)
                    p.drain()
                p.tensor_tensor(bonus_sum[:, :], bonus[:, 0:S], bonus[:, S:2 * S], ALU.add)
                p.drain()
                p.tensor_tensor(b3, bonus_sum[:, :].unsqueeze(1).to_broadcast([P, SH, S]), vv, ALU.mult).then_inc(sig["bonus"].sem, 1)
                yield
                yield
            yield
            yield
            p_rstd(p, K, g, "y", S)
            yield
            yield

        @block.gpsimd
        def _(p):
            for K in (FB, BB):
                for f in K.free:
                    p.sem_inc(f, 1)
            p.sem_inc(stored.sem, 16)
            p.memset(vb[:, :, :, :, :, :], 0.0)
            p.drain()
            p.memset(BB.kb[:, :, :, :], 0.0).then_inc(ready.sem, 1)
            p.memset(va[:, :, :, D], 1.0).then_inc(ready.sem, 1)
            p.memset(ones_bf[:, :], 1.0).then_inc(ready.sem, 1)
            p.drain()
            p.memset(mask0[0:1, :, :], 0.0).then_inc(ready.sem, 1)
            for h in range(2):
                p.drain()
                ins = p.memset(vb[h * S:(h + 1) * S, :, :, :, h, D], 1.0)
            ins.then_inc(ready.sem, 1)
            p.wait_ge(loaded.sem, 16 * NLOADS)
            p.wait_ge(ready.sem, NREADY)
            all_groups(p, p_front, p_back)

    return nc


def kernel(**inputs):
    import numpy as np
    import concourse.bacc as bacc
    from concourse.bass_utils import run_bass_kernel_spmd

    inp = {k: np.asarray(v) for k, v in inputs.items()}

    def tiles(w):
        k = w.shape[0] // P
        return w.reshape(k, P, w.shape[1]).transpose(1, 0, 2).reshape(P, -1)

    def by_parity(w):
        return w.reshape(PAIRS, 2, D, -1).transpose(1, 0, 2, 3).reshape(C, -1)

    def by_half(w):
        w = w.reshape(-1, PT_, 2, 2, D).transpose(0, 2, 1, 3, 4)
        return w.reshape(-1, C)

    L0 = {k[9:]: v for k, v in inp.items() if k.startswith("L0_xattn_")}
    L1 = {k[9:]: v for k, v in inp.items() if k.startswith("L1_xattn_")}
    L2 = {k[9:]: v for k, v in inp.items() if k.startswith("L2_xattn_")}
    L3 = {k[9:]: v for k, v in inp.items() if k.startswith("L3_xattn_")}
    kv0, kvb0 = L0["kv_w"].reshape(C, C, 2), L0["kv_b"].reshape(C, 2)
    w = {
        "l0_q": L0["q_w"], "l0_k": kv0[:, :, 0], "l0_v": kv0[:, :, 1], "l0_o": by_parity(L0["out_w"]),
        "l0_w1": L0["mlp_w1"], "l0_w2": L0["mlp_w2"], "maa_w1": L1["maa_w1"], "decay_w1": L1["decay_w1"],
        "maa_w2": L1["maa_w2"][0:4].reshape(P, C), "wr": L1["Wr"].T, "wk": L1["Wk"].T, "wv": L1["Wv"].T, "wg": L1["Wg"].T,
        "wo": L1["Wo"].T, "fwk": L1["fWk"].T, "fwr": L1["fWr"].T, "fwv": L1["fWv"].T,
        "l2_q": L2["w_qkv"][:, 0:C], "l2_k": L2["w_qkv"][:, C:2 * C], "l2_v": by_half(L2["w_qkv"][:, 2 * C:]),
        "l2_o": by_parity(L2["w_ao"]), "l2_q2": L2["w_q"], "l2_k2": L2["w_kv"][:, 0:C], "l2_v2": by_half(L2["w_kv"][:, C:]),
        "l2_o2": by_parity(L2["w_co"]), "l2_w1": L2["w1"], "l2_w2": L2["w2"],
        "l3_q": L3["Wq"].T, "l3_k": L3["Wk"].T, "l3_v": by_half(L3["Wv"].T), "l3_o": by_parity(L3["Wo"].T),
    }
    v = {
        "l0_bq": L0["q_b"], "l0_bk": kvb0[:, 0], "l0_post": L0["postnorm_w"], "l0_b1": L0["mlp_b1"],
        "ln1_w": L1["ln1_w"], "ln1_b": L1["ln1_b"], "ln2_w": L1["ln2_w"], "ln2_b": L1["ln2_b"],
        "maa_x": L1["maa_x"], "maa_k": L1["maa_k"], "maa_v": L1["maa_v"], "maa_r": L1["maa_r"], "maa_g": L1["maa_g"],
        "maa_w": L1["maa_w"], "decay": L1["time_decay"], "gn_w": L1["gn_w"], "gn_b": L1["gn_b"],
        "fmaa_k": L1["fmaa_k"], "fmaa_r": L1["fmaa_r"], "l2_ln1_s": L2["ln1_s"], "l2_ln1_b": L2["ln1_b"],
        "l2_ln2_s": L2["ln2_s"], "l2_ln2_b": L2["ln2_b"], "l2_ln3_s": L2["ln3_s"], "l2_ln3_b": L2["ln3_b"],
        "l2_bq": L2["b_qkv"][0:C], "l2_bk": L2["b_qkv"][C:2 * C], "l2_bq2": L2["b_q"], "l2_bk2": L2["b_kv"][0:C],
        "l2_b1": L2["b1"], "l3_ln_s": L3["ln_gamma"], "l3_ln_b": L3["ln_beta"],
    }
    rows = {"l0_bv": kvb0[:, 1], "l0_bo": L0["out_b"], "l0_b2": L0["mlp_b2"], "l2_bo": L2["b_ao"], "l2_bo2": L2["b_co"], "l2_b2": L2["b2"]}
    ctx = inp["ctx_2048"]
    arrays = {
        "x": inp["x"], "ctx": ctx, "s0": ctx[:, 2:2 + SH, :].reshape(NG, P, SH * SH),
        "w_front": np.concatenate([tiles(w[n]) for n in FRONT_W], axis=1),
        "w_back": np.concatenate([tiles(w[n]) for n in BACK_W], axis=1),
        "maa_w2g": L1["maa_w2"][4], "decay_w2": L1["decay_w2"], "faaaa": L1["faaaa"].reshape(-1, SH),
        "vecs": np.concatenate([v[n].reshape(-1, P).T for n in VECS], axis=1),
        "rows": np.concatenate([rows[n] for n in ROWS]).reshape(1, -1),
        "bv_half": np.concatenate([by_half(L2["b_qkv"][2 * C:]).reshape(2, P), by_half(L2["b_kv"][C:]).reshape(2, P)], axis=1),
        "gate": L3["gate"].reshape(1, 1), "ident": np.eye(P, dtype=np.float32),
        "parity": np.stack([(np.arange(P) // D) % 2 == r for r in range(2)], axis=1).astype(np.float32),
        "mask0": inp["mask_BxS2_ik0"].reshape(NG, 1, T), "mask3": inp["mask_BxS2_bf1"].view(np.uint8).reshape(NG, 1, T),
        "self_mask": inp["mask_1x1xSxS2_fc1"].reshape(S, S), "cross_mask": inp["mask_Bx1xSxS2_ff1"].reshape(NG, G, S, S),
    }
    nc = bacc.Bacc("TRN2", target_bir_lowering=False, num_devices=1)
    ins, aps = {}, {}
    for name, arr in arrays.items():
        arr = np.ascontiguousarray(arr)
        ins[f"in_{name}"] = arr
        aps[name] = nc.dram_tensor(f"in_{name}", arr.shape, mybir.dt.from_np(arr.dtype), kind="ExternalInput").ap()
    aps["out"] = nc.dram_tensor("out_x", (B, S, C), F32, kind="ExternalOutput").ap()
    bass_four_layers_kernel(nc, aps)
    r = run_bass_kernel_spmd(nc, [ins], core_ids=[0])
    return r.results[0]["out_x"]
```

```python
from contextlib import ExitStack

import concourse.bass as bass
from concourse import mybir

ALU = mybir.AluOpType
ACT = mybir.ActivationFunctionType
AX_X = mybir.AxisListType.X
F32 = mybir.dt.float32
BF16 = mybir.dt.bfloat16
I32 = mybir.dt.int32

P = 128
B, S, C = 32, 64, 256
G = 4
NG = B // G
T = G * S
TT = T // P
CT = C // P
D = 16
PAIRS = C // (2 * D)
PT_ = 4
SH = 8
FF = 4 * C
FT = FF // P
MASKED = -1e30
RSQRT_SEED = float(0x5F3759DF)

VECS = ["l0_bq", "l0_bk", "l0_post", "l0_b1", "ln1_w", "ln1_b", "ln2_w", "ln2_b", "maa_x", "maa_k", "maa_v",
        "maa_r", "maa_g", "maa_w", "decay", "gn_w", "gn_b", "fmaa_k", "fmaa_r", "l2_ln1_s", "l2_ln1_b",
        "l2_ln2_s", "l2_ln2_b", "l2_ln3_s", "l2_ln3_b", "l2_bq", "l2_bk", "l2_bq2", "l2_bk2", "l2_b1",
        "l3_ln_s", "l3_ln_b"]
VEC_WIDTH = {v: (FT if v in ("l0_b1", "l2_b1") else CT) for v in VECS}
VEC_AT = {v: sum(VEC_WIDTH[u] for u in VECS[:i]) for i, v in enumerate(VECS)}
NVEC = sum(VEC_WIDTH.values())
ROWS = ["l0_bv", "l0_bo", "l0_b2", "l2_bo", "l2_bo2", "l2_b2"]
FRONT_W = {"l0_q": (2, 256), "l0_k": (2, 256), "l0_v": (2, 256), "l0_o": (2, 256), "l0_w1": (2, 1024),
           "l0_w2": (8, 256), "maa_w1": (2, 160), "decay_w1": (2, 64), "maa_w2": (1, 256),
           "wr": (2, 256), "wk": (2, 256), "wv": (2, 256), "wg": (2, 256)}
BACK_W = {"wo": (2, 256), "fwk": (2, 256), "fwr": (2, 256), "fwv": (2, 256), "l2_q": (2, 256), "l2_k": (2, 256),
          "l2_v": (2, 256), "l2_o": (2, 256), "l2_q2": (2, 256), "l2_k2": (2, 256), "l2_v2": (2, 256),
          "l2_o2": (2, 256), "l2_w1": (2, 1024), "l2_w2": (8, 256), "l3_q": (2, 256), "l3_k": (2, 256),
          "l3_v": (2, 256), "l3_o": (2, 256)}
MIXES = [("maa_k", 1), ("maa_v", 2), ("maa_r", 3), ("maa_g", 4), ("maa_w", 0)]
KINDS = {"r": 0, "k": 1, "v": 2, "w": 3}


def width(table):
    return sum(k * n for k, n in table.values())


def bass_four_layers_kernel(nc, a):
    with ExitStack() as ctx:
        def sb(name, shape, dt=F32):
            return ctx.enter_context(nc.sbuf_tensor(name, [P] + shape, dt))

        passed = {}

        def after_wait(eng, name):
            if name not in passed:
                passed[name] = ctx.enter_context(nc.semaphore(f"{name}_passed"))
            eng.sem_inc(passed[name], 1)

        def part(tile, at, k, n):
            return tile[:, at:at + k * n].rearrange("p (k n) -> p k n", k=k)

        class Signal:

            def __init__(self, name, per, step=1):
                self.sem, self.per, self.step = ctx.enter_context(nc.semaphore(name)), per, step

            def at(self, g, k):
                assert 1 <= k <= self.per
                return (g * self.per + k) * self.step

            def before(self, g):
                return (g * self.per + 1) * self.step

        class Half:

            def __init__(self, name, tiles):
                self.bank = [ctx.enter_context(nc.psum_tensor(f"{name}_bank{i}", [P, 512], F32)) for i in range(4)]
                self.full = [ctx.enter_context(nc.semaphore(f"{name}_full{i}")) for i in range(4)]
                self.free = [ctx.enter_context(nc.semaphore(f"{name}_free{i}")) for i in range(4)]
                self.at, self.fills, self.frees = {}, [0] * 4, [0] * 4
                turn = 0
                for key, where, readers in tiles:
                    if where is None:
                        where, turn = turn, (turn + 1) % 3
                    self.at[key] = (where, self.fills[where] + 1, self.frees[where] + 1, readers)
                    self.fills[where] += 1
                    self.frees[where] += readers
                self.xn = sb(f"{name}_xn", [TT, C])
                self.xnT = sb(f"{name}_xnT", [CT, T])
                self.heads = self.xn[:, :, :].rearrange("p t c -> p (t c)").rearrange("p (b k) -> p b k", b=G)
                self.headsT = self.xnT[:, :, :].rearrange("p r (b q) -> p r b q", b=G)
                self.stats = sb(f"{name}_stats", [TT, 6])
                self.mv = sb(f"{name}_mv", [TT, 2])
                self.nmax = sb(f"{name}_nmax", [4, PAIRS])
                self.rden = sb(f"{name}_rden", [2, 2 * PAIRS])

            def tile(self, *key):
                return self.bank[self.at[key][0]]

            def full_sem(self, *key):
                return self.full[self.at[key][0]]

            def full_at(self, g, *key):
                i, full, _, _ = self.at[key]
                return g * self.fills[i] + full

            def free_sem(self, *key):
                return self.free[self.at[key][0]]

            def free_at(self, g, *key):
                i, _, free, _ = self.at[key]
                return g * self.frees[i] + free

            def taken_at(self, g, *key, readers=None):
                i, _, free, n = self.at[key]
                return g * self.frees[i] + free + (n if readers is None else readers)

            def latest(self, keys):
                return list({self.at[key][0]: key for key in keys}.values())

        LAG = {"l0": 1, "a": 1, "b": 1, "c": 1}
        MASK_STEP = {"l0": 0, "a": 1, "b": 1, "c": 0}
        O_BANK = 3

        def attention_tiles(tag, units, per_out):
            out, lag = [], LAG[tag]
            for step in range(units + 2 + lag):
                if 0 <= step - 1 - lag < units:
                    out.append((("probsT", tag, step - 1 - lag), None, 1))
                if step < units:
                    out.append((("scores", tag, step), None, 1))
                if step >= 2 + lag and (step - 2 - lag) % per_out == 0:
                    out.append((("heads", tag, (step - 2 - lag) // per_out), O_BANK, 1))
            return out + [(("headsT", tag), None, 1), (("rows", tag), None, 1)]

        def mlp_tiles(tag):
            return [(("hidden", tag, m), None, 1) for m in range(FT // 2)] + [(("rows", tag), None, 1)]

        mix_tiles = []
        for n in range(len(MIXES) + 1):
            if n < len(MIXES):
                mix_tiles.append((("mix", MIXES[n][0]), None, 1))
            if n >= 1:
                name = MIXES[n - 1][0]
                if name == "maa_w":
                    mix_tiles += [(("decay1",), None, 1), (("decay2",), None, 1)]
                else:
                    mix_tiles.append((("proj", name), None, 2 if name == "maa_g" else 1))
        front_tiles = (
            [(("inT", ct), None, 1) for ct in range(CT)] + [(("q", "l0", 0), None, 1), (("q", "l0", 1), None, 1)]
            + [(("k", "l0", m), None, 2) for m in range(CT)] + [(("v", "l0", j), None, 1) for j in range(2)]
            + attention_tiles("l0", 2 * G, 4) + [(("normT", "l0"), None, 1)] + mlp_tiles("l0m")
            + [(("normT", "ln1"), None, 1), (("lora",), None, 1)] + mix_tiles
        )
        back_tiles = (
            [(("ctxT",), None, 1), (("rows", "wo"), None, 1), (("normT", "ln2"), None, 1), (("fk",), None, 1), (("fr",), None, 1), (("fv",), None, 1)]
            + [(("normT", "a"), None, 1), (("q", "a", 0), None, 1), (("q", "a", 1), None, 1), (("k", "a"), None, 2), (("v", "a"), None, 1)]
            + attention_tiles("a", G, 2)
            + [(("normT", "b"), None, 1), (("q", "b", 0), None, 1), (("q", "b", 1), None, 1), (("k", "b"), None, 2), (("v", "b"), None, 1)]
            + attention_tiles("b", G, 2)
            + [(("normT", "m"), None, 1)] + mlp_tiles("l2m")
            + [(("normT", "c"), None, 1), (("xT",), None, 1), (("q", "c", 0), None, 1), (("q", "c", 1), None, 1), (("k", "c"), None, 2), (("v", "c"), None, 1)]
            + attention_tiles("c", G, 2)
        )
        FB = Half("front", front_tiles)
        BB = Half("back", back_tiles)

        w_front = sb("w_front", [width(FRONT_W)])
        w_back = sb("w_back", [width(BACK_W)])

        def weights(tile, table):
            out, at = {}, 0
            for name, (k, n) in table.items():
                out[name] = tile[:, at:at + k * n].rearrange("p (k n) -> p k n", k=k)
                at += k * n
            return out

        W = {**weights(w_front, FRONT_W), **weights(w_back, BACK_W)}
        maa_w2g = sb("maa_w2g", [C])
        decay_w2 = sb("decay_w2", [C])
        vecs = sb("vecs", [NVEC])
        rows = sb("rows", [len(ROWS) * C])
        bv = sb("bv", [2 * C])
        ident = sb("ident", [P])
        parity = sb("parity", [2])
        par16 = sb("par16", [2])
        par4 = sb("par4", [2])
        qb = sb("qb", [3, 2])
        bonus_u = sb("bonus_u", [SH])
        tgate = sb("tgate", [2])
        ones_bf = sb("ones_bf", [P], BF16)
        mask3_raw = sb("mask3_raw", [T], mybir.dt.uint8)
        mask0 = sb("mask0", [G, P], BF16)
        mask3 = sb("mask3", [T], BF16)
        self_m = sb("self_m", [S])
        self_c = sb("self_c", [S])
        cross_m = sb("cross_m", [G, S])
        cross_c = sb("cross_c", [G, S])

        mask0_raw = FB.xnT[:, 0, :].bitcast(I32)
        x_in = sb("x_in", [TT, C])
        ctx_in = FB.xn
        in_region = sb("in_region", [CT * G * P])
        inT = in_region[:, :].rearrange("p (h b t) -> p h b t", h=CT, b=G)
        x1 = sb("x1", [TT, C])
        xaS = sb("xaS", [CT, G, S + 1])
        gate2 = sb("gate2", [CT, T])
        sx = part(in_region, 0, CT, T)
        lora_t = part(in_region, CT * T, 2, T)
        wide_region = sb("wide_region", [FT * T])
        FB.hidden = part(wide_region, 0, FT, T)
        rkvw = wide_region[:, :].rearrange("p (k h t) -> p k h t", k=4, h=CT)
        attn_region = sb("attn_region", [2 * CT * T + 2 * 512])
        FB.qeo = attn_region[:, 0:2 * CT * T].rearrange("p (m b r q) -> p m b r q", m=CT, b=G, r=2)
        FB.probs = part(attn_region, 2 * CT * T, 2, 512)
        dec_t = attn_region[:, 0:T]
        mixed = attn_region[:, 2 * CT * T:].rearrange("p (i h t) -> p i h t", i=2, h=CT)
        y_region = sb("y_region", [2 * 512])
        FB.probsT = part(y_region, 0, 2, 512)
        bonus, y = y_region[:, 0:SH * S], y_region[:, SH * S:]
        ysq = FB.xn[:, :, :].rearrange("p t c -> p (t c)")
        ysum = sb("ysum", [S])
        bonus_sum = sb("bonus_sum", [S])
        s0 = sb("s0", [SH * SH])
        z = attn_region[:, :].rearrange("p (k x) -> p k x", k=4)
        key_region = sb("key_region", [CT * PT_ * 2 * T])
        FB.kb = key_region[:, :].rearrange("p (m j t) -> p m j t", m=CT, j=PT_)
        HS = SH // 2
        state, decay = (key_region[:, i * HS * SH * S:(i + 1) * HS * SH * S].rearrange("p (s v t) -> p s v t", s=HS, v=SH)
                        for i in range(2))
        va = sb("va", [G, 2 * PAIRS, D + 1])
        sumsq = sb("sumsq", [TT])
        FB.nw = sb("front_nw", [3, S])

        ctx_b = sb("ctx_b", [TT, C])
        ctxT = sb("ctxT", [CT, G, S])
        bx = sb("bx", [TT, C])
        g_in = sb("g_in", [CT, T])
        xcS = sb("xcS", [CT, G, S + 1])
        vb = sb("vb", [G, PT_, 2, 2, D + 1])
        rr = sb("rr", [TT, C])
        yT = sb("yT", [CT, T])
        o_out = part(yT[:, :, :].rearrange("p h t -> p (h t)"), 0, TT, C)
        BB.nw = sb("back_nw", [3, TT])
        mix_region = sb("mix_region", [4 * CT * T])
        sxc, xk2, xr2, kk = (part(mix_region, i * CT * T, CT, T) for i in range(4))
        BB.qeo = mix_region[:, 0:2 * CT * T].rearrange("p (m b r q) -> p m b r q", m=CT, b=G, r=2)
        BB.probs = part(mix_region, 2 * CT * T, 2, 512)
        BB.probsT = sb("back_probsT", [2, 512])
        BB.hidden = sb("back_hidden", [FT, T])
        BB.kb = sb("back_kb", [CT, PT_, T])

        def vec(name, i=0):
            at = VEC_AT[name] + i
            return vecs[:, at:at + 1]

        def row(name):
            at = ROWS.index(name) * C
            return rows[:, at:at + C]

        d_rkvw = nc.dram_tensor("d_rkvw", [NG, 4, P, SH * S], F32, kind="Internal").ap()
        d_gate = nc.dram_tensor("d_gate", [NG, CT, P, T], F32, kind="Internal").ap()
        d_x1 = nc.dram_tensor("d_x1", [NG, T, C], F32, kind="Internal").ap()
        d_y = nc.dram_tensor("d_y", [NG, P, SH * S], F32, kind="Internal").ap()
        x_d = a["x"].rearrange("(g b) s c -> g (b s) c", g=NG)
        ctx_d = a["ctx"].rearrange("(g b) s c -> g (b s) c", g=NG)
        out_d = a["out"].rearrange("(g b) s c -> g (b s) c", g=NG)

        loaded = Signal("front_loaded", 1, 16)
        mlp_loaded = Signal("mlp_loaded", 1, 16)
        back_consts = Signal("back_consts_loaded", 1, 16)
        NLOADS, NBACK_LOADS = 11, 6
        ready = Signal("constants_ready", 1)
        NREADY = 6
        back_ready = Signal("back_constants_ready", 1)
        NBACK_READY = 2
        stored = Signal("stored", 1, 16)
        sig = {}

        def new(name, per, step=1):
            sig[name] = Signal(name, per, step)

        new("x_loaded", 3, 16)
        new("back_loaded", 6, 16)
        new("mask0", 1)
        new("mask3", 1)
        new("x_bias", 2)
        new("x1_stored", 1, 16)
        for tag in ("l0", "a", "b", "c"):
            units = 2 * G if tag == "l0" else G
            if tag in "ab":
                new(f"added_{tag}", units)
                new(f"shifted_{tag}", units)
            if tag != "l0":
                new(f"probs_{tag}", units)
        for tag in ("l0", "ln1", "ln2", "a", "b", "m", "c"):
            new(f"variance_{tag}", 1)
            new(f"rstd_{tag}", 1)
            new(f"normed_{tag}", 1)
        new("state_col1", 1)
        new("xxx", 1)
        new("max_l0", 2 * G)
        new("mix", 5)
        new("w", 1)
        new("scratch_stored", 10, 16)
        new("z_loaded", 2, 16)
        new("state_in", 4)
        new("decay_in", 4)
        new("scanned", 2)
        new("y_part", 1)
        new("keys_cleared", 1)
        new("bonus", 1)
        new("variance_y", 1)
        new("rstd_y", 1)
        new("y_normed", 1)
        new("y_stored", 1, 16)
        new("yT_loaded", CT * G, 16)
        new("gated", 1)
        new("bx_bias", 3)
        new("state_col2", 1)
        new("xk2", 1)
        new("xr2", 1)
        new("kk", 1)

        STAGES = (
            "FFFFBBBFFFBFBBFFBFBBBFBFBFBFFBFBBBBFBFFFFBFBBBFBFBFFFBFBFBFBFBBBBFFFBBBBFBFBFBBBBFBBBBBBFBB"
        )

        def run(front=None, back=None):
            stages = {"F": front, "B": back}
            for half in STAGES:
                if stages[half] is not None:
                    next(stages[half])
            for half in (front, back):
                assert half is None or next(half, "end") == "end"

        def all_groups(eng, front, back, prepare=None):
            run(front=front(eng, 0))
            if prepare is not None:
                eng.wait_ge(back_consts.sem, 16 * NBACK_LOADS)
                prepare()
                eng.wait_ge(back_ready.sem, NBACK_READY)
            with eng.Fori(0, NG - 1) as g:
                run(front=front(eng, g + 1), back=back(eng, g))
            run(back=back(eng, NG - 1))

        def is_first(g):
            return isinstance(g, int) and g == 0

        block = ctx.enter_context(nc.Block())

        def store_kind(sp, g, kind):
            n = KINDS[kind]
            for ct in range(CT):
                dst = d_rkvw[g, n].rearrange("(b h) (s t) -> (h s) b t", b=G, s=SH)[ct * P:(ct + 1) * P]
                sp.dma_start(dst, rkvw[:, n, ct, :].rearrange("p (b t) -> p b t", b=G)).then_inc(sig["scratch_stored"].sem, 16)

        def idle(stages):
            for _ in range(stages):
                yield

        def sp_front(sp, g):
            yield from idle(22)
            sp.wait_ge(FB.free_sem("rows", "l0m"), FB.taken_at(g, "rows", "l0m"))
            after_wait(sp, "sync")
            sp.dma_start(d_x1[g].rearrange("(t p) c -> p t c", p=P), x1[:, :, :]).then_inc(sig["x1_stored"].sem, 16)
            yield
            yield from idle(3)
            for n, kind in enumerate(("k", "v", "r")):
                sp.wait_ge(FB.free_sem("proj", MIXES[n][0]), FB.taken_at(g, "proj", MIXES[n][0]))
                after_wait(sp, "sync")
                store_kind(sp, g, kind)
                yield
            yield
            sp.wait_ge(FB.free_sem("proj", "maa_g"), FB.taken_at(g, "proj", "maa_g"))
            after_wait(sp, "sync")
            for ct in range(CT):
                sp.dma_start(d_gate[g, ct], gate2[:, ct, :]).then_inc(sig["scratch_stored"].sem, 16)
            yield
            sp.wait_ge(sig["w"].sem, sig["w"].at(g, 1))
            after_wait(sp, "sync")
            store_kind(sp, g, "w")
            yield
            sp.wait_ge(sig["x1_stored"].sem, sig["x1_stored"].at(g, 1))
            sp.wait_ge(sig["scratch_stored"].sem, sig["scratch_stored"].at(g, 10))
            after_wait(sp, "sync")
            sp.dma_start(z[:, :, :], d_rkvw[g].rearrange("k p x -> p k x")).then_inc(sig["z_loaded"].sem, 16)
            sp.dma_start(s0[:, :], a["s0"][g]).then_inc(sig["z_loaded"].sem, 16)
            yield
            yield from idle(6)
            sp.wait_ge(sig["y_normed"].sem, sig["y_normed"].at(g, 1))
            after_wait(sp, "sync")
            sp.dma_start(d_y[g], y[:, :]).then_inc(sig["y_stored"].sem, 16)
            yield

        def sp_back(sp, g):
            sp.wait_ge(sig["y_stored"].sem, sig["y_stored"].at(g, 1))
            after_wait(sp, "sync")
            sp.dma_start(ctx_b[:, :, :], ctx_d[g].rearrange("(t p) c -> p t c", p=P)).then_inc(sig["back_loaded"].sem, 16)
            sp.dma_start(mask3_raw[0:1, :], a["mask3"][g]).then_inc(sig["back_loaded"].sem, 16)
            for half in range(2):
                sp.dma_start(cross_m[64 * half:64 * half + 64, :, :], a["cross_mask"][g].rearrange("b q k -> q b k")).then_inc(sig["back_loaded"].sem, 16)
            sp.dma_start(bx[:, :, :], d_x1[g].rearrange("(t p) c -> p t c", p=P)).then_inc(sig["back_loaded"].sem, 16)
            sp.dma_start(g_in[:, :, :], d_gate[g].rearrange("h p x -> p h x")).then_inc(sig["back_loaded"].sem, 16)
            sp.wait_ge(stored.sem, stored.before(g))
            after_wait(sp, "sync")
            for ct in range(CT):
                for b in range(G):
                    src = d_y[g].rearrange("(b h) (v t) -> b (h v) t", b=G, v=SH)
                    sp.dma_start(yT[:, ct, b * S:(b + 1) * S], src[b, ct * P:(ct + 1) * P]).then_inc(sig["yT_loaded"].sem, 16)
            yield
            yield from idle(49)
            sp.wait_ge(BB.free_sem("rows", "c"), BB.taken_at(g, "rows", "c"))
            after_wait(sp, "sync")
            sp.dma_start(out_d[g].rearrange("(t p) c -> p t c", p=P), o_out[:, :, :]).then_inc(stored.sem, 16)
            yield

        @block.sync
        def _(sp):
            def load(dst, src, part=loaded):
                sp.dma_start(dst, src).then_inc(part.sem, 16)

            nf = width(FRONT_W)
            load(ident[:, :], a["ident"])
            load(parity[:, :], a["parity"])
            load(w_front[:, 0:2048], a["w_front"][:, 0:2048])
            load(vecs[:, :], a["vecs"])
            load(rows[:, :], a["rows"].partition_broadcast(P))
            load(maa_w2g[0:32, :], a["maa_w2g"])
            load(decay_w2[0:64, :], a["decay_w2"])
            for b in range(G):
                load(bonus_u[b * 32:(b + 1) * 32, :], a["faaaa"])
            load(w_front[:, 2048:nf], a["w_front"][:, 2048:nf], mlp_loaded)
            load(bv[:, :], a["bv"].partition_broadcast(P), back_consts)
            load(tgate[:, 0:1], a["gate"].partition_broadcast(P), back_consts)
            load(self_m[0:64, :], a["self_mask"], back_consts)
            load(self_m[64:128, :], a["self_mask"], back_consts)
            load(w_back[:, 0:4096], a["w_back"][:, 0:4096], back_consts)
            load(w_back[:, 4096:], a["w_back"][:, 4096:], back_consts)
            all_groups(sp, sp_front, sp_back)
            sp.wait_ge(stored.sem, 16 * (NG + 1))

        def tokens(ap):
            return ap.rearrange("p (b t) -> p b t", b=G)

        def pe_transposes(pe, K, g, key, sources):
            pe.wait_ge(K.free_sem(*key), K.free_at(g, *key))
            t = K.tile(*key)
            for i, src in enumerate(sources):
                ins = pe.transpose(t[:, i * P:(i + 1) * P], src, ident[:, :])
            ins.then_inc(K.full_sem(*key), 1)

        def pe_cols(pe, K, g, key, w, x, halves=CT):
            pe.wait_ge(K.free_sem(*key), K.free_at(g, *key))
            t = K.tile(*key)
            for m in range(halves):
                for ct in range(CT):
                    o = t[:, m * T:(m + 1) * T]
                    r = x(ct)
                    if len(r.shape) == 3:
                        o = o.rearrange("p (b t) -> p b t", b=G)
                    ins = pe.matmul(o, w[:, ct, m * P:(m + 1) * P], r, start=(ct == 0), stop=(ct == CT - 1))
            ins.then_inc(K.full_sem(*key), 1)

        def pe_queries(pe, K, g, tag, w, x):
            for m in range(CT):
                pe.wait_ge(K.free_sem("q", tag, m), K.free_at(g, "q", tag, m))
                t = K.tile("q", tag, m)
                for ct in range(CT):
                    r = x(ct)
                    o = tokens(t[:, 0:T]) if len(r.shape) == 3 else t[:, 0:T]
                    ins = pe.matmul(o, w[:, ct, m * P:(m + 1) * P], r, start=(ct == 0), stop=(ct == CT - 1))
                ins.then_inc(K.full_sem("q", tag, m), 1)

        def pe_rows(pe, K, g, key, w, x, n_k, wait=None):
            pe.wait_ge(K.free_sem(*key), K.free_at(g, *key))
            t = K.tile(*key)
            for tt in range(TT):
                for k in range(n_k):
                    if wait is not None and tt == 0:
                        wait(k)
                    ins = pe.matmul(t[:, tt * C:(tt + 1) * C], x(k, tt), w[:, k, :], start=(k == 0), stop=(k == n_k - 1))
            ins.then_inc(K.full_sem(*key), 1)

        def pe_attention(pe, K, g, tag, w_o):
            units, per_out = (2 * G, 4) if tag == "l0" else (G, 2)
            keys = P if tag == "l0" else S

            def scores(u):
                pe.wait_ge(K.free_sem("scores", tag, u), K.free_at(g, "scores", tag, u))
                t = K.tile("scores", tag, u)
                b = u // 2 if tag == "l0" else u
                for m in ([u % 2] if tag == "l0" else range(CT)):
                    at = 0 if tag == "l0" else m * PT_ * keys
                    o = t[:, at:at + PT_ * keys].rearrange("p (j k) -> p j k", j=PT_)
                    q = K.qeo[:, m, b, :, :].rearrange("p r q -> p (r q)")
                    masked = tag in ("l0", "c")
                    ins = pe.matmul(o, q, K.kb[:, m, :, b * keys:(b + 1) * keys], start=True, stop=not masked)
                    if masked:
                        mask = mask0[0:1, b, :] if tag == "l0" else mask3[0:1, b * S:(b + 1) * S]
                        ins = pe.matmul(o, ones_bf[0:1, :], mask.unsqueeze(1).to_broadcast([1, PT_, keys]),
                                        start=False, stop=True)
                ins.then_inc(K.full_sem("scores", tag, u), 1)

            def weighted(u):
                pe.wait_ge(K.free_sem("probsT", tag, u), K.taken_at(g, "probsT", tag, u))
                key = ("heads", tag, u // per_out)
                if u % per_out == 0:
                    pe.wait_ge(K.free_sem(*key), K.free_at(g, *key))
                t = K.tile(*key)
                b = u // 2 if tag == "l0" else u
                base = (b % 2) * PAIRS * (D + 1)
                for i in range(PT_):
                    for r in range(2):
                        pT = K.probsT[:, u % 2, i * P + r * S:i * P + (r + 1) * S]
                        if tag == "l0":
                            at, n = base + ((u % 2) * PT_ + i) * (D + 1), D + 1
                            v = va[:, b, (u % 2) * PAIRS + 2 * i + r, :]
                        else:
                            at, n = base + i * 2 * (D + 1), 2 * (D + 1)
                            v = vb[:, b, i, r, :, :].rearrange("p h e -> p (h e)")
                        ins = pe.matmul(t[r * S:(r + 1) * S, at:at + n], pT, v, start=True, stop=True)
                if u % per_out == per_out - 1:
                    ins.then_inc(K.full_sem(*key), 1)

            kv = [(x, "l0", m) for x in "kv" for m in range(CT)] if tag == "l0" else [("k", tag), ("v", tag)]
            for key in K.latest([("q", tag, m) for m in range(CT)] + kv):
                pe.wait_ge(K.free_sem(*key), K.taken_at(g, *key))
            if tag in ("l0", "c"):
                pe.wait_ge(sig["mask0" if tag == "l0" else "mask3"].sem, sig["mask0" if tag == "l0" else "mask3"].at(g, 1))
            lag = LAG[tag]
            for step in range(units + 2 + lag):
                u = step - 1 - lag
                if 0 <= u < units:
                    if tag == "l0":
                        pe.wait_ge(K.free_sem("scores", tag, u), K.taken_at(g, "scores", tag, u))
                    else:
                        pe.wait_ge(sig[f"probs_{tag}"].sem, sig[f"probs_{tag}"].at(g, u + 1))
                    pe_transposes(pe, K, g, ("probsT", tag, u), [K.probs[:, u % 2, i * P:(i + 1) * P] for i in range(4)])
                if step < units:
                    scores(step)
                if u >= 1:
                    weighted(u - 1)
                yield
            pe.wait_ge(K.free_sem("heads", tag, 1), K.taken_at(g, "heads", tag, 1))
            pe_transposes(pe, K, g, ("headsT", tag), [K.heads[:, b, :] for b in range(G)])
            yield
            pe.wait_ge(K.free_sem("headsT", tag), K.taken_at(g, "headsT", tag))
            pe_rows(pe, K, g, ("rows", tag), w_o,
                    lambda r, tt: K.headsT[:, r, 2 * tt:2 * tt + 2, :].rearrange("p b q -> p (b q)"), 2)
            yield

        def pe_normT(pe, K, g, tag):
            pe.wait_ge(sig[f"normed_{tag}"].sem, sig[f"normed_{tag}"].at(g, 1))
            pe_transposes(pe, K, g, ("normT", tag), [K.xn[:, tt, ct * P:(ct + 1) * P] for ct in range(CT) for tt in range(TT)])

        def pe_mlp(pe, K, g, tag, w1, w2):
            for m in range(FT // 2):
                pe.wait_ge(K.free_sem("hidden", tag, m), K.free_at(g, "hidden", tag, m))
                t = K.tile("hidden", tag, m)
                for i in range(2):
                    for ct in range(CT):
                        ins = pe.matmul(t[:, i * T:(i + 1) * T], w1[:, ct, (2 * m + i) * P:(2 * m + i + 1) * P],
                                        K.xnT[:, ct, :], start=(ct == 0), stop=(ct == CT - 1))
                ins.then_inc(K.full_sem("hidden", tag, m), 1)
                yield
            pe_rows(pe, K, g, ("rows", tag), w2, lambda k, tt: K.hidden[:, k, tt * P:(tt + 1) * P], FT,
                    wait=lambda k: pe.wait_ge(K.free_sem("hidden", tag, k // 2), K.taken_at(g, "hidden", tag, k // 2)))
            yield

        def pe_kv(pe, K, g, tag, x, w_k, w_v):
            yield
            pe_cols(pe, K, g, ("k", tag), w_k, x)
            yield
            pe.wait_ge(K.free_sem("v", tag), K.free_at(g, "v", tag))
            t = K.tile("v", tag)
            for tt in range(TT):
                for ct in range(CT):
                    xb = x(ct)
                    xb = xb[:, 2 * tt:2 * tt + 2, :].rearrange("p b t -> p (b t)") if len(xb.shape) == 3 else xb[:, tt * P:(tt + 1) * P]
                    ins = pe.matmul(t[:, tt * C:(tt + 1) * C], xb, w_v[:, ct, :], start=(ct == 0), stop=(ct == CT - 1))
            ins.then_inc(K.full_sem("v", tag), 1)

        def pe_front(pe, g):
            K = FB
            pe.wait_ge(sig["x_loaded"].sem, sig["x_loaded"].at(g, 3))
            for ct in range(CT):
                pe_transposes(pe, K, g, ("inT", ct),
                              [t[:, tt, ct * P:(ct + 1) * P] for t in (ctx_in, x_in) for tt in range(TT)])
            yield
            for ct in range(CT):
                pe.wait_ge(K.free_sem("inT", ct), K.taken_at(g, "inT", ct))
            pe_queries(pe, K, g, "l0", W["l0_q"], lambda ct: inT[:, ct, :, S:P])
            yield
            for m in range(CT):
                pe.wait_ge(K.free_sem("k", "l0", m), K.free_at(g, "k", "l0", m))
                t = K.tile("k", "l0", m)
                for ct in range(CT):
                    ins = pe.matmul(t[:, :], W["l0_k"][:, ct, m * P:(m + 1) * P],
                                    inT[:, ct, :, :].rearrange("p b t -> p (b t)"), start=(ct == 0), stop=(ct == CT - 1))
                ins.then_inc(K.full_sem("k", "l0", m), 1)
            yield
            for j in range(2):
                pe.wait_ge(K.free_sem("v", "l0", j), K.free_at(g, "v", "l0", j))
                t = K.tile("v", "l0", j)
                for i in range(2):
                    for ct in range(CT):
                        ins = pe.matmul(t[:, i * C:(i + 1) * C], inT[:, ct, 2 * j + i, :], W["l0_v"][:, ct, :],
                                        start=(ct == 0), stop=(ct == CT - 1))
                ins.then_inc(K.full_sem("v", "l0", j), 1)
            yield
            yield from pe_attention(pe, K, g, "l0", W["l0_o"])
            pe_normT(pe, K, g, "l0")
            yield
            pe.wait_ge(K.free_sem("normT", "l0"), K.taken_at(g, "normT", "l0"))
            if is_first(g):
                pe.wait_ge(mlp_loaded.sem, 16)
            yield from pe_mlp(pe, K, g, "l0m", W["l0_w1"], W["l0_w2"])
            pe_normT(pe, K, g, "ln1")
            yield
            pe.wait_ge(sig["xxx"].sem, sig["xxx"].at(g, 1))
            pe.wait_ge(K.free_sem("lora"), K.free_at(g, "lora"))
            t = K.tile("lora")
            for ct in range(CT):
                pe.matmul(t[:, 0:T], W["maa_w1"][:, ct, 0:P], mixed[:, 0, ct, :], start=(ct == 0), stop=(ct == CT - 1))
            for ct in range(CT):
                ins = pe.matmul(t[0:32, T:2 * T], W["maa_w1"][:, ct, P:160], mixed[:, 0, ct, :],
                                start=(ct == 0), stop=(ct == CT - 1))
            ins.then_inc(K.full_sem("lora"), 1)
            yield
            pe.wait_ge(K.free_sem("lora"), K.taken_at(g, "lora"))
            for n in range(len(MIXES) + 1):
                if n < len(MIXES):
                    name, f = MIXES[n]
                    pe.wait_ge(K.free_sem("mix", name), K.free_at(g, "mix", name))
                    t = K.tile("mix", name)
                    for ct in range(CT):
                        if f < 4:
                            w, r = W["maa_w2"][32 * f:32 * f + 32, 0, ct * P:(ct + 1) * P], lora_t[32 * f:32 * f + 32, 0, :]
                        else:
                            w, r = maa_w2g[0:32, ct * P:(ct + 1) * P], lora_t[0:32, 1, :]
                        ins = pe.matmul(t[:, ct * T:(ct + 1) * T], w, r, start=True, stop=True)
                    ins.then_inc(K.full_sem("mix", name), 1)
                if n >= 1:
                    name = MIXES[n - 1][0]
                    pe.wait_ge(sig["mix"].sem, sig["mix"].at(g, n))
                    x = lambda ct: mixed[:, n % 2, ct, :]
                    if name != "maa_w":
                        pe_cols(pe, K, g, ("proj", name), W["w" + name[-1]], x)
                        yield
                        continue
                    pe.wait_ge(K.free_sem("decay1"), K.free_at(g, "decay1"))
                    t = K.tile("decay1")
                    for ct in range(CT):
                        ins = pe.matmul(t[0:64, 0:T], W["decay_w1"][:, ct, :], x(ct), start=(ct == 0), stop=(ct == CT - 1))
                    ins.then_inc(K.full_sem("decay1"), 1)
                    yield
                    pe.wait_ge(K.free_sem("decay1"), K.taken_at(g, "decay1"))
                    pe.wait_ge(K.free_sem("decay2"), K.free_at(g, "decay2"))
                    t = K.tile("decay2")
                    for m in range(CT):
                        ins = pe.matmul(t[:, m * T:(m + 1) * T], decay_w2[0:64, m * P:(m + 1) * P], dec_t[0:64, :],
                                        start=True, stop=True)
                    ins.then_inc(K.full_sem("decay2"), 1)
                    yield
                else:
                    yield
            yield from idle(8)

        def pe_back(pe, g):
            K = BB
            pe.wait_ge(sig["back_loaded"].sem, sig["back_loaded"].at(g, 6))
            pe_transposes(pe, K, g, ("ctxT",), [ctx_b[:, tt, ct * P:(ct + 1) * P] for ct in range(CT) for tt in range(TT)])
            yield
            pe.wait_ge(sig["gated"].sem, sig["gated"].at(g, 1))
            pe_rows(pe, K, g, ("rows", "wo"), W["wo"], lambda ct, tt: yT[:, ct, tt * P:(tt + 1) * P], CT)
            yield
            yield
            pe_normT(pe, K, g, "ln2")
            yield
            pe.wait_ge(sig["xk2"].sem, sig["xk2"].at(g, 1))
            pe_cols(pe, K, g, ("fk",), W["fwk"], lambda ct: xk2[:, ct, :])
            pe.wait_ge(sig["xr2"].sem, sig["xr2"].at(g, 1))
            pe_rows(pe, K, g, ("fr",), W["fwr"], lambda ct, tt: xr2[:, ct, tt * P:(tt + 1) * P], CT)
            yield
            pe.wait_ge(sig["kk"].sem, sig["kk"].at(g, 1))
            pe_rows(pe, K, g, ("fv",), W["fwv"], lambda ct, tt: kk[:, ct, tt * P:(tt + 1) * P], CT)
            yield
            x = lambda ct: K.xnT[:, ct, :]
            pe_normT(pe, K, g, "a")
            yield
            pe.wait_ge(K.free_sem("normT", "a"), K.taken_at(g, "normT", "a"))
            pe_queries(pe, K, g, "a", W["l2_q"], x)
            yield from pe_kv(pe, K, g, "a", x, W["l2_k"], W["l2_v"])
            yield
            yield from pe_attention(pe, K, g, "a", W["l2_o"])
            pe_normT(pe, K, g, "b")
            yield
            pe.wait_ge(K.free_sem("normT", "b"), K.taken_at(g, "normT", "b"))
            pe_queries(pe, K, g, "b", W["l2_q2"], x)
            pe.wait_ge(K.free_sem("ctxT"), K.taken_at(g, "ctxT"))
            yield from pe_kv(pe, K, g, "b", lambda ct: ctxT[:, ct, :, :], W["l2_k2"], W["l2_v2"])
            yield
            yield from pe_attention(pe, K, g, "b", W["l2_o2"])
            pe_normT(pe, K, g, "m")
            yield
            pe.wait_ge(K.free_sem("normT", "m"), K.taken_at(g, "normT", "m"))
            yield from pe_mlp(pe, K, g, "l2m", W["l2_w1"], W["l2_w2"])
            pe_normT(pe, K, g, "c")
            pe.wait_ge(K.free_sem("rows", "l2m"), K.taken_at(g, "rows", "l2m"))
            pe_transposes(pe, K, g, ("xT",), [bx[:, tt, ct * P:(ct + 1) * P] for ct in range(CT) for tt in range(TT)])
            yield
            pe.wait_ge(K.free_sem("xT"), K.taken_at(g, "xT"))
            pe_queries(pe, K, g, "c", W["l3_q"], lambda ct: yT[:, ct, :])
            pe.wait_ge(K.free_sem("normT", "c"), K.taken_at(g, "normT", "c"))
            yield from pe_kv(pe, K, g, "c", x, W["l3_k"], W["l3_v"])
            yield
            yield from pe_attention(pe, K, g, "c", W["l3_o"])

        @block.tensor
        def _(pe):
            pe.wait_ge(loaded.sem, 16 * NLOADS)
            pe.wait_ge(ready.sem, NREADY)
            all_groups(pe, pe_front, pe_back, lambda: None)

        def v_variance(v, K, g, tag, x):
            v.drain()
            for tt in range(TT):
                v.bn_stats(K.stats[:, tt, :], x[:, tt, :])
            v.drain()
            for tt in range(TT):
                v.bn_aggr(K.mv[:, tt, :], K.stats[:, tt, :])
            v.drain()
            v.tensor_scalar(K.nw[:, 0, 0:TT], K.mv[:, :, 1], 1e-5, None, ALU.add).then_inc(sig[f"variance_{tag}"].sem, 1)

        def v_norm(v, K, g, tag, x):
            v.wait_ge(sig[f"rstd_{tag}"].sem, sig[f"rstd_{tag}"].at(g, 1))
            for tt in range(TT):
                ins = v.tensor_scalar(K.xn[:, tt, :], x[:, tt, :], K.mv[:, tt, 0:1], K.nw[:, 1, tt:tt + 1],
                                      ALU.subtract, ALU.mult)
            ins.then_inc(sig[f"normed_{tag}"].sem, 1)

        def v_queries(v, K, g, tag, bias, scale):
            v.wait_ge(K.full_sem("q", tag, 1), K.full_at(g, "q", tag, 1))
            t = K.tile("q", tag, 1)
            for r in range(2):
                src = tokens(t[:, 0:T])
                if bias:
                    ins = v.tensor_scalar(K.qeo[:, 1, :, r, :], src, vec(bias, 1), scale[:, r:r + 1], ALU.add, ALU.mult)
                else:
                    ins = v.tensor_scalar(K.qeo[:, 1, :, r, :], src, scale[:, r:r + 1], None, ALU.mult)
            ins.then_inc(K.free_sem("q", tag, 1), 1)

        def v_keys(v, K, g, tag, bias):
            v.wait_ge(K.full_sem("k", tag), K.full_at(g, "k", tag))
            t = K.tile("k", tag)
            for j in (2, 3):
                q = slice(32 * j, 32 * j + 32)
                src = t[q, :].rearrange("p (m t) -> p m t", m=CT)
                if bias:
                    at = VEC_AT[bias]
                    ins = v.tensor_tensor(K.kb[q, :, j, 0:T], src, vecs[q, at:at + CT].unsqueeze(2).to_broadcast([32, CT, T]), ALU.add)
                else:
                    ins = v.tensor_copy(K.kb[q, :, j, 0:T], src)
            ins.then_inc(K.free_sem("k", tag), 1)

        def v_values(v, K, g, tag, bias_at):
            v.wait_ge(K.full_sem("v", tag), K.full_at(g, "v", tag))
            t = K.tile("v", tag)
            for u in range(2):
                for h in range(2):
                    q = slice(u * S, (u + 1) * S)
                    src = t[q, :].rearrange("p (t h e d) -> p t h e d", t=TT, h=2, d=D)[:, :, h]
                    dst = vb[h * S:(h + 1) * S, u:G:2, :, :, h, 0:D].rearrange("p b i r d -> p b (i r) d")
                    if bias_at is None:
                        ins = v.tensor_copy(dst, src)
                    else:
                        bias = bv[q, bias_at + h * P:bias_at + (h + 1) * P].rearrange("p (e d) -> p e d", d=D)
                        ins = v.tensor_tensor(dst, src, bias.unsqueeze(1).to_broadcast([S, TT, 2 * PT_, D]), ALU.add)
            ins.then_inc(K.free_sem("v", tag), 1)

        def v_attention(v, K, g, tag):
            units, per_out = (2 * G, 4) if tag == "l0" else (G, 2)
            n, keys = (PT_, P) if tag == "l0" else (PAIRS, S)

            def grid(ap):
                return ap.rearrange("p (j k) -> p j k", j=n)

            def shift(u, src, slot):
                v.tensor_reduce(K.nmax[:, u % 4, 0:n], src, AX_X, ALU.max, negate=True)
                v.drain()
                ins = v.tensor_tensor(grid(K.probs[:, slot, :]), src, K.nmax[:, u % 4, 0:n].unsqueeze(2).to_broadcast([P, n, keys]), ALU.add)
                return ins

            if tag == "a":
                v.wait_ge(sig["back_loaded"].sem, sig["back_loaded"].at(g, 6))

            def masked(u):
                v.wait_ge(K.full_sem("scores", tag, u), K.full_at(g, "scores", tag, u))
                t = K.tile("scores", tag, u)
                m = self_m[:, :] if tag == "a" else cross_m[:, u, :]
                ins = v.tensor_tensor(grid(K.probs[:, u % 2, :]), grid(t[:, :]), m.unsqueeze(1).to_broadcast([P, n, keys]), ALU.mult)
                ins.then_inc(K.free_sem("scores", tag, u), 1)

            def out(j):
                v.wait_ge(K.full_sem("heads", tag, j), K.full_at(g, "heads", tag, j))
                t = K.tile("heads", tag, j)
                o = t[:, 0:2 * PAIRS * (D + 1)].rearrange("p (n e) -> p n e", e=D + 1)
                v.reciprocal(K.rden[:, j, :], o[:, :, D])
                v.drain()
                ins = v.tensor_tensor(K.heads[:, 2 * j:2 * j + 2, :].rearrange("p b (n d) -> p (b n) d", d=D), o[:, :, 0:D],
                                      K.rden[:, j, :].unsqueeze(2).to_broadcast([P, 2 * PAIRS, D]), ALU.mult)
                ins.then_inc(K.free_sem("heads", tag, j), 1)

            lag = LAG[tag]
            for step in range(units + 2 + lag):
                if tag in "ab":
                    if step < units:
                        masked(step)
                    if 1 <= step <= units:
                        u = step - 1
                        v.wait_ge(sig[f"added_{tag}"].sem, sig[f"added_{tag}"].at(g, u + 1))
                        shift(u, grid(K.probs[:, u % 2, :]), u % 2).then_inc(sig[f"shifted_{tag}"].sem, 1)
                elif step < units:
                    v.wait_ge(K.full_sem("scores", tag, step), K.full_at(g, "scores", tag, step))
                    t = K.tile("scores", tag, step)
                    if tag == "l0":
                        v.tensor_reduce(K.nmax[:, step % 4, 0:n], grid(t[:, :]), AX_X, ALU.max, negate=True).then_inc(sig["max_l0"].sem, 1)
                    else:
                        ins = shift(step, grid(t[:, :]), step % 2)
                        ins.then_inc(K.free_sem("scores", tag, step), 1)
                done = step - 1 - lag
                if done >= per_out and done % per_out == 0:
                    out(done // per_out - 1)
                yield
            yield

        def v_add_rows(v, K, g, key, out, x):
            v.wait_ge(K.full_sem(*key), K.full_at(g, *key))
            t = K.tile(*key)
            ins = v.tensor_tensor(out[:, :, :].rearrange("p t c -> p (t c)"), t[:, :], x[:, :, :].rearrange("p t c -> p (t c)"), ALU.add)
            ins.then_inc(K.free_sem(*key), 1)
            return ins

        def v_front(v, g):
            K = FB
            v.wait_ge(K.full_sem("inT", 1), K.full_at(g, "inT", 1))
            t = K.tile("inT", 1)
            ins = v.tensor_copy(inT[:, 1, :, :].rearrange("p b (u t) -> p u b t", u=2), t[:, :].rearrange("p (u b t) -> p u b t", u=2, b=G))
            ins.then_inc(K.free_sem("inT", 1), 1)
            yield
            v_queries(v, K, g, "l0", "l0_bq", par16)
            yield
            for m in range(CT):
                v.wait_ge(K.full_sem("k", "l0", m), K.full_at(g, "k", "l0", m))
                t = K.tile("k", "l0", m)
                v.wait_ge(sig["keys_cleared"].sem, sig["keys_cleared"].at(g, 1))
                for j in (2, 3):
                    q = slice(32 * j, 32 * j + 32)
                    ins = v.tensor_scalar(K.kb[q, m, j, :], t[q, :], vecs[q, VEC_AT["l0_bk"] + m:VEC_AT["l0_bk"] + m + 1], None, ALU.add)
                ins.then_inc(K.free_sem("k", "l0", m), 1)
            yield
            for j in range(2):
                v.wait_ge(K.full_sem("v", "l0", j), K.full_at(g, "v", "l0", j))
                t = K.tile("v", "l0", j)
                ins = v.tensor_tensor(va[:, 2 * j:2 * j + 2, :, 0:D], t[:, :].rearrange("p (b h d) -> p b h d", b=2, d=D),
                                      row("l0_bv").rearrange("p (h d) -> p h d", d=D).unsqueeze(1).to_broadcast([P, 2, 2 * PAIRS, D]), ALU.add)
                ins.then_inc(K.free_sem("v", "l0", j), 1)
            yield
            yield from v_attention(v, K, g, "l0")
            v.wait_ge(sig["x_bias"].sem, sig["x_bias"].at(g, 2))
            v_add_rows(v, K, g, ("rows", "l0"), x1, x1)
            yield
            v.wait_ge(sig["rstd_l0"].sem, sig["rstd_l0"].at(g, 1))
            for tt in range(TT):
                ins = v.tensor_scalar(K.xn[:, tt, :], x1[:, tt, :], K.nw[:, 1, tt:tt + 1], None, ALU.mult)
            ins.then_inc(sig["normed_l0"].sem, 1)
            yield
            yield from idle(FT // 2)
            v_add_rows(v, K, g, ("rows", "l0m"), x1, x_in)
            v_variance(v, K, g, "ln1", x1)
            yield
            v_norm(v, K, g, "ln1", x1)
            yield
            v_shift(v, K, g, "ln1", "state_col1", xaS, sx)
            for ct in range(CT):
                ins = v.scalar_tensor_tensor(tokens(mixed[:, 0, ct, :]), tokens(sx[:, ct, :]), vec("maa_x", ct), xaS[:, ct, :, 1:S + 1],
                                             ALU.mult, ALU.add)
            ins.then_inc(sig["xxx"].sem, 1)
            yield
            for n, (name, _) in enumerate(MIXES):
                v.wait_ge(K.full_sem("mix", name), K.full_at(g, "mix", name))
                t = K.tile("mix", name)
                if n >= 2:
                    v.wait_ge(K.full_sem("proj", MIXES[n - 2][0]), K.full_at(g, "proj", MIXES[n - 2][0]))
                for ct in range(CT):
                    ins = v.scalar_tensor_tensor(mixed[:, (n + 1) % 2, ct, :], t[:, ct * T:(ct + 1) * T], vec(name, ct), sx[:, ct, :],
                                                 ALU.add, ALU.mult)
                ins.then_inc(K.free_sem("mix", name), 1)
                yield
            v.wait_ge(K.full_sem("proj", "maa_g"), K.full_at(g, "proj", "maa_g"))
            t = K.tile("proj", "maa_g")
            v.wait_ge(K.free_sem("proj", "maa_g"), K.taken_at(g, "proj", "maa_g", readers=1))
            ins = v.scalar_tensor_tensor(gate2[:, :, :].rearrange("p h t -> p (h t)"), gate2[:, :, :].rearrange("p h t -> p (h t)"), 1.0,
                                         t[:, :], ALU.add, ALU.mult)
            ins.then_inc(K.free_sem("proj", "maa_g"), 1)
            yield
            yield
            yield from v_recurrence(v, K, g)

        def v_shift(v, K, g, tag, col, x, out):
            v.wait_ge(K.free_sem("normT", tag), K.taken_at(g, "normT", tag))
            v.wait_ge(sig[col].sem, sig[col].at(g, 1))
            v.tensor_tensor(out[:, :, :].rearrange("p h (b t) -> p (h b) t", b=G),
                            x[:, :, :, 0:S].rearrange("p h b t -> p (h b) t"),
                            x[:, :, :, 1:S + 1].rearrange("p h b t -> p (h b) t"), ALU.subtract)
            v.drain()

        def v_recurrence(v, K, g):
            flat, half = "p s v t -> p (s v t)", "p v t -> p (v t)"
            r = z[:, 0, :].rearrange("p (s t) -> p s t", s=SH)
            yield
            for i in range(2):
                v.wait_ge(sig["state_in"].sem, sig["state_in"].at(g, 2 * i + 2))
                v.wait_ge(sig["decay_in"].sem, sig["decay_in"].at(g, 2 * i + 2))
                v.tensor_tensor_scan(state.rearrange(flat), decay.rearrange(flat), state.rearrange(flat), 0.0, ALU.mult, ALU.add).then_inc(sig["scanned"].sem, 1)
                v.drain()
                yield
                v.tensor_tensor(state, state, r[:, i * HS:(i + 1) * HS].unsqueeze(2).to_broadcast([P, HS, SH, S]), ALU.mult)
                v.drain()
                v.tensor_tensor(state[:, 0:2].rearrange(flat), state[:, 0:2].rearrange(flat), state[:, 2:4].rearrange(flat), ALU.add)
                v.drain()
                if i == 0:
                    v.tensor_tensor(y, state[:, 0].rearrange(half), state[:, 1].rearrange(half), ALU.add).then_inc(sig["y_part"].sem, 1)
                    yield
                    yield
            v.tensor_tensor(state[:, 0].rearrange(half), state[:, 0].rearrange(half), state[:, 1].rearrange(half), ALU.add)
            v.drain()
            v.tensor_tensor(y, y, state[:, 0].rearrange(half), ALU.add)
            v.drain()
            v.wait_ge(sig["bonus"].sem, sig["bonus"].at(g, 1))
            v.tensor_tensor(y, y, bonus, ALU.add)
            v.drain()
            yield
            y3, ysq3 = (q.rearrange("p (v t) -> p v t", v=SH) for q in (y, ysq))
            v.tensor_reduce(ysum[:, :], y3.rearrange("p v t -> p t v"), AX_X, ALU.add)
            v.drain()
            v.scalar_tensor_tensor(y3, ysum[:, :].unsqueeze(1).to_broadcast([P, SH, S]), -1.0 / SH, y3, ALU.mult, ALU.add)
            v.drain()
            v.tensor_tensor(ysq, y, y, ALU.mult)
            v.drain()
            v.tensor_reduce(ysum[:, :], ysq3.rearrange("p v t -> p t v"), AX_X, ALU.add)
            v.drain()
            v.tensor_scalar(K.nw[:, 0, :], ysum[:, :], 1.0 / SH, 1e-5, ALU.mult, ALU.add).then_inc(sig["variance_y"].sem, 1)
            yield
            v.wait_ge(sig["rstd_y"].sem, sig["rstd_y"].at(g, 1))
            v.tensor_tensor(y3, y3, K.nw[:, 1, :].unsqueeze(1).to_broadcast([P, SH, S]), ALU.mult).then_inc(sig["y_normed"].sem, 1)
            yield
        def v_back(v, g):
            K = BB
            yield
            v.wait_ge(sig["yT_loaded"].sem, sig["yT_loaded"].at(g, CT * G))
            for ct in range(CT):
                v.tensor_scalar(yT[:, ct, :], yT[:, ct, :], vec("gn_w", ct), vec("gn_b", ct), ALU.mult, ALU.add)
            v.drain()
            f = "p h t -> p (h t)"
            v.scalar_tensor_tensor(yT[:, :, :].rearrange(f), yT[:, :, :].rearrange(f), 0.5, g_in[:, :, :].rearrange(f),
                                                    ALU.mult, ALU.mult).then_inc(sig["gated"].sem, 1)
            yield
            v_add_rows(v, K, g, ("rows", "wo"), bx, bx)
            v_variance(v, K, g, "ln2", bx)
            yield
            v_norm(v, K, g, "ln2", bx)
            yield
            v_shift(v, K, g, "ln2", "state_col2", xcS, sxc)
            for out, name, done in ((xk2, "fmaa_k", "xk2"), (xr2, "fmaa_r", "xr2")):
                for ct in range(CT):
                    ins = v.scalar_tensor_tensor(tokens(out[:, ct, :]), tokens(sxc[:, ct, :]), vec(name, ct), xcS[:, ct, :, 1:S + 1],
                                                 ALU.mult, ALU.add)
                ins.then_inc(sig[done].sem, 1)
            yield
            v.wait_ge(K.full_sem("fv"), K.full_at(g, "fv"))
            t = K.tile("fv")
            v.wait_ge(K.free_sem("fr"), K.taken_at(g, "fr"))
            f = "p t c -> p (t c)"
            ins = v.scalar_tensor_tensor(rr.rearrange(f), rr.rearrange(f), 1.0, t[:, :], ALU.add, ALU.mult)
            ins.then_inc(K.free_sem("fv"), 1)
            v.drain()
            v.scalar_tensor_tensor(bx[:, :, :].rearrange(f), rr.rearrange(f), 0.5, bx[:, :, :].rearrange(f), ALU.mult, ALU.add)
            v_variance(v, K, g, "a", bx)
            yield
            for n, (tag, after, bq, bk) in enumerate((("a", "b", "l2_bq", "l2_bk"), ("b", "m", "l2_bq2", "l2_bk2"))):
                v_norm(v, K, g, tag, bx)
                yield
                v_queries(v, K, g, tag, bq, par4)
                yield
                v_keys(v, K, g, tag, bk)
                yield
                v_values(v, K, g, tag, n * C)
                yield
                yield from v_attention(v, K, g, tag)
                v.wait_ge(sig["bx_bias"].sem, sig["bx_bias"].at(g, n + 1))
                v_add_rows(v, K, g, ("rows", tag), bx, bx)
                v_variance(v, K, g, after, bx)
                yield
            v_norm(v, K, g, "m", bx)
            yield
            yield from idle(FT // 2)
            v.wait_ge(sig["bx_bias"].sem, sig["bx_bias"].at(g, 3))
            v_add_rows(v, K, g, ("rows", "l2m"), bx, bx)
            v_variance(v, K, g, "c", ctx_b)
            yield
            v_norm(v, K, g, "c", ctx_b)
            yield
            v_queries(v, K, g, "c", None, par4)
            yield
            v_keys(v, K, g, "c", None)
            yield
            v_values(v, K, g, "c", None)
            yield
            yield from v_attention(v, K, g, "c")
            v.wait_ge(K.full_sem("rows", "c"), K.full_at(g, "rows", "c"))
            t = K.tile("rows", "c")
            ins = v.scalar_tensor_tensor(o_out.rearrange(f), t[:, :], tgate[:, 1:2], bx[:, :, :].rearrange(f), ALU.mult, ALU.add)
            ins.then_inc(K.free_sem("rows", "c"), 1)
            yield

        @block.vector
        def _(v):
            v.wait_ge(loaded.sem, 16 * NLOADS)
            v.tensor_scalar(par16[:, :], parity[:, :], 1.0 / 16, None, ALU.mult)
            v.tensor_scalar(par4[:, :], parity[:, :], 1.0 / 4, None, ALU.mult)
            v.drain()
            for i, (name, par) in enumerate((("l0_bq", par16), ("l2_bq", par4), ("l2_bq2", par4))):
                v.tensor_scalar(qb[:, i, :], par[:, :], vec(name), None, ALU.mult)
            v.drain().then_inc(ready.sem, 1)
            v.wait_ge(ready.sem, NREADY)
            all_groups(v, v_front, v_back,
                       lambda: v.tensor_scalar(self_c[:, :], self_m[:, :], 10000.0, -10000.0, ALU.mult, ALU.add).then_inc(back_ready.sem, 1))

        def a_normT(s, K, g, tag, out, scale, shift):
            s.wait_ge(K.full_sem("normT", tag), K.full_at(g, "normT", tag))
            t = K.tile("normT", tag)
            for ct in range(CT):
                o, src = out(ct), t[:, ct * T:(ct + 1) * T]
                if len(o.shape) == 3:
                    src = tokens(src)
                ins = s.activation(o, src, ACT.Identity, scale=vec(scale, ct), bias=vec(shift, ct) if shift else 0.0)
            ins.then_inc(K.free_sem("normT", tag), 1)

        def a_queries(s, K, g, tag, bias, scale):
            s.wait_ge(K.full_sem("q", tag, 0), K.full_at(g, "q", tag, 0))
            t = K.tile("q", tag, 0)
            for r in range(2):
                ins = s.activation(K.qeo[:, 0, :, r, :], tokens(t[:, 0:T]), ACT.Identity, scale=scale[:, r:r + 1],
                                   bias=qb[:, bias, r:r + 1] if bias is not None else 0.0)
            ins.then_inc(K.free_sem("q", tag, 0), 1)

        def a_keys(s, K, g, tag, bias):
            s.wait_ge(K.full_sem("k", tag), K.full_at(g, "k", tag))
            t = K.tile("k", tag)
            for j in (0, 1):
                q = slice(32 * j, 32 * j + 32)
                if bias is None:
                    ins = s.copy(K.kb[q, :, j, 0:T], t[q, :].rearrange("p (m t) -> p m t", m=CT))
                    continue
                for m in range(CT):
                    at = VEC_AT[bias] + m
                    ins = s.activation(K.kb[q, m, j, 0:T], t[q, m * T:(m + 1) * T], ACT.Identity, bias=vecs[q, at:at + 1])
            ins.then_inc(K.free_sem("k", tag), 1)

        def a_attention(s, K, g, tag):
            units, lag = 2 * G if tag == "l0" else G, LAG[tag]
            if tag == "l0" and not is_first(g):
                s.wait_ge(sig["y_stored"].sem, sig["y_stored"].at(g - 1, 1))
            for step in range(units + 2 + lag):
                if 0 <= step - MASK_STEP[tag] < units:
                    u = step - MASK_STEP[tag]
                    if tag == "l0":
                        s.wait_ge(sig["max_l0"].sem, sig["max_l0"].at(g, u + 1))
                        t = K.tile("scores", tag, u)
                        for i in range(PT_):
                            ins = s.activation(K.probs[:, u % 2, i * P:(i + 1) * P], t[:, i * P:(i + 1) * P], ACT.Exp, bias=K.nmax[:, u % 4, i:i + 1])
                        ins.then_inc(K.free_sem("scores", tag, u), 1)
                    else:
                        if tag == "c":
                            s.wait_ge(K.free_sem("scores", tag, u), K.taken_at(g, "scores", tag, u))
                        else:
                            s.wait_ge(sig[f"shifted_{tag}"].sem, sig[f"shifted_{tag}"].at(g, u + 1))
                        s.activation(K.probs[:, u % 2, :], K.probs[:, u % 2, :], ACT.Exp).then_inc(sig[f"probs_{tag}"].sem, 1)
                if 0 <= step - lag - 1 < units:
                    u = step - lag - 1
                    s.wait_ge(K.full_sem("probsT", tag, u), K.full_at(g, "probsT", tag, u))
                    t = K.tile("probsT", tag, u)
                    ins = s.copy(K.probsT[:, u % 2, :], t[:, :])
                    ins.then_inc(K.free_sem("probsT", tag, u), 1)
                yield
            s.wait_ge(K.full_sem("headsT", tag), K.full_at(g, "headsT", tag))
            t = K.tile("headsT", tag)
            ins = s.copy(K.headsT.rearrange("p r b q -> p b r q"), t[:, :].rearrange("p (b r q) -> p b r q", b=G, r=2))
            ins.then_inc(K.free_sem("headsT", tag), 1)
            yield

        def a_mlp(s, K, g, tag, bias):
            for m in range(FT // 2):
                s.wait_ge(K.full_sem("hidden", tag, m), K.full_at(g, "hidden", tag, m))
                t = K.tile("hidden", tag, m)
                for i in range(2):
                    ins = s.activation(K.hidden[:, 2 * m + i, :], t[:, i * T:(i + 1) * T], ACT.Gelu_apprx_tanh, bias=vec(bias, 2 * m + i))
                ins.then_inc(K.free_sem("hidden", tag, m), 1)
                yield

        def a_front(s, g):
            K = FB
            s.wait_ge(K.full_sem("inT", 0), K.full_at(g, "inT", 0))
            t = K.tile("inT", 0)
            ins = s.copy(inT[:, 0, :, :].rearrange("p b (u t) -> p u b t", u=2), t[:, :].rearrange("p (u b t) -> p u b t", u=2, b=G))
            ins.then_inc(K.free_sem("inT", 0), 1)
            yield
            a_queries(s, K, g, "l0", 0, par16)
            yield
            for m in range(CT):
                s.wait_ge(K.full_sem("k", "l0", m), K.full_at(g, "k", "l0", m))
                t = K.tile("k", "l0", m)
                s.wait_ge(sig["keys_cleared"].sem, sig["keys_cleared"].at(g, 1))
                for j in (0, 1):
                    q = slice(32 * j, 32 * j + 32)
                    at = VEC_AT["l0_bk"] + m
                    ins = s.activation(K.kb[q, m, j, :], t[q, :], ACT.Identity, bias=vecs[q, at:at + 1])
                ins.then_inc(K.free_sem("k", "l0", m), 1)
            yield
            yield
            yield from a_attention(s, K, g, "l0")
            s.wait_ge(K.free_sem("rows", "l0"), K.taken_at(g, "rows", "l0"))
            for tt in range(TT):
                s.activation(K.xn[:, tt, :], x1[:, tt, :], ACT.Square, accum_out=sumsq[:, tt:tt + 1])
            s.drain().then_inc(sig["variance_l0"].sem, 1)
            yield
            a_normT(s, K, g, "l0", lambda ct: K.xnT[:, ct, :], "l0_post", None)
            yield
            yield from a_mlp(s, K, g, "l0m", "l0_b1")
            yield
            a_normT(s, K, g, "ln1", lambda ct: xaS[:, ct, :, 1:S + 1], "ln1_w", "ln1_b")
            yield
            s.wait_ge(K.full_sem("lora"), K.full_at(g, "lora"))
            t = K.tile("lora")
            s.activation(lora_t[:, 0, :], t[:, 0:T], ACT.Tanh)
            ins = s.activation(lora_t[0:32, 1, :], t[0:32, T:2 * T], ACT.Tanh)
            ins.then_inc(K.free_sem("lora"), 1)
            yield
            yield
            for name, _ in MIXES[:-1]:
                s.wait_ge(K.full_sem("proj", name), K.full_at(g, "proj", name))
                t = K.tile("proj", name)
                if name == "maa_g":
                    ins = s.activation(gate2[:, :, :].rearrange("p h t -> p (h t)"), t[:, :], ACT.Tanh, scale=0.5)
                else:
                    ins = s.copy(rkvw[:, KINDS[name[-1]], :, :].rearrange("p h t -> p (h t)"), t[:, :])
                ins.then_inc(K.free_sem("proj", name), 1)
                yield
            s.wait_ge(K.full_sem("decay1"), K.full_at(g, "decay1"))
            t = K.tile("decay1")
            ins = s.activation(dec_t[0:64, :], t[0:64, 0:T], ACT.Tanh)
            ins.then_inc(K.free_sem("decay1"), 1)
            yield
            s.wait_ge(K.full_sem("decay2"), K.full_at(g, "decay2"))
            t = K.tile("decay2")
            for ct in range(CT):
                ins = s.activation(rkvw[:, KINDS["w"], ct, :], t[:, ct * T:(ct + 1) * T], ACT.Exp, bias=vec("decay", ct))
            ins.then_inc(K.free_sem("decay2"), 1)
            s.drain()
            w = rkvw[:, KINDS["w"], :, :].rearrange("p h t -> p (h t)")
            s.activation(w, w, ACT.Exp, scale=-1.0).then_inc(sig["w"].sem, 1)
            yield
            s.wait_ge(sig["z_loaded"].sem, sig["z_loaded"].at(g, 2))
            for i in range(2):
                if i == 1:
                    s.wait_ge(sig["scanned"].sem, sig["scanned"].at(g, 1))
                w = z[:, 3, :].rearrange("p (s t) -> p s t", s=SH)[:, i * HS:(i + 1) * HS, 0:S - 1]
                s.copy(decay[:, :, :, 1:S], w.unsqueeze(2).to_broadcast([P, HS, SH, S - 1])).then_inc(sig["decay_in"].sem, 1)
                yield
                if i == 0:
                    yield
                    yield
            yield from idle(4)

        def a_back(s, g):
            K = BB
            s.wait_ge(K.full_sem("ctxT"), K.full_at(g, "ctxT"))
            t = K.tile("ctxT")
            ins = s.copy(ctxT[:, :, :, :].rearrange("p h b t -> p (h b t)"), t[:, :])
            ins.then_inc(K.free_sem("ctxT"), 1)
            yield
            yield
            yield
            a_normT(s, K, g, "ln2", lambda ct: xcS[:, ct, :, 1:S + 1], "ln2_w", "ln2_b")
            yield
            s.wait_ge(K.full_sem("fk"), K.full_at(g, "fk"))
            t = K.tile("fk")
            f = "p h t -> p (h t)"
            ins = s.activation(kk[:, :, :].rearrange(f), t[:, :], ACT.Relu)
            ins.then_inc(K.free_sem("fk"), 1)
            s.drain()
            s.activation(kk[:, :, :].rearrange(f), kk[:, :, :].rearrange(f), ACT.Square).then_inc(sig["kk"].sem, 1)
            s.wait_ge(K.full_sem("fr"), K.full_at(g, "fr"))
            t = K.tile("fr")
            ins = s.activation(rr.rearrange("p t c -> p (t c)"), t[:, :], ACT.Tanh, scale=0.5)
            ins.then_inc(K.free_sem("fr"), 1)
            yield
            yield
            for n, (tag, ln, bk) in enumerate((("a", "l2_ln1", "l2_bk"), ("b", "l2_ln2", "l2_bk2"))):
                a_normT(s, K, g, tag, lambda ct: K.xnT[:, ct, :], ln + "_s", ln + "_b")
                yield
                a_queries(s, K, g, tag, n + 1, par4)
                yield
                a_keys(s, K, g, tag, bk)
                yield
                yield
                yield from a_attention(s, K, g, tag)
                yield
            a_normT(s, K, g, "m", lambda ct: K.xnT[:, ct, :], "l2_ln3_s", "l2_ln3_b")
            yield
            yield from a_mlp(s, K, g, "l2m", "l2_b1")
            yield
            a_normT(s, K, g, "c", lambda ct: K.xnT[:, ct, :], "l3_ln_s", "l3_ln_b")
            s.wait_ge(K.full_sem("xT"), K.full_at(g, "xT"))
            t = K.tile("xT")
            ins = s.copy(yT[:, :, :].rearrange(f), t[:, :])
            ins.then_inc(K.free_sem("xT"), 1)
            yield
            a_queries(s, K, g, "c", None, par4)
            yield
            a_keys(s, K, g, "c", None)
            yield
            yield
            yield from a_attention(s, K, g, "c")
            yield

        @block.scalar
        def _(s):
            s.wait_ge(loaded.sem, 16 * NLOADS)
            s.wait_ge(ready.sem, NREADY)
            all_groups(s, a_front, a_back,
                       lambda: s.activation(tgate[:, 1:2], tgate[:, 0:1], ACT.Tanh).then_inc(back_ready.sem, 1))

        def p_rstd(p, K, g, tag, n=TT):
            p.wait_ge(sig[f"variance_{tag}"].sem, sig[f"variance_{tag}"].at(g, 1))
            after_wait(p, "pool")
            x, r, t = K.nw[:, 0, 0:n], K.nw[:, 1, 0:n], K.nw[:, 2, 0:n]
            if tag == "l0":
                p.tensor_scalar(x, sumsq[:, :], 1.0 / C, 1e-6, ALU.mult, ALU.add)
                p.drain()
            p.tensor_scalar(r.bitcast(I32), x.bitcast(I32), -0.5, RSQRT_SEED, ALU.mult, ALU.add)
            p.drain()
            for step in range(3):
                p.tensor_tensor(t, r, r, ALU.mult)
                p.drain()
                p.tensor_tensor(t, t, x, ALU.mult)
                p.drain()
                p.tensor_scalar(t, t, -0.5, 1.5, ALU.mult, ALU.add)
                p.drain()
                ins = p.tensor_tensor(r, t, r, ALU.mult)
                if step < 2:
                    p.drain()
            ins.then_inc(sig[f"rstd_{tag}"].sem, 1)

        def p_back(p, g):
            K = BB
            p.wait_ge(sig["back_loaded"].sem, sig["back_loaded"].at(g, 6))
            after_wait(p, "pool")
            p.tensor_scalar(mask3[0:1, :], mask3_raw[0:1, :], 0, MASKED, ALU.is_equal, ALU.mult).then_inc(sig["mask3"].sem, 1)
            p.tensor_scalar(cross_c[:, :, :], cross_m[:, :, :], 10000.0, -10000.0, ALU.mult, ALU.add)
            p.drain()
            p.wait_ge(K.free_sem("ctxT"), K.taken_at(g, "ctxT"))
            after_wait(p, "pool")
            p.tensor_copy(xcS[:, :, :, 0], ctxT[:, :, :, 0]).then_inc(sig["state_col2"].sem, 1)
            yield
            yield
            p_rstd(p, K, g, "ln2")
            yield
            yield
            yield
            p_rstd(p, K, g, "a")
            yield
            for n, (tag, bias) in enumerate((("a", "l2_bo"), ("b", "l2_bo2"), ("m", "l2_b2"))):
                p.wait_ge(sig[f"normed_{tag}"].sem, sig[f"normed_{tag}"].at(g, 1))
                p.tensor_tensor(bx[:, :, :], bx[:, :, :], row(bias).unsqueeze(1).to_broadcast([P, TT, C]), ALU.add).then_inc(sig["bx_bias"].sem, 1)
                yield
                if tag == "m":
                    continue
                yield from idle(3)
                for u in range(G):
                    p.wait_ge(K.free_sem("scores", tag, u), K.taken_at(g, "scores", tag, u))
                    c = self_c[:, :] if tag == "a" else cross_c[:, u, :]
                    q = K.probs[:, u % 2, :].rearrange("p (j k) -> p j k", j=PAIRS)
                    p.tensor_tensor(q, q, c.unsqueeze(1).to_broadcast([P, PAIRS, S]), ALU.add).then_inc(sig[f"added_{tag}"].sem, 1)
                    yield
                yield from idle(4)
                p_rstd(p, K, g, "b" if tag == "a" else "m")
                yield
            yield from idle(4)
            p_rstd(p, K, g, "c")
            yield from idle(14)

        def p_front(p, g):
            K = FB
            p.dma_start(x_in[:, :, :], x_d[g].rearrange("(t p) c -> p t c", p=P)).then_inc(sig["x_loaded"].sem, 16)
            p.dma_start(ctx_in[:, :, :], ctx_d[g].rearrange("(t p) c -> p t c", p=P)).then_inc(sig["x_loaded"].sem, 16)
            p.dma_start(mask0_raw[0:1, :], a["mask0"][g]).then_inc(sig["x_loaded"].sem, 16)
            p.drain()
            p.memset(K.kb, 0.0).then_inc(sig["keys_cleared"].sem, 1)
            if is_first(g):
                p.wait_ge(loaded.sem, 16 * NLOADS)
                p.wait_ge(ready.sem, NREADY)
            p.wait_ge(sig["x_loaded"].sem, sig["x_loaded"].at(g, 3))
            after_wait(p, "pool")
            p.tensor_scalar(mask0[0:1, :, 0:S], mask0_raw[0:1, :].rearrange("p (b k) -> p b k", b=G), 0, MASKED, ALU.is_equal, ALU.mult).then_inc(sig["mask0"].sem, 1)
            p.tensor_tensor(x1[:, :, :], x_in[:, :, :], row("l0_bo").unsqueeze(1).to_broadcast([P, TT, C]), ALU.add).then_inc(sig["x_bias"].sem, 1)
            yield
            p.drain()
            for ct in range(CT):
                p.wait_ge(K.free_sem("inT", ct), K.taken_at(g, "inT", ct))
            p.tensor_tensor(x_in[:, :, :], x_in[:, :, :], row("l0_b2").unsqueeze(1).to_broadcast([P, TT, C]), ALU.add).then_inc(sig["x_bias"].sem, 1)
            p.tensor_copy(xaS[:, :, :, 0], inT[:, :, :, 1]).then_inc(sig["state_col1"].sem, 1)
            yield
            yield from idle(14)
            p_rstd(p, K, g, "l0")
            yield from idle(6)
            p_rstd(p, K, g, "ln1")
            yield from idle(3)
            for n in range(len(MIXES)):
                p.wait_ge(K.free_sem("mix", MIXES[n][0]), K.taken_at(g, "mix", MIXES[n][0]))
                m = mixed[:, (n + 1) % 2, :, :].rearrange("p h (b t) -> p (h b) t", b=G)
                p.tensor_tensor(m, m, xaS[:, :, :, 1:S + 1].rearrange("p h b t -> p (h b) t"), ALU.add).then_inc(sig["mix"].sem, 1)
                yield
            yield from idle(2)
            p.wait_ge(sig["z_loaded"].sem, sig["z_loaded"].at(g, 2))
            r, k, vv = (z[:, i, :].rearrange("p (s t) -> p s t", s=SH) for i in range(3))
            for i in range(2):
                if i == 1:
                    p.wait_ge(sig["y_part"].sem, sig["y_part"].at(g, 1))
                h = slice(i * HS, (i + 1) * HS)
                p.tensor_tensor(state[:, :, :, 1:S], k[:, h, 0:S - 1].unsqueeze(2).to_broadcast([P, HS, SH, S - 1]),
                                vv[:, :, 0:S - 1].unsqueeze(1).to_broadcast([P, HS, SH, S - 1]), ALU.mult).then_inc(sig["state_in"].sem, 1)
                p.tensor_copy(state[:, :, :, 0], s0[:, :].rearrange("p (s v) -> p s v", s=SH)[:, h]).then_inc(sig["state_in"].sem, 1)
                p.memset(decay[:, :, :, 0:1], 0.0).then_inc(sig["decay_in"].sem, 1)
                yield
                if i == 1:
                    continue
                p.tensor_tensor(bonus, z[:, 0, :], z[:, 1, :], ALU.mult)
                p.drain()
                b3 = bonus.rearrange("p (s t) -> p s t", s=SH)
                p.tensor_tensor(b3, b3, bonus_u[:, :].unsqueeze(2).to_broadcast([P, SH, S]), ALU.mult)
                p.drain()
                for n in (4, 2):
                    p.tensor_tensor(bonus[:, 0:n * S], bonus[:, 0:n * S], bonus[:, n * S:2 * n * S], ALU.add)
                    p.drain()
                p.tensor_tensor(bonus_sum[:, :], bonus[:, 0:S], bonus[:, S:2 * S], ALU.add)
                p.drain()
                p.tensor_tensor(b3, bonus_sum[:, :].unsqueeze(1).to_broadcast([P, SH, S]), vv, ALU.mult).then_inc(sig["bonus"].sem, 1)
                yield
                yield
            yield
            yield
            p_rstd(p, K, g, "y", S)
            yield
            yield

        @block.gpsimd
        def _(p):
            for K in (FB, BB):
                for f in K.free:
                    p.sem_inc(f, 1)
            p.sem_inc(stored.sem, 16)
            p.memset(vb[:, :, :, :, :, :], 0.0)
            p.drain()
            p.memset(BB.kb[:, :, :, :], 0.0).then_inc(ready.sem, 1)
            p.memset(va[:, :, :, D], 1.0).then_inc(ready.sem, 1)
            p.memset(ones_bf[:, :], 1.0).then_inc(ready.sem, 1)
            p.drain()
            p.memset(mask0[0:1, :, :], 0.0).then_inc(ready.sem, 1)
            for h in range(2):
                p.drain()
                ins = p.memset(vb[h * S:(h + 1) * S, :, :, :, h, D], 1.0)
            ins.then_inc(ready.sem, 1)
            all_groups(p, p_front, p_back, lambda: None)

    return nc


def kernel(**inputs):
    import numpy as np
    import concourse.bacc as bacc
    from concourse.bass_utils import run_bass_kernel_spmd

    inp = {k: np.asarray(v) for k, v in inputs.items()}

    def tiles(w):
        k = w.shape[0] // P
        return w.reshape(k, P, w.shape[1]).transpose(1, 0, 2).reshape(P, -1)

    def by_parity(w):
        return w.reshape(PAIRS, 2, D, -1).transpose(1, 0, 2, 3).reshape(C, -1)

    def by_half(w):
        w = w.reshape(-1, PT_, 2, 2, D).transpose(0, 2, 1, 3, 4)
        return w.reshape(-1, C)

    L0 = {k[9:]: v for k, v in inp.items() if k.startswith("L0_xattn_")}
    L1 = {k[9:]: v for k, v in inp.items() if k.startswith("L1_xattn_")}
    L2 = {k[9:]: v for k, v in inp.items() if k.startswith("L2_xattn_")}
    L3 = {k[9:]: v for k, v in inp.items() if k.startswith("L3_xattn_")}
    kv0, kvb0 = L0["kv_w"].reshape(C, C, 2), L0["kv_b"].reshape(C, 2)
    w = {
        "l0_q": L0["q_w"], "l0_k": kv0[:, :, 0], "l0_v": kv0[:, :, 1], "l0_o": by_parity(L0["out_w"]),
        "l0_w1": L0["mlp_w1"], "l0_w2": L0["mlp_w2"], "maa_w1": L1["maa_w1"], "decay_w1": L1["decay_w1"],
        "maa_w2": L1["maa_w2"][0:4].reshape(P, C), "wr": L1["Wr"].T, "wk": L1["Wk"].T, "wv": L1["Wv"].T, "wg": L1["Wg"].T,
        "wo": L1["Wo"].T, "fwk": L1["fWk"].T, "fwr": L1["fWr"].T, "fwv": L1["fWv"].T,
        "l2_q": L2["w_qkv"][:, 0:C], "l2_k": L2["w_qkv"][:, C:2 * C], "l2_v": by_half(L2["w_qkv"][:, 2 * C:]),
        "l2_o": by_parity(L2["w_ao"]), "l2_q2": L2["w_q"], "l2_k2": L2["w_kv"][:, 0:C], "l2_v2": by_half(L2["w_kv"][:, C:]),
        "l2_o2": by_parity(L2["w_co"]), "l2_w1": L2["w1"], "l2_w2": L2["w2"],
        "l3_q": L3["Wq"].T, "l3_k": L3["Wk"].T, "l3_v": by_half(L3["Wv"].T), "l3_o": by_parity(L3["Wo"].T),
    }
    v = {
        "l0_bq": L0["q_b"], "l0_bk": kvb0[:, 0], "l0_post": L0["postnorm_w"], "l0_b1": L0["mlp_b1"],
        "ln1_w": L1["ln1_w"], "ln1_b": L1["ln1_b"], "ln2_w": L1["ln2_w"], "ln2_b": L1["ln2_b"],
        "maa_x": L1["maa_x"], "maa_k": L1["maa_k"], "maa_v": L1["maa_v"], "maa_r": L1["maa_r"], "maa_g": L1["maa_g"],
        "maa_w": L1["maa_w"], "decay": L1["time_decay"], "gn_w": L1["gn_w"], "gn_b": L1["gn_b"],
        "fmaa_k": L1["fmaa_k"], "fmaa_r": L1["fmaa_r"], "l2_ln1_s": L2["ln1_s"], "l2_ln1_b": L2["ln1_b"],
        "l2_ln2_s": L2["ln2_s"], "l2_ln2_b": L2["ln2_b"], "l2_ln3_s": L2["ln3_s"], "l2_ln3_b": L2["ln3_b"],
        "l2_bq": L2["b_qkv"][0:C], "l2_bk": L2["b_qkv"][C:2 * C], "l2_bq2": L2["b_q"], "l2_bk2": L2["b_kv"][0:C],
        "l2_b1": L2["b1"], "l3_ln_s": L3["ln_gamma"], "l3_ln_b": L3["ln_beta"],
    }
    rows = {"l0_bv": kvb0[:, 1], "l0_bo": L0["out_b"], "l0_b2": L0["mlp_b2"], "l2_bo": L2["b_ao"], "l2_bo2": L2["b_co"], "l2_b2": L2["b2"]}
    ctx = inp["ctx_2048"]
    arrays = {
        "x": inp["x"], "ctx": ctx, "s0": ctx[:, 2:2 + SH, :].reshape(NG, P, SH * SH),
        "w_front": np.concatenate([tiles(w[n]) for n in FRONT_W], axis=1),
        "w_back": np.concatenate([tiles(w[n]) for n in BACK_W], axis=1),
        "maa_w2g": L1["maa_w2"][4], "decay_w2": L1["decay_w2"], "faaaa": L1["faaaa"].reshape(-1, SH),
        "vecs": np.concatenate([v[n].reshape(-1, P).T for n in VECS], axis=1),
        "rows": np.concatenate([rows[n] for n in ROWS]).reshape(1, -1),
        "bv": np.concatenate([by_half(L2["b_qkv"][2 * C:]), by_half(L2["b_kv"][C:])], axis=1),
        "gate": L3["gate"].reshape(1, 1), "ident": np.eye(P, dtype=np.float32),
        "parity": np.stack([(np.arange(P) // D) % 2 == r for r in range(2)], axis=1).astype(np.float32),
        "mask0": inp["mask_BxS2_ik0"].reshape(NG, 1, T), "mask3": inp["mask_BxS2_bf1"].view(np.uint8).reshape(NG, 1, T),
        "self_mask": inp["mask_1x1xSxS2_fc1"].reshape(S, S), "cross_mask": inp["mask_Bx1xSxS2_ff1"].reshape(NG, G, S, S),
    }
    nc = bacc.Bacc("TRN2", target_bir_lowering=False, num_devices=1)
    ins, aps = {}, {}
    for name, arr in arrays.items():
        arr = np.ascontiguousarray(arr)
        ins[f"in_{name}"] = arr
        aps[name] = nc.dram_tensor(f"in_{name}", arr.shape, mybir.dt.from_np(arr.dtype), kind="ExternalInput").ap()
    aps["out"] = nc.dram_tensor("out_x", (B, S, C), F32, kind="ExternalOutput").ap()
    bass_four_layers_kernel(nc, aps)
    r = run_bass_kernel_spmd(nc, [ins], core_ids=[0])
    return r.results[0]["out_x"]
```
